# Optimizing a Trainium2 kernel written in Bass

```python
import numpy as np
import jax
import jax.numpy as jnp

def _softmax(x, axis=-1):
    return jax.nn.softmax(x, axis=axis)

def _gelu(x):
    return jax.nn.gelu(x, approximate=True)

def _silu(x):
    return jax.nn.silu(x)

def _sigmoid(x):
    return jax.nn.sigmoid(x)

def _layernorm(x, axis=-1, eps=1e-05):
    m = jnp.mean(x, axis=axis, keepdims=True)
    v = jnp.var(x, axis=axis, keepdims=True)
    return (x - m) / jnp.sqrt(v + eps)

def _scatter_add(tgt, idx, src, axis=0):
    return tgt.at[idx].add(src)

def _segment_sum(src, seg, n):
    return jax.ops.segment_sum(src, seg, n)
kernel_name = 'mk_early_fusion_d1_tok_img1024_r4_399f87'

def setup_inputs(seed: int=0):
    np.random.seed(seed)
    _w = jnp.asarray

    def _rec_inputs():
        import jax
        import jax.numpy as jnp
        _rk = jax.random.key(seed)
        x = -0.00016672 + 0.999947 * jax.random.normal(jax.random.fold_in(_rk, 1), (64, 3, 64, 64), jnp.float32)
        txt = -0.000497171 + 0.57724 * jax.random.normal(jax.random.fold_in(_rk, 2), (64, 77, 256), jnp.float32)
        return (x, txt)
    x, txt = _rec_inputs()

    def _L0_tok_setup():
        import jax, jax.numpy as jnp
        import numpy as np
        IMG = 96
        PATCH = 16
        CH = 3
        EMBED = 256
        PATCH_DIM = CH * PATCH * PATCH

        def _patchify(x):
            B, C, H, Wd = x.shape
            hp, wp = (H // PATCH, Wd // PATCH)
            p = x.reshape(B, C, hp, PATCH, wp, PATCH)
            p = p.transpose(0, 2, 4, 1, 3, 5)
            return p.reshape(B, hp * wp, C * PATCH * PATCH)
        key = jax.random.key(seed)
        kx, kw, kb, kc = jax.random.split(key, 4)
        x = jax.random.normal(kx, (64, CH, IMG, IMG), dtype=jnp.float32)
        bound = 1.0 / np.sqrt(PATCH_DIM)
        W = jax.random.uniform(kw, (PATCH_DIM, EMBED), minval=-bound, maxval=bound, dtype=jnp.float32)
        b = jax.random.uniform(kb, (EMBED,), minval=-bound, maxval=bound, dtype=jnp.float32)
        cls_token = jnp.zeros((1, 1, EMBED), dtype=jnp.float32)
        return {'x': x, 'W': W, 'b': b, 'cls_token': cls_token}
    _L0_tok_all = _L0_tok_setup()
    _L0_tok_in = {k: v for k, v in _L0_tok_all.items() if k in ('W', 'b', 'cls_token')}
    del _L0_tok_all

    def _L0_attn_setup():
        import jax, jax.numpy as jnp
        import numpy as np
        NUM_HEADS = 16
        key = jax.random.key(seed)
        ks = jax.random.split(key, 6)
        B, S, D = (2, 512, 256)
        x = jax.random.normal(ks[0], (B, S, D), dtype=jnp.float32)
        scale = 1.0 / np.sqrt(D)
        Wq = jax.random.normal(ks[1], (D, D), dtype=jnp.float32) * scale
        Wk = jax.random.normal(ks[2], (D, D), dtype=jnp.float32) * scale
        Wv = jax.random.normal(ks[3], (D, D), dtype=jnp.float32) * scale
        Wo = jax.random.normal(ks[4], (D, D), dtype=jnp.float32) * scale
        bo = jax.random.normal(ks[5], (D,), dtype=jnp.float32) * 0.01
        return {'x': x, 'Wq': Wq, 'Wk': Wk, 'Wv': Wv, 'Wo': Wo, 'bo': bo}
    _L0_attn_all = _L0_attn_setup()
    _L0_attn_in = {k: v for k, v in _L0_attn_all.items() if k in ('Wq', 'Wk', 'Wv', 'Wo', 'bo')}
    del _L0_attn_all

    def _L0_ffn_setup():
        import jax, jax.numpy as jnp
        import numpy as np
        B, T, C, H, E = (4, 512, 256, 512, 8)
        CAPACITY_FACTOR = 1.0
        key = jax.random.key(seed)
        ks = jax.random.split(key, 5)
        scale = 0.02
        return {'x': jax.random.normal(ks[0], (B, T, C), dtype=jnp.float32), 'Wg': jax.random.normal(ks[1], (E, C), dtype=jnp.float32) * scale, 'W1': jax.random.normal(ks[2], (E, H, C), dtype=jnp.float32) * scale, 'W2': jax.random.normal(ks[3], (E, C, H), dtype=jnp.float32) * scale, 'W3': jax.random.normal(ks[4], (E, H, C), dtype=jnp.float32) * scale}
    _L0_ffn_all = _L0_ffn_setup()
    _L0_ffn_in = {k: v for k, v in _L0_ffn_all.items() if k in ('Wg', 'W1', 'W2', 'W3')}
    del _L0_ffn_all
    return {'x': x, 'txt': txt, 'L0_tok_W': _L0_tok_in['W'], 'L0_tok_b': _L0_tok_in['b'], 'L0_tok_cls_token': _L0_tok_in['cls_token'], 'L0_attn_Wq': _L0_attn_in['Wq'], 'L0_attn_Wk': _L0_attn_in['Wk'], 'L0_attn_Wv': _L0_attn_in['Wv'], 'L0_attn_Wo': _L0_attn_in['Wo'], 'L0_attn_bo': _L0_attn_in['bo'], 'L0_ffn_Wg': _L0_ffn_in['Wg'], 'L0_ffn_W1': _L0_ffn_in['W1'], 'L0_ffn_W2': _L0_ffn_in['W2'], 'L0_ffn_W3': _L0_ffn_in['W3']}

def reference(x, txt, L0_tok_W, L0_tok_b, L0_tok_cls_token, L0_attn_Wq, L0_attn_Wk, L0_attn_Wv, L0_attn_Wo, L0_attn_bo, L0_ffn_Wg, L0_ffn_W1, L0_ffn_W2, L0_ffn_W3):
    import jax
    import jax.numpy as jnp

    def _L0_tok_ref(x, W, b, cls_token):
        import jax, jax.numpy as jnp
        import numpy as np
        IMG = 96
        PATCH = 16
        CH = 3
        EMBED = 256
        PATCH_DIM = CH * PATCH * PATCH

        def _patchify(x):
            B, C, H, Wd = x.shape
            hp, wp = (H // PATCH, Wd // PATCH)
            p = x.reshape(B, C, hp, PATCH, wp, PATCH)
            p = p.transpose(0, 2, 4, 1, 3, 5)
            return p.reshape(B, hp * wp, C * PATCH * PATCH)
        B = x.shape[0]
        patches = _patchify(x)
        proj = jnp.einsum('bnd,de->bne', patches, W) + b
        cls = jnp.broadcast_to(cls_token, (B, 1, cls_token.shape[-1]))
        return jnp.concatenate((cls, proj), axis=1)

    def _L0_attn_ref(x, Wq, Wk, Wv, Wo, bo):
        import jax, jax.numpy as jnp
        import numpy as np
        NUM_HEADS = 16
        B, S, D = x.shape
        H = NUM_HEADS
        hd = D // H

        def split_heads(t):
            return t.reshape(B, S, H, hd).transpose(0, 2, 1, 3)
        q = split_heads(x @ Wq)
        k = split_heads(x @ Wk)
        v = split_heads(x @ Wv)
        scores = jnp.einsum('bhsd,bhtd->bhst', q, k)
        causal = jnp.triu(jnp.ones((S, S), dtype=bool), k=1)
        scores = jnp.where(causal, -jnp.inf, scores)
        attn = jax.nn.softmax(scores * hd ** (-0.5), axis=-1)
        out = jnp.einsum('bhst,bhtd->bhsd', attn, v)
        out = out.transpose(0, 2, 1, 3).reshape(B, S, D)
        return out @ Wo + bo

    def _L0_ffn_ref(x, Wg, W1, W2, W3):
        import jax, jax.numpy as jnp
        import numpy as np
        B, T, C, H, E = (4, 512, 256, 512, 8)
        CAPACITY_FACTOR = 1.0
        b, t, c = x.shape
        e = Wg.shape[0]
        n = b * t
        capacity = max(1, int(CAPACITY_FACTOR * n / e))
        x_flat = x.reshape(n, c)
        scores = (x_flat @ Wg.T).T
        top_vals, token_idx = jax.lax.top_k(scores, capacity)
        token_w = jax.nn.softmax(top_vals, axis=-1)
        xg = x_flat[token_idx]
        h = jax.nn.silu(jnp.einsum('eic,ehc->eih', xg, W1)) * jnp.einsum('eic,ehc->eih', xg, W3)
        y = jnp.einsum('eih,ech->eic', h, W2) * token_w[..., None]
        out = jnp.zeros_like(x_flat).at[token_idx.reshape(-1)].add(y.reshape(-1, c))
        return out.reshape(b, t, c)
    h = _L0_tok_ref(x, L0_tok_W, L0_tok_b, L0_tok_cls_token)
    h = jnp.concatenate([h, txt], axis=1)
    h = h + _L0_attn_ref(_layernorm(h, axis=-1), L0_attn_Wq, L0_attn_Wk, L0_attn_Wv, L0_attn_Wo, L0_attn_bo)
    h = h + _L0_ffn_ref(_layernorm(h, axis=-1), L0_ffn_Wg, L0_ffn_W1, L0_ffn_W2, L0_ffn_W3)
    return h

_drawn_inputs = setup_inputs


def setup_inputs(seed=0):
    import zlib

    import numpy as np

    out = dict(_drawn_inputs(seed))
    spreads = {'L0_tok_cls_token': (0.0, 0.1)}
    factors = {'L0_attn_bo': 3.542,
     'L0_ffn_Wg': 8.0,
     'L0_ffn_W1': 8.0,
     'L0_ffn_W2': 8.0,
     'L0_ffn_W3': 8.0}
    for name, (base, spread) in spreads.items():
        noise = np.random.default_rng([zlib.crc32(name.encode()), seed]).standard_normal(out[name].shape)
        drawn = base * np.exp(spread * noise) if base else spread * noise
        out[name] = jnp.asarray(drawn.astype(out[name].dtype))
    for name, factor in factors.items():
        out[name] = (out[name] * factor).astype(out[name].dtype)
    return out
```

```python
import concourse.bass as bass
from concourse import mybir
from contextlib import ExitStack

F32 = mybir.dt.float32
BF16 = mybir.dt.bfloat16
I32 = mybir.dt.int32
U32 = mybir.dt.uint32
ALU = mybir.AluOpType
ACT = mybir.ActivationFunctionType
AX = mybir.AxisListType

ITEMS, CHANNELS, IMAGE = 64, 3, 64
PATCH = 16
GRID = IMAGE // PATCH
PATCHES = GRID * GRID
PATCH_DIM = CHANNELS * PATCH * PATCH
TEXT = 77
DIM = 256
ROWS = 1 + PATCHES + TEXT
HEADS, HEAD = 16, 16
EXPERTS, HIDDEN = 8, 512
TOKENS = ITEMS * ROWS
CAPACITY = TOKENS // EXPERTS
EPS = 1e-5
P = 128
CHUNKS = DIM // P
PER = 4
GROUPS = ITEMS // PER
SPAN = PER * ROWS
LOOP = 8
MASKED = -1e30
ROW = DIM + EXPERTS
BISECTIONS = 36
TILES = -(-CAPACITY // P)
LAST = CAPACITY - (TILES - 1) * P
HALVES = ((0, 3), (3, TILES))
HM = HIDDEN // P
SEGS = P // EXPERTS
CUTS = [(c * P, min(P, SPAN - c * P)) for c in range(-(-SPAN // P))]
OWN_TOP, ROUTED = 3, 3 + 2 + 4 * BISECTIONS + 16
TAG = 64


class Step:

    def __init__(self, b, turn=None, stride=LOOP):
        self.b, self.turn, self.stride = b, turn, stride

    def n(self, f):
        v = f(self.b)
        return v if self.turn is None else v + (f(self.b + self.stride) - v) * self.turn


FIRST_STEPS, LAST_STEP = 2 * LOOP, 4 * (GROUPS - 1) + 10
LOOP_TURNS = GROUPS // 2 - 3


def run_steps(eng, step):
    for b in range(FIRST_STEPS):
        step(Step(b))
    with eng.Fori(0, LOOP_TURNS) as turn:
        for b in range(FIRST_STEPS, FIRST_STEPS + LOOP):
            step(Step(b, turn))
    for b in range(FIRST_STEPS + LOOP * LOOP_TURNS, LAST_STEP):
        step(Step(b))


def run_experts(eng, step):
    for e in range(2):
        step(Step(e))
    with eng.Fori(0, EXPERTS // 2 - 2) as turn:
        for e in range(2, 4):
            step(Step(e, turn, stride=2))
    for e in range(EXPERTS - 2, EXPERTS):
        step(Step(e))


def ring_tiles(b):
    g = b // PER
    tiles = []
    if 1 <= b <= ITEMS:
        tiles += [("probsT", b - 1)] * 4
    k = b % PER
    if k == 0:
        if g + 1 < GROUPS:
            tiles += [("xT", g + 1)] * 2
        if 0 <= g - 2 < GROUPS:
            tiles += [("gate", g - 2)]
    if k == 1:
        if g + 1 < GROUPS:
            tiles += [("q", g + 1)] * 2
        if 0 <= g - 2 < GROUPS:
            tiles += [("gateT", g - 2)]
    if k == 2 and g + 1 < GROUPS:
        tiles += [("k", g + 1)] * 2
    if k == 3:
        if g + 1 < GROUPS:
            tiles += [("v", g + 1)] * 2
        if 0 <= g - 1 < GROUPS:
            tiles += [("x2T", g - 1)] * 2
    return tiles


UNITS = 2 * GRID
RING0 = 2 * UNITS + 8
RING_AT = {}
_n = RING0
for _b in range(LAST_STEP):
    for _t in ring_tiles(_b):
        RING_AT.setdefault(_t, _n)
        _n += 1
for _i, _kind in enumerate(("xT", "q", "k", "v")):
    RING_AT[(_kind, 0)] = 2 * UNITS + 2 * _i
RING_END = _n


PER_TURN = RING_AT[("k", 4)] - RING_AT[("k", 2)]


def build(nc, x, txt, tok_W, tok_b, cls_token, Wq, Wk, Wv, Wo, bo, Wg, W1, W2, W3, out):
    out_rows = out.rearrange("b s c -> (b s) c")
    patch_rows = nc.dram_tensor("patch_rows", [ITEMS, PATCHES, DIM], F32).ap()
    stored = nc.dram_tensor("stored", [TOKENS, ROW], F32).ap()
    gate_rows = nc.dram_tensor("gate_rows", [EXPERTS, TOKENS], F32).ap()

    ctx = ExitStack()
    with ctx:
        def sb(name, shape, dt=F32):
            return ctx.enter_context(nc.sbuf_tensor(name, shape, dt))

        def sem(name):
            return ctx.enter_context(nc.semaphore(name))

        ident = sb("ident", [P, P])
        ident_b = sb("ident_b", [P, P], BF16)
        iota_f = sb("iota_f", [P, P])

        ARENA = 43000
        arena = sb("arena", [P, ARENA])

        class Carve:
            def __init__(self):
                self.at = 0

            def __call__(self, *shape, dt=F32, parts=P):
                n = 1
                for s in shape:
                    n *= s
                words = n if dt in (F32, I32, U32) else (n + 1) // 2
                ap = arena[0:parts, self.at:self.at + words]
                self.at += (words + 7) // 8 * 8
                assert self.at <= ARENA, self.at
                if dt != F32:
                    ap = ap.bitcast(dt)[:, 0:n]
                if len(shape) > 1:
                    names = "abcde"[:len(shape)]
                    ap = ap.rearrange(f"p ({' '.join(names)}) -> p {' '.join(names)}",
                                      **dict(zip(names[1:], shape[1:])))
                return ap

        at = Carve()
        h = at(ITEMS, DIM, parts=ROWS)
        wq, wk, wv, wo = (at(CHUNKS, DIM) for _ in range(4))
        wgT = at(CHUNKS, EXPERTS)
        wg_rows = at(DIM, parts=EXPERTS)
        bo_rep = at(DIM, parts=ROWS)
        parity = at(2)
        mask = at(4, ROWS, dt=BF16, parts=ROWS)
        minus_half = at(PER, parts=ROWS)
        v = [at(PER, HEADS, 32, parts=ROWS) for _ in range(2)]
        working = at.at
        xn = at(PER, DIM, parts=ROWS)
        xT = at(CHUNKS, SPAN)
        qT = [at(CHUNKS, SPAN) for _ in range(2)]
        kT = [at(CHUNKS, PER, 2, ROWS) for _ in range(2)]
        prob = [at(4, 4, ROWS, parts=ROWS) for _ in range(2)]
        probT = at(4, 4, ROWS, parts=ROWS)
        attnT = at(4, ROWS)
        attn = at(DIM, parts=ROWS)
        attn_nT = at(CHUNKS, ROWS)
        xn2 = [at(PER, ROW, parts=ROWS) for _ in range(2)]
        x2T = at(CHUNKS, SPAN)
        gate_sb = [at(SPAN, parts=EXPERTS) for _ in range(2)]
        top = at(4, 4, parts=ROWS)
        recip = at(4, 4, parts=ROWS)
        stats = [at(PER, 6, parts=ROWS) for _ in range(2)]
        mean_var = [at(PER, 2, parts=ROWS) for _ in range(2)]
        spread = [at(PER, parts=ROWS) for _ in range(2)]
        rstd = [at(PER, parts=ROWS) for _ in range(2)]
        pt = Carve()
        pt.at = working
        images = [pt(CHANNELS, PATCH * IMAGE) for _ in range(2)]
        columns = [pt(CHANNELS, GRID, PATCH * PATCH) for _ in range(2)]
        tokw = pt(PATCH_DIM // P, DIM)
        tokb = pt(DIM)
        patchT = [pt(PATCH_DIM // P, P) for _ in range(2)]
        patch_sb = [pt(DIM) for _ in range(2)]

        rt = Carve()
        sc = rt(SPAN)
        work = [rt(SPAN) for _ in range(5)]
        ints = [rt(SPAN, dt=I32) for _ in range(3)]
        low, high, middle, count = (rt(1) for _ in range(4))
        picks = rt(2, dt=I32)
        row_top, abs_top, bound, own_top, row_sum, need, limit, sure_n, limit2 = (rt(1) for _ in range(9))
        top_row = rt(EXPERTS)
        own_sums = rt(EXPERTS)
        same_block = rt(P)
        before_block = rt(P)
        all_ones = rt(P)
        own = rt(EXPERTS)
        top_all = rt(EXPERTS)
        recip_all = rt(EXPERTS)
        slotT = [rt(len(CUTS), EXPERTS, SEGS) for _ in range(2)]
        tag = [rt(len(CUTS), SEGS) for _ in range(2)]
        tag_i = rt(3, len(CUTS), SEGS, dt=I32)
        onehot = rt(len(CUTS), SEGS, P, dt=BF16)
        match = rt(len(CUTS), SEGS, TILES)
        tagged = rt(len(CUTS), SEGS, 2, TILES, dt=BF16)
        number = rt(2, TILES)
        index = [rt(TILES, dt=U32) for _ in range(2)]
        xg = [rt(TILES, ROW) for _ in range(2)]
        xgT = rt(CHUNKS, CAPACITY)
        w1_raw, w3_raw = ([rt(HM, DIM) for _ in range(2)] for _ in range(2))
        w2_raw = [rt(CHUNKS, HIDDEN) for _ in range(2)]
        w1T, w3T = ([rt(CHUNKS, HIDDEN) for _ in range(2)] for _ in range(2))
        w2T = [rt(HM, DIM) for _ in range(2)]
        gated = [rt(3 * P) for _ in range(2)]
        hT = rt(HM, CAPACITY)
        token_w = [rt(TILES) for _ in range(2)]
        y = [rt(TILES, DIM) for _ in range(2)]

        S = ctx.enter_context(nc.psum_tensor("S", [P, 4, 512], F32))
        R = [ctx.enter_context(nc.psum_tensor(f"R{i}", [P, 512], F32)) for i in range(2)]
        B6 = ctx.enter_context(nc.psum_tensor("B6", [P, 512], F32))
        B7 = ctx.enter_context(nc.psum_tensor("B7", [P, 512], F32))

        (s_weights, s_patchw, s_text, s_rows_in) = map(sem, ("s_weights", "s_patchw", "s_text", "s_rows_in"))
        s_images = [sem(f"s_images{i}") for i in range(2)]
        s_columns = sem("s_columns")
        s_build, s_const = sem("s_build"), sem("s_const")
        s_patch, s_patch_sb = sem("s_patch"), sem("s_patch_sb")
        s_patch_out = [sem(f"s_patch_out{i}") for i in range(2)]
        s_wgT, s_wgT_sb = sem("s_wgT"), sem("s_wgT_sb")
        s_ring, s_moved = sem("s_ring"), sem("s_moved")
        s_scores, s_max, s_sub, s_exp = map(sem, ("s_scores", "s_max", "s_sub", "s_exp"))
        s_attnT, s_attnT_sb, s_turned, s_recip, s_norm = map(
            sem, ("s_attnT", "s_attnT_sb", "s_turned", "s_recip", "s_norm"))
        s_attn_nT, s_attn_nT_sb, s_proj, s_res = map(sem, ("s_attn_nT", "s_attn_nT_sb", "s_proj", "s_res"))
        s_stats = [sem(f"s_stats{i}") for i in range(2)]
        s_aggr = [sem(f"s_aggr{i}") for i in range(2)]
        s_var = [sem(f"s_var{i}") for i in range(2)]
        s_rstd = [sem(f"s_rstd{i}") for i in range(2)]
        s_normed = [sem(f"s_normed{i}") for i in range(2)]
        s_bias, s_h_out = sem("s_bias"), sem("s_h_out")
        s_stored = [sem(f"s_stored{i}") for i in range(2)]
        s_gate_out = [sem(f"s_gate_out{i}") for i in range(2)]
        s_sc, s_consts2, s_build2 = map(sem, ("s_sc", "s_consts2", "s_build2"))
        s_dve, s_rowtop, s_abs, s_pe, s_count, s_total, s_expd = map(
            sem, ("s_dve", "s_rowtop", "s_abs", "s_pe", "s_count", "s_total", "s_expd"))
        s_slots, s_slotT, s_slotT_sb = map(sem, ("s_slots", "s_slotT", "s_slotT_sb"))
        s_match, s_onehot, s_list, s_number, s_index = map(
            sem, ("s_match", "s_onehot", "s_list", "s_number", "s_index"))
        s_raw = [sem(f"s_raw{i}") for i in range(2)]
        s_xg = [sem(f"s_xg{i}") for i in range(2)]
        s_ering, s_emoved = sem("s_ering"), sem("s_emoved")
        s_hidden, s_silu, s_hT = map(sem, ("s_hidden", "s_silu", "s_hT"))
        s_wexp, s_tokw, s_y, s_y_sb = map(sem, ("s_wexp", "s_tokw", "s_y", "s_y_sb"))
        s_added = [sem(f"s_added{i}") for i in range(2)]

        block = ctx.enter_context(nc.Block())

        XG_TILES, W_TILES = TILES // 2, 6
        EXPERT_TILES = XG_TILES + W_TILES

        def moved(kind, which, i=0):
            return RING_AT[(kind, which)] + i + 1

        def ering(e, i):
            return W_TILES + e * EXPERT_TILES + i

        def in_register(eng, n):
            counts = [k if isinstance(k, int) else eng.to_reg(k) for k in n]
            eng.wait_ge(s_const, 1)
            return counts

        def tile_rows(t):
            return P if t < TILES - 1 else LAST

        @block.sync
        def _(sp):
            xv = x.rearrange("b c (g i) w -> b g c (i w)", g=GRID)
            for t in range(2):
                for c in range(CHANNELS):
                    sp.dma_start(images[t][:, c, :], xv[32 * t:32 * (t + 1), :, c, :]).then_inc(s_images[t], 16)
                if t == 0:
                    sp.dma_start(tokw, tok_W.rearrange("(k p) e -> p k e", p=P)).then_inc(s_patchw, 16)
                    sp.dma_start(tokb, tok_b.rearrange("(a e) -> a e", a=1).to_broadcast([P, DIM])
                                 ).then_inc(s_patchw, 16)
            n = ITEMS // 8
            for q in range(8):
                sp.dma_start(h[1 + PATCHES:ROWS, n * q:n * (q + 1), :],
                             txt[n * q:n * (q + 1)].rearrange("b s c -> s b c")).then_inc(s_text, 16)
            sp.dma_start(h[0:1, :, :], cls_token.to_broadcast([1, ITEMS, DIM])).then_inc(s_text, 16)
            for w, dram in ((wq, Wq), (wk, Wk), (wv, Wv)):
                sp.dma_start(w, dram.rearrange("(k p) e -> p k e", p=P)).then_inc(s_weights, 16)
            for r in range(4):
                for c in range(CHUNKS):
                    p0 = (r % 2) * 64 + c * 32
                    sp.dma_start(wo[p0:p0 + 32, r // 2, :],
                                 Wo[c * P + 32 * r:c * P + 32 * r + 32, :]).then_inc(s_weights, 16)
            sp.dma_start(wg_rows, Wg).then_inc(s_weights, 16)
            sp.dma_start(bo_rep, bo.rearrange("(a e) -> a e", a=1).to_broadcast([ROWS, DIM])
                         ).then_inc(s_weights, 16)
            by_row = patch_rows.rearrange("b (i j) e -> (b i) j e", i=GRID)
            for u in range(UNITS):
                t, j = divmod(u, GRID)
                sp.wait_ge(s_patch_sb, u + 1)
                sp.dma_start(by_row[P * t:P * (t + 1), j, :], patch_sb[u % 2]
                             ).then_inc(s_patch_out[u % 2], 16)
            for i in range(2):
                sp.wait_ge(s_patch_out[i], 16 * UNITS // 2)
            sp.dma_start(h[1:1 + PATCHES, :, :], patch_rows.rearrange("b n e -> n b e")).then_inc(s_rows_in, 16)

            def store_group(s):
                par = s.b % 2
                g = s.n(lambda g: g)
                sp.wait_ge(s_res, s.n(lambda g: PER * (g + 1)))
                sp.dma_start(out.rearrange("b s c -> s b c")[:, bass.ds(g * PER, PER), :],
                             h[:, bass.ds(g * PER, PER), :]).then_inc(s_h_out, 16)
                sp.wait_ge(s_moved, s.n(lambda g: moved("gate", g)))
                sp.dma_start(gate_rows[:, bass.ds(g * SPAN, SPAN)], gate_sb[par]).then_inc(s_gate_out[par], 16)
                sp.wait_ge(s_moved, s.n(lambda g: moved("gateT", g)))
                sp.dma_start(stored.rearrange("(b s) c -> s b c", s=ROWS)[:, bass.ds(g * PER, PER), :],
                             xn2[par]).then_inc(s_stored[par], 16)

            for g in range(2):
                store_group(Step(g))
            with sp.Fori(0, GROUPS // 2 - 3) as turn:
                for g in range(2, 4):
                    store_group(Step(g, turn, stride=2))
            for g in range(GROUPS - 4, GROUPS):
                store_group(Step(g))

            for i in range(2):
                sp.wait_ge(s_gate_out[i], 16 * GROUPS // 2)
                sp.wait_ge(s_stored[i], 16 * GROUPS // 2)
            sp.wait_ge(s_h_out, 16 * GROUPS)
            sp.dma_start(sc, gate_rows.rearrange("e (g t) -> (e g) t", g=SEGS)).then_inc(s_sc, 16)

            def load_expert(s):
                par = s.b % 2
                if s.b >= 0:
                    sp.wait_ge(s_ering, s.n(lambda e: ering(e - 1, XG_TILES + W_TILES)))
                e = s.n(lambda e: e + 2)
                sp.dma_start(w1_raw[par], W1.rearrange("e (m p) c -> p e m c", p=P)[:, e]).then_inc(s_raw[par], 16)
                sp.dma_start(w3_raw[par], W3.rearrange("e (m p) c -> p e m c", p=P)[:, e]).then_inc(s_raw[par], 16)
                sp.dma_start(w2_raw[par], W2.rearrange("e (m p) c -> p e m c", p=P)[:, e]).then_inc(s_raw[par], 16)

            load_expert(Step(-2))
            load_expert(Step(-1))
            with sp.Fori(0, EXPERTS // 2 - 1) as turn:
                for e in range(2):
                    load_expert(Step(e, turn, stride=2))
            for i in range(2):
                sp.wait_ge(s_added[i], 16 * TILES * EXPERTS // 2)

        @block.gpsimd
        def _(pool):
            pool.memset(ident[:, :], 0.0)
            pool.memset(mask, 0.0)
            pool.memset(minus_half, -0.5)
            pool.memset(parity, 1.0)
            for i in range(2):
                pool.memset(v[i], 0.0)
            pool.iota(iota_f[:, :], pattern=[[1, P]], base=0, channel_multiplier=0,
                      allow_small_or_imprecise_dtypes=True).then_inc(s_build, 1)
            pool.wait_ge(s_build, 1)
            for q in range(4):
                pool.memset(parity[32 * q:32 * q + 16, 1:2], 0.0).then_inc(s_build, 1)
                pool.wait_ge(s_build, q + 2)
            pool.affine_select(out=ident[:, :], in_=ident[:, :], compare_op=ALU.not_equal, fill=1.0, base=0,
                               pattern=[[-1, P]], channel_multiplier=1)
            pool.affine_select(out=mask, in_=mask, compare_op=ALU.is_ge, fill=MASKED, base=0,
                               pattern=[[0, 4], [-1, ROWS]], channel_multiplier=1)
            for i in range(2):
                last = pool.memset(v[i].rearrange("p a b c -> p (a b) c")[:, :, HEAD:HEAD + 1], 1.0)
            last.then_inc(s_build, 1)
            pool.wait_ge(s_build, 6)
            pool.tensor_copy(ident_b[:, :], ident[:, :])
            pool.tensor_scalar(parity[:, 0:1], parity[:, 1:2], -1.0, 1.0, ALU.mult, ALU.add).then_inc(s_const, 1)

            def power(norm, count):
                pool.wait_ge(s_var[norm], count)
                pool.tensor_tensor(rstd[norm], spread[norm], minus_half, ALU.pow).then_inc(s_rstd[norm], 1)

            def add_bias(g, count):
                pool.wait_ge(s_normed[0], count)
                rows = h[:, bass.ds(g * PER, PER), :]
                pool.tensor_tensor(rows, rows, bo_rep.unsqueeze(1).to_broadcast([ROWS, PER, DIM]), ALU.add
                                   ).then_inc(s_bias, 1)

            pool.wait_ge(s_weights, 16 * 13)
            for g in range(2):
                power(0, g + 1)
                add_bias(g, g + 1)

            def step(s):
                b = s.b
                if b % PER == 2 and 0 <= b // PER - 1 < GROUPS:
                    power(1, s.n(lambda b: b // PER))
                if b % PER == 3 and b // PER + 2 < GROUPS:
                    power(0, s.n(lambda b: b // PER + 3))
                    add_bias(s.n(lambda b: b // PER + 2), s.n(lambda b: b // PER + 3))

            run_steps(pool, step)

            pool.wait_ge(s_sc, 16)
            pool.memset(all_ones, 1.0)
            pool.memset(own, 1.0)
            pool.memset(work[3], 0.0)
            for i in range(2):
                pool.memset(slotT[i], -1.0)
                pool.memset(xg[i][:, TILES - 1, :], 0.0)
            pool.iota(tag_i[:, 0], pattern=[[P, len(CUTS)], [SPAN, SEGS]], base=0, channel_multiplier=1
                      ).then_inc(s_build2, 1)
            pool.wait_ge(s_build2, 1)
            pool.affine_select(out=own, in_=own, compare_op=ALU.is_ge, fill=0.0, base=0,
                               pattern=[[-SEGS, EXPERTS]], channel_multiplier=1).then_inc(s_build2, 1)
            pool.wait_ge(s_build2, 2)
            pool.affine_select(out=own, in_=own, compare_op=ALU.is_ge, fill=0.0, base=SEGS - 1,
                               pattern=[[SEGS, EXPERTS]], channel_multiplier=-1).then_inc(s_build2, 1)
            pool.wait_ge(s_build2, 3)
            pool.tensor_copy(same_block.rearrange("p (e s) -> p e s", s=SEGS),
                             own.unsqueeze(2).to_broadcast([P, EXPERTS, SEGS])).then_inc(s_build2, 1)
            pool.wait_ge(s_build2, 4)
            pool.affine_select(out=before_block, in_=same_block, compare_op=ALU.is_gt, fill=0.0, base=0,
                               pattern=[[1, P]], channel_multiplier=-1).then_inc(s_consts2, 1)
            pool.wait_ge(s_rowtop, 2)
            pool.partition_all_reduce(bound, abs_top, P, bass.bass_isa.ReduceOp.max).then_inc(s_abs, 1)

            def gather(s, ahead):
                par = (s.b + ahead) % 2
                chosen, used = in_register(pool, [s.n(lambda e: e + ahead + 1),
                                                  s.n(lambda e: TILES * max(e + ahead - 1, 0))])
                pool.wait_ge(s_index, chosen)
                pool.wait_ge(s_y_sb, used)
                for t in range(TILES):
                    n = tile_rows(t)
                    pool.indirect_dma_start(
                        out=xg[par][0:n, t, :], out_offset=None, in_=stored,
                        in_offset=bass.IndirectOffsetOnAxis(ap=index[par][0:n, t:t + 1], axis=0),
                    ).then_inc(s_xg[par], 16)

            def scatter(s):
                par = s.b % 2
                weighted, landed = in_register(pool, [s.n(lambda e: TILES * (e + 1)),
                                                      s.n(lambda e: 16 * TILES * ((e + 1) // 2))])
                pool.wait_ge(s_y_sb, weighted)
                pool.wait_ge(s_added[1 - par], landed)
                for t in range(TILES):
                    n = tile_rows(t)
                    pool.indirect_dma_start(
                        out=out_rows, out_offset=bass.IndirectOffsetOnAxis(ap=index[par][0:n, t:t + 1], axis=0),
                        in_=y[par][0:n, t, :], in_offset=None, compute_op=ALU.add,
                    ).then_inc(s_added[par], 16)

            def expert(s):
                if s.b + 1 < EXPERTS:
                    gather(s, 1)
                scatter(s)

            gather(Step(0), 0)
            gather(Step(0), 1)
            scatter(Step(0))
            with pool.Fori(0, EXPERTS // 2 - 1) as turn:
                for e in range(1, 3):
                    expert(Step(e, turn, stride=2))
            expert(Step(EXPERTS - 1))

        @block.scalar
        def _(act):
            def move(dst, src, scale=None, signal=True):
                ins = act.activation(dst, src, ACT.Copy) if scale is None else \
                    act.activation(dst, src, ACT.Identity, scale=scale)
                if signal:
                    ins.then_inc(s_moved, 1)

            for u in range(UNITS):
                if u >= 2:
                    act.wait_ge(s_patch, u - 1)
                act.wait_ge(s_ring, 2 * u + 1)
                move(patchT[u % 2][:, 0:4, :], R[0][:, :].rearrange("p (k n) -> p k n", k=4))
                act.wait_ge(s_ring, 2 * u + 2)
                move(patchT[u % 2][:, 4:6, :], R[1][:, 0:2 * P].rearrange("p (k n) -> p k n", k=2))
            act.wait_ge(s_const, 1)

            def piece(kind, s, which, gpar):
                def tile(i):
                    act.wait_ge(s_ring, s.n(lambda b: moved(kind, which(b), i)))
                    return R[(RING_AT[(kind, which(s.b))] + i) % 2]

                if kind == "xT":
                    for i in range(2):
                        move(xT[:, i, :], tile(i)[:, 0:SPAN])
                if kind == "q":
                    for i in range(2):
                        move(qT[gpar][:, i, :], tile(i)[:, 0:SPAN])
                if kind == "k":
                    for i in range(2):
                        src = tile(i)[:, 0:SPAN].rearrange("p (i t) -> p i t", i=PER)
                        for odd in range(2):
                            move(kT[gpar][:, i, :, odd, :], src, parity[:, odd:odd + 1], signal=odd == 1)
                if kind == "v":
                    for i in range(2):
                        move(v[gpar][:, 2 * i:2 * i + 2, :, 0:HEAD],
                             tile(i)[0:ROWS, :].rearrange("p (i h d) -> p i h d", i=2, d=HEAD))
                if kind == "x2T":
                    for i in range(2):
                        move(x2T[:, i, :], tile(i)[:, 0:SPAN])
                if kind == "gate":
                    if which(s.b) >= 2:
                        act.wait_ge(s_gate_out[gpar], s.n(lambda b: 16 * (which(b) // 2)))
                    move(gate_sb[gpar], tile(0)[0:EXPERTS, 0:SPAN])
                if kind == "gateT":
                    move(xn2[gpar][:, :, DIM:ROW],
                         tile(0)[0:ROWS, 0:PER * EXPERTS].rearrange("p (i e) -> p i e", i=PER))

            for kind in ("xT", "q", "k", "v"):
                piece(kind, Step(0), lambda b: 0, 0)

            def step(s):
                b = s.b
                if 2 <= b < ITEMS + 2:
                    act.wait_ge(s_attn_nT, s.n(lambda b: b - 1))
                    if b > 2:
                        act.wait_ge(s_proj, s.n(lambda b: b - 2))
                    act.activation(attn_nT, B7[:, 0:2 * ROWS].rearrange("p (c t) -> p c t", c=2), ACT.Copy
                                   ).then_inc(s_attn_nT_sb, 1)
                if 1 <= b <= ITEMS:
                    if b > 1:
                        act.wait_ge(s_attnT, s.n(lambda b: b - 1))
                    first = RING_AT[("probsT", b - 1)]
                    for r in range(4):
                        act.wait_ge(s_ring, s.n(lambda b: moved("probsT", b - 1, r)))
                        move(probT[:, r], R[(first + r) % 2][0:ROWS, 0:SPAN].rearrange("p (j t) -> p j t", j=4))
                if b < ITEMS:
                    act.wait_ge(s_sub, s.n(lambda b: b + 1))
                    act.activation(prob[b % 2], prob[b % 2], ACT.Exp, scale=HEAD ** -0.5).then_inc(s_exp, 1)
                if 1 <= b <= ITEMS:
                    act.wait_ge(s_attnT, s.n(lambda b: b))
                    if b > 1:
                        act.wait_ge(s_turned, s.n(lambda b: b - 1))
                    act.activation(attnT, B6[:, 0:SPAN].rearrange("p (r t) -> p r t", r=4), ACT.Copy
                                   ).then_inc(s_attnT_sb, 1)
                seen = set()
                for kind, which in ring_tiles(b):
                    if kind != "probsT" and kind not in seen:
                        seen.add(kind)
                        lag = which - b // PER
                        piece(kind, s, lambda b, lag=lag: b // PER + lag, which % 2)

            run_steps(act, step)

            act.wait_ge(s_dve, OWN_TOP)
            act.activation(work[0], sc, ACT.Exp, bias=own_top).then_inc(s_expd, 1)

            def emove(i, dst, src):
                act.activation(dst, src, ACT.Copy).then_inc(s_emoved, 1)

            def weights(s, first):
                par = (s.b + 1) % 2
                for i in range(W_TILES):
                    act.wait_ge(s_ering, s.n(lambda e: ering(e, XG_TILES + i + 1)))
                    src = R[ering(s.b, XG_TILES + i) % 2]
                    if i < 4:
                        dst = (w1T if i < 2 else w3T)[par][:, i % 2, :]
                        emove(i, dst, src[:, :])
                    else:
                        emove(i, w2T[par][:, 2 * (i - 4):2 * (i - 4) + 2, :],
                              src[:, :].rearrange("p (m c) -> p m c", m=2))

            weights(Step(-1), None)

            def expert(s):
                par = s.b % 2
                e = s.n(lambda e: e)
                for i in range(XG_TILES):
                    act.wait_ge(s_ering, s.n(lambda e: ering(e, i + 1)))
                    w = tile_rows(2 * i + 1) + P
                    emove(i, xgT[:, :, 2 * P * i:2 * P * i + w],
                          R[ering(s.b, i) % 2][:, :].rearrange("p (c t) -> p c t", c=2)[:, :, 0:w])
                act.wait_ge(s_xg[par], s.n(lambda e: 16 * TILES * (e // 2 + 1)))
                act.activation(token_w[par], xg[par][:, :, bass.ds(e + DIM, 1)].rearrange("p t a -> p (t a)"),
                               ACT.Exp, bias=top_all[:, bass.ds(e, 1)]).then_inc(s_wexp, 1)
                for i in range(2 * HM):
                    t0, t1 = HALVES[i // HM]
                    n = sum(tile_rows(t) for t in range(t0, t1))
                    act.wait_ge(s_hidden, s.n(lambda e: 2 * HM * e + i + 1))
                    if i >= 2:
                        act.wait_ge(s_hT, s.n(lambda e: 2 * HM * e + i - 1))
                    act.activation(gated[i % 2][:, 0:n], S[:, 2 * (i % 2), 0:n], ACT.Silu).then_inc(s_silu, 1)
                if s.b + 1 < EXPERTS:
                    weights(s, None)
                act.wait_ge(s_tokw, s.n(lambda e: e + 1))
                if s.b >= 2:
                    act.wait_ge(s_added[par], s.n(lambda e: 16 * TILES * (e // 2)))
                for t in range(TILES):
                    n = tile_rows(t)
                    act.wait_ge(s_y, s.n(lambda e: TILES * e + t + 1))
                    act.activation(y[par][0:n, t, :], (B6, B7)[t % 2][0:n, 0:DIM], ACT.Identity,
                                   scale=token_w[par][0:n, t:t + 1]).then_inc(s_y_sb, 1)

            run_experts(act, expert)

        @block.vector
        def _(dve):
            for t in range(2):
                dve.wait_ge(s_images[t], 16 * CHANNELS)
                for c in range(CHANNELS):
                    last = dve.tensor_copy(
                        columns[t][:, c].rearrange("p j (i w) -> p j i w", i=PATCH),
                        images[t][:, c, :].rearrange("p (i j w) -> p j i w", i=PATCH, j=GRID))
                last.then_inc(s_columns, 1)
            dve.wait_ge(s_patchw, 32)
            for u in range(UNITS):
                dve.wait_ge(s_patch, u + 1)
                if u >= 2:
                    dve.wait_ge(s_patch_out[u % 2], 16 * (u // 2))
                dve.tensor_tensor(patch_sb[u % 2], (B6, B7)[u % 2][:, 0:DIM], tokb, ALU.add
                                  ).then_inc(s_patch_sb, 1)
            dve.wait_ge(s_wgT, 1)
            dve.tensor_copy(wgT, B6[:, 0:CHUNKS * EXPERTS].rearrange("p (c e) -> p c e", c=CHUNKS)
                            ).then_inc(s_wgT_sb, 1)

            def norm_stats(norm, g, count):
                for i in range(PER):
                    last = dve.bn_stats(stats[norm][:, i, :], h[:, g * PER + i, :])
                last.then_inc(s_stats[norm], 1)
                count, = in_register(dve, [count])
                dve.wait_ge(s_stats[norm], count)
                for i in range(PER):
                    last = dve.bn_aggr(mean_var[norm][:, i, :], stats[norm][:, i, :])
                last.then_inc(s_aggr[norm], 1)
                dve.wait_ge(s_aggr[norm], count)
                dve.tensor_scalar(spread[norm], mean_var[norm][:, :, 1], EPS, None, ALU.add
                                  ).then_inc(s_var[norm], 1)

            def norm_rows(norm, g, dst, count):
                dve.wait_ge(s_rstd[norm], count)
                for i in range(PER):
                    last = dve.tensor_scalar(dst[:, i, 0:DIM], h[:, g * PER + i, :],
                                             mean_var[norm][:, i, 0:1], rstd[norm][:, i:i + 1],
                                             ALU.subtract, ALU.mult)
                last.then_inc(s_normed[norm], 1)

            dve.wait_ge(s_text, 16 * 9)
            dve.wait_ge(s_rows_in, 16)
            dve.wait_ge(s_const, 1)
            for g in range(2):
                norm_stats(0, g, g + 1)
                if g > 0:
                    dve.wait_ge(s_ring, moved("xT", 0, 1))
                norm_rows(0, g, xn, g + 1)

            def step(s):
                b = s.b
                second = b % PER == 2 and 0 <= b // PER - 1 < GROUPS
                first = b % PER == 3 and b // PER + 2 < GROUPS
                if 2 <= b < ITEMS + 2:
                    turned = B7[0:ROWS, :].rearrange("p (h f) -> p h f", f=32)
                    dve.wait_ge(s_turned, s.n(lambda b: b - 1))
                    if b > 2:
                        dve.wait_ge(s_attn_nT, s.n(lambda b: b - 2))
                    dve.reciprocal(recip.rearrange("p r j -> p (r j)"), turned[:, :, HEAD]).then_inc(s_recip, 1)
                    dve.wait_ge(s_recip, s.n(lambda b: b - 1))
                    dve.tensor_tensor(attn.rearrange("p (h d) -> p h d", d=HEAD), turned[:, :, 0:HEAD],
                                      recip.rearrange("p r j -> p (r j)").unsqueeze(2)
                                      .to_broadcast([ROWS, HEADS, HEAD]), ALU.mult).then_inc(s_norm, 1)
                if second:
                    dve.wait_ge(s_res, s.n(lambda b: b // PER * PER))
                    norm_stats(1, s.n(lambda b: b // PER - 1), s.n(lambda b: b // PER))
                if first:
                    norm_stats(0, s.n(lambda b: b // PER + 2), s.n(lambda b: b // PER + 3))
                if b < ITEMS:
                    scores = S[0:ROWS, :, 0:SPAN].rearrange("p r (j t) -> p r j t", j=4)
                    dve.wait_ge(s_scores, s.n(lambda b: b + 1))
                    dve.tensor_reduce(top, scores, AX.X, ALU.max).then_inc(s_max, 1)
                    dve.wait_ge(s_max, s.n(lambda b: b + 1))
                    if b >= 2:
                        dve.wait_ge(s_ring, s.n(lambda b: moved("probsT", b - 2, 3)))
                    dve.tensor_tensor(prob[b % 2], scores, top.unsqueeze(3).to_broadcast([ROWS, 4, 4, ROWS]),
                                      ALU.subtract).then_inc(s_sub, 1)
                if second:
                    par = (b // PER - 1) % 2
                    if b // PER - 1 >= 2:
                        dve.wait_ge(s_stored[par], s.n(lambda b: 16 * ((b // PER - 1) // 2)))
                    norm_rows(1, s.n(lambda b: b // PER - 1), xn2[par], s.n(lambda b: b // PER))
                if first:
                    dve.wait_ge(s_ring, s.n(lambda b: moved("xT", b // PER + 1, 1)))
                    norm_rows(0, s.n(lambda b: b // PER + 2), xn, s.n(lambda b: b // PER + 3))
                if 2 <= b < ITEMS + 2:
                    if (b - 2) % PER == 0:
                        dve.wait_ge(s_bias, s.n(lambda b: (b - 2) // PER + 1))
                    dve.wait_ge(s_proj, s.n(lambda b: b - 1))
                    row = h[:, s.n(lambda b: b - 2), :]
                    dve.tensor_tensor(row, row, B7[0:ROWS, DIM:2 * DIM], ALU.add).then_inc(s_res, 1)

            run_steps(dve, step)

            chain = [0]

            def then(ins):
                chain[0] += 1
                ins.then_inc(s_dve, 1)
                dve.wait_ge(s_dve, chain[0])

            dve.wait_ge(s_sc, 16)
            dve.wait_ge(s_consts2, 1)
            dve.tensor_reduce(row_top, sc, AX.X, ALU.max).then_inc(s_rowtop, 1)
            dve.tensor_reduce(abs_top, sc, AX.X, ALU.max, apply_absolute_value=True).then_inc(s_rowtop, 1)
            dve.wait_ge(s_pe, 1)
            then(dve.tensor_reduce(top_row[0:1, :], B7[0:1, 0:P].rearrange("p (e s) -> p e s", s=SEGS),
                                   AX.X, ALU.max, negate=True))
            dve.wait_ge(s_pe, 2)
            then(dve.tensor_copy(top_all, B7[:, DIM:DIM + EXPERTS]))
            then(dve.tensor_tensor_reduce(own_sums, top_all, own, 1.0, 0.0, ALU.mult, ALU.add, own_top))
            assert chain[0] == OWN_TOP
            dve.wait_ge(s_abs, 1)
            then(dve.tensor_scalar(high, bound, 1.001, 1e-30, ALU.mult, ALU.add))
            then(dve.tensor_scalar(low, high, -1.0, None, ALU.mult))
            start, links = chain[0], 4
            with dve.Fori(0, BISECTIONS) as turn:
                def link(ins, k):
                    ins.then_inc(s_dve, 1)
                    count, = in_register(dve, [turn * links + (start + k)])
                    dve.wait_ge(s_dve, count)

                link(dve.tensor_scalar(middle, low, high, 0.5, ALU.add, ALU.mult), 1)
                dve.tensor_scalar(work[1], sc, middle, None, ALU.is_ge, ALU.add, accum_out=count
                                  ).then_inc(s_count, 1)
                dve.wait_ge(s_total, turn + 1)
                link(dve.tensor_scalar(picks[:, 0:1], B6[:, 0:1], float(CAPACITY), None, ALU.is_ge), 2)
                link(dve.tensor_scalar(picks[:, 1:2], B6[:, 0:1], float(CAPACITY), None, ALU.is_lt), 3)
                dve.copy_predicated(low, picks[:, 0:1], middle)
                link(dve.copy_predicated(high, picks[:, 1:2], middle), 4)
            chain[0] += links * BISECTIONS
            sure, maybe, order, zero = work[1], work[2], work[4], work[3]
            then(dve.tensor_scalar(sure, sc, high, None, ALU.is_ge, ALU.add, accum_out=count))
            dve.tensor_copy(sure_n, count).then_inc(s_count, 1)
            then(dve.scalar_tensor_tensor(maybe, sc, low, sure, ALU.is_ge, ALU.subtract))
            then(dve.tensor_tensor_scan(order, maybe, zero, 0.0, ALU.add, ALU.add))
            dve.tensor_copy(limit, order[:, SPAN - 1:SPAN]).then_inc(s_count, 1)
            dve.wait_ge(s_total, BISECTIONS + 2)
            then(dve.tensor_scalar(need, B6[:, 0:1], -1.0, float(CAPACITY), ALU.mult, ALU.add))
            then(dve.tensor_tensor(need, need, B6[:, 1:2], ALU.subtract))
            then(dve.scalar_tensor_tensor(maybe, order, need, maybe, ALU.is_le, ALU.mult))
            then(dve.tensor_tensor(sure, sure, maybe, ALU.add))
            then(dve.tensor_tensor_scan(order, sure, zero, 0.0, ALU.add, ALU.add))
            dve.tensor_copy(limit2, order[:, SPAN - 1:SPAN]).then_inc(s_count, 1)
            dve.wait_ge(s_expd, 1)
            then(dve.tensor_tensor_reduce(maybe, work[0], sure, 1.0, 0.0, ALU.mult, ALU.add, row_sum))
            dve.tensor_scalar(own_sums, own, row_sum, None, ALU.mult).then_inc(s_count, 1)
            dve.wait_ge(s_total, BISECTIONS + 3)
            then(dve.scalar_tensor_tensor(order, order, B6[:, 2:3], sure, ALU.add, ALU.mult))
            then(dve.tensor_scalar(ints[0], order, -1.0, None, ALU.add))
            dve.tensor_scalar(ints[1], ints[0], 7, None, ALU.arith_shift_right)
            then(dve.tensor_scalar(ints[2], ints[0], P - 1, None, ALU.bitwise_and))
            dve.tensor_copy(work[1], ints[1])
            dve.tensor_copy(work[2], ints[2]).then_inc(s_slots, 1)
            dve.tensor_scalar(tag_i[:, 1], tag_i[:, 0], 6, None, ALU.arith_shift_right)
            then(dve.tensor_scalar(tag_i[:, 2], tag_i[:, 0], TAG - 1, None, ALU.bitwise_and))
            dve.tensor_copy(tag[0], tag_i[:, 1])
            then(dve.tensor_copy(tag[1], tag_i[:, 2]))
            dve.wait_ge(s_total, BISECTIONS + 4)
            then(dve.reciprocal(recip_all, B7[:, DIM:DIM + EXPERTS]))
            for i in range(2):
                dve.wait_ge(s_slotT, len(CUTS) * (i + 1))
                for c, (t0, n) in enumerate(CUTS):
                    last = dve.tensor_copy(slotT[i][0:n, c].rearrange("p e s -> p (e s)"),
                                           S[0:n, i, c * P:(c + 1) * P])
            then(last)

            def one_hots(s, ahead):
                if s.b + ahead > 0:
                    dve.wait_ge(s_list, s.n(lambda e: e + ahead))
                at_e = s.n(lambda e: e + ahead)
                tile_of = slotT[0][:, :, bass.ds(at_e, 1), :].rearrange("p c a s -> p c (a s)")
                row_of = slotT[1][:, :, bass.ds(at_e, 1), :].rearrange("p c a s -> p c (a s)")
                shape = [P, len(CUTS), SEGS]
                dve.tensor_tensor(match, tile_of.unsqueeze(3).to_broadcast(shape + [TILES]),
                                  iota_f[:, 0:TILES].unsqueeze(1).unsqueeze(1).to_broadcast(shape + [TILES]),
                                  ALU.is_equal).then_inc(s_match, 1)
                dve.tensor_tensor(onehot, row_of.unsqueeze(3).to_broadcast(shape + [P]),
                                  iota_f[:, :].unsqueeze(1).unsqueeze(1).to_broadcast(shape + [P]), ALU.is_equal)
                dve.wait_ge(s_match, s.n(lambda e: e + ahead + 1))
                for i in range(2):
                    last = dve.tensor_tensor(tagged[:, :, :, i, :], match,
                                             tag[i].unsqueeze(3).to_broadcast(shape + [TILES]), ALU.mult)
                last.then_inc(s_onehot, 1)

            def list_tokens(s, ahead):
                par = (s.b + ahead) % 2
                dve.wait_ge(s_list, s.n(lambda e: e + ahead + 1))
                dve.tensor_copy(number, B7[:, DIM:DIM + 2 * TILES].rearrange("p (a t) -> p a t", a=2)
                                ).then_inc(s_number, 1)
                dve.wait_ge(s_number, s.n(lambda e: e + ahead + 1))
                if s.b + ahead >= 2:
                    dve.wait_ge(s_added[par], s.n(lambda e: 16 * TILES * ((e + ahead) // 2)))
                dve.scalar_tensor_tensor(index[par], number[:, 0], float(TAG), number[:, 1], ALU.mult, ALU.add
                                         ).then_inc(s_index, 1)

            one_hots(Step(0), 0)
            list_tokens(Step(0), 0)
            one_hots(Step(0), 1)

            def expert(s):
                par = s.b % 2
                if s.b + 1 < EXPERTS:
                    list_tokens(s, 1)
                dve.wait_ge(s_wexp, s.n(lambda e: e + 1))
                dve.tensor_scalar(token_w[par], token_w[par], recip_all[:, bass.ds(s.n(lambda e: e), 1)], None,
                                  ALU.mult).then_inc(s_tokw, 1)
                for i in range(2 * HM):
                    t0, t1 = HALVES[i // HM]
                    n = sum(tile_rows(t) for t in range(t0, t1))
                    dve.wait_ge(s_silu, s.n(lambda e: 2 * HM * e + i + 1))
                    dve.tensor_tensor(hT[:, i % HM, t0 * P:t0 * P + n], gated[i % 2][:, 0:n],
                                      S[:, 2 * (i % 2) + 1, 0:n], ALU.mult).then_inc(s_hT, 1)
                if s.b + 2 < EXPERTS:
                    one_hots(s, 2)

            run_experts(dve, expert)

        @block.tensor
        def _(pe):
            def ring_free(n):
                pe.wait_ge(s_moved, n)

            def turn_patches(u):
                t, j = divmod(u, GRID)
                if u % GRID == 0:
                    pe.wait_ge(s_columns, t + 1)
                for i in range(2):
                    if 2 * u + i >= 2:
                        ring_free(2 * u + i - 1)
                    for k in range(4 * i, min(4 * i + 4, PATCH_DIM // P)):
                        c, half = divmod(k, 2)
                        last = pe.transpose(R[i][:, P * (k % 4):P * (k % 4 + 1)],
                                            columns[t][:, c, j, P * half:P * (half + 1)], ident[:, :])
                    last.then_inc(s_ring, 1)

            def project_patches(u):
                pe.wait_ge(s_moved, 2 * u + 2)
                if u >= 2:
                    pe.wait_ge(s_patch_sb, u - 1)
                for k in range(PATCH_DIM // P):
                    last = pe.matmul((B6, B7)[u % 2][:, 0:DIM], patchT[u % 2][:, k, :], tokw[:, k, :],
                                     start=(k == 0), stop=(k == PATCH_DIM // P - 1))
                last.then_inc(s_patch, 1)

            pe.wait_ge(s_const, 1)
            turn_patches(0)
            pe.wait_ge(s_patchw, 32)
            for u in range(UNITS):
                if u + 1 < UNITS:
                    turn_patches(u + 1)
                project_patches(u)
            pe.wait_ge(s_weights, 16 * 13)
            pe.wait_ge(s_patch_sb, UNITS)
            for c in range(CHUNKS):
                last = pe.transpose(B6[:, c * EXPERTS:(c + 1) * EXPERTS], wg_rows[:, c * P:(c + 1) * P],
                                    ident[0:EXPERTS, 0:EXPERTS])
            last.then_inc(s_wgT, 1)

            def piece(kind, s, which, gpar):
                def tile(i):
                    ring_free(s.n(lambda b: RING_AT[(kind, which(b))] + i - 1))
                    return R[(RING_AT[(kind, which(s.b))] + i) % 2]

                if kind == "xT":
                    pe.wait_ge(s_normed[0], s.n(lambda b: which(b) + 1))
                    for i in range(2):
                        dst = tile(i)
                        for j in range(PER):
                            last = pe.transpose(dst[:, ROWS * j:ROWS * (j + 1)], xn[:, j, P * i:P * (i + 1)],
                                                ident[0:ROWS, 0:ROWS])
                        last.then_inc(s_ring, 1)
                if kind in ("q", "k"):
                    w = wq if kind == "q" else wk
                    pe.wait_ge(s_moved, s.n(lambda b: moved("xT", which(b), 1)))
                    for i in range(2):
                        dst = tile(i)
                        for k in range(CHUNKS):
                            last = pe.matmul(dst[:, 0:SPAN], w[:, k, P * i:P * (i + 1)], xT[:, k, :],
                                             start=(k == 0), stop=(k == CHUNKS - 1))
                        last.then_inc(s_ring, 1)
                if kind == "v":
                    for i in range(2):
                        dst = tile(i)
                        for j in range(2):
                            for k in range(CHUNKS):
                                last = pe.matmul(dst[0:ROWS, DIM * j:DIM * (j + 1)],
                                                 xT[:, k, ROWS * (2 * i + j):ROWS * (2 * i + j + 1)], wv[:, k, :],
                                                 start=(k == 0), stop=(k == CHUNKS - 1))
                        last.then_inc(s_ring, 1)
                if kind == "x2T":
                    pe.wait_ge(s_normed[1], s.n(lambda b: which(b) + 1))
                    for i in range(2):
                        dst = tile(i)
                        for j in range(PER):
                            last = pe.transpose(dst[:, ROWS * j:ROWS * (j + 1)],
                                                xn2[gpar][:, j, P * i:P * (i + 1)], ident[0:ROWS, 0:ROWS])
                        last.then_inc(s_ring, 1)
                if kind == "gate":
                    dst = tile(0)
                    pe.wait_ge(s_moved, s.n(lambda b: moved("x2T", which(b), 1)))
                    for k in range(CHUNKS):
                        last = pe.matmul(dst[0:EXPERTS, 0:SPAN], wgT[:, k, :], x2T[:, k, :],
                                         start=(k == 0), stop=(k == CHUNKS - 1))
                    last.then_inc(s_ring, 1)
                if kind == "gateT":
                    free, = in_register(pe, [s.n(lambda b: max(RING_AT[("gateT", which(b))] - 1,
                                                               moved("gate", which(b))))])
                    dst = R[RING_AT[("gateT", which(s.b))] % 2]
                    ring_free(free)
                    for j in range(PER):
                        last = pe.transpose(dst[0:ROWS, EXPERTS * j:EXPERTS * (j + 1)],
                                            gate_sb[gpar][:, ROWS * j:ROWS * (j + 1)],
                                            ident[0:EXPERTS, 0:EXPERTS])
                    last.then_inc(s_ring, 1)

            for kind in ("xT", "q", "k", "v"):
                piece(kind, Step(0), lambda b: 0, 0)
            pe.wait_ge(s_wgT_sb, 1)

            def head(r, j):
                return HEADS // 2 * (j // 2) + 2 * r + j % 2

            def step(s):
                b = s.b
                if 2 <= b < ITEMS + 2:
                    pe.wait_ge(s_attnT_sb, s.n(lambda b: b - 1))
                    if b > 2:
                        pe.wait_ge(s_res, s.n(lambda b: b - 2))
                    for r in range(4):
                        last = pe.transpose(B7[0:ROWS, P * r:P * (r + 1)], attnT[:, r, :], ident[:, :])
                    last.then_inc(s_turned, 1)
                if b < ITEMS:
                    gpar, item = b // PER % 2, b % PER
                    if item == 0:
                        pe.wait_ge(s_moved, s.n(lambda b: moved("k", b // PER, 1)))
                    if b > 0:
                        pe.wait_ge(s_sub, s.n(lambda b: b))
                    for r in range(4):
                        pe.matmul(S[0:ROWS, r, 0:SPAN], ident_b[0:ROWS, 0:ROWS],
                                  mask.rearrange("p j t -> p (j t)"), start=True, stop=False,
                                  skip_group_check=True)
                    for c in range(CHUNKS):
                        for r in range(4):
                            q = 32 * r
                            last = pe.matmul(S[0:ROWS, r, 2 * ROWS * c:2 * ROWS * (c + 1)],
                                             qT[gpar][q:q + 32, c, ROWS * item:ROWS * (item + 1)],
                                             kT[gpar][q:q + 32, c, item].rearrange("p o t -> p (o t)"),
                                             start=False, stop=(c == 1), skip_group_check=True)
                    last.then_inc(s_scores, 1)
                if 2 <= b < ITEMS + 2:
                    pe.wait_ge(s_norm, s.n(lambda b: b - 1))
                    for c in range(CHUNKS):
                        last = pe.transpose(B7[:, ROWS * c:ROWS * (c + 1)], attn[:, P * c:P * (c + 1)],
                                            ident[0:ROWS, 0:ROWS])
                    last.then_inc(s_attn_nT, 1)
                if 1 <= b <= ITEMS:
                    gpar, item = (b - 1) // PER % 2, (b - 1) % PER
                    first = RING_AT[("probsT", b - 1)]
                    pe.wait_ge(s_exp, s.n(lambda b: b))
                    if item == 0:
                        pe.wait_ge(s_moved, s.n(lambda b: moved("v", (b - 1) // PER, 1)))

                    def turn(r):
                        ring_free(s.n(lambda b: RING_AT[("probsT", b - 1)] + r - 1))
                        for j in range(4):
                            last = pe.transpose(R[(first + r) % 2][0:ROWS, ROWS * j:ROWS * (j + 1)],
                                                prob[(b - 1) % 2][:, r, j, :], ident[0:ROWS, 0:ROWS])
                        last.then_inc(s_ring, 1)

                    def outputs(r):
                        pe.wait_ge(s_moved, s.n(lambda b: moved("probsT", b - 1, r)))
                        if r == 0 and b > 1:
                            pe.wait_ge(s_attnT_sb, s.n(lambda b: b - 1))
                        for j in range(4):
                            last = pe.matmul(B6[32 * j:32 * (j + 1), ROWS * r:ROWS * (r + 1)],
                                             v[gpar][:, item, head(r, j), :], probT[:, r, j, :],
                                             start=True, stop=True, skip_group_check=True)
                        if r == 3:
                            last.then_inc(s_attnT, 1)

                    turn(0)
                    turn(1)
                    outputs(0)
                    turn(2)
                    outputs(1)
                    turn(3)
                    outputs(2)
                    outputs(3)
                if 2 <= b < ITEMS + 2:
                    pe.wait_ge(s_attn_nT_sb, s.n(lambda b: b - 1))
                    for c in range(CHUNKS):
                        last = pe.matmul(B7[0:ROWS, DIM:2 * DIM], attn_nT[:, c, :], wo[:, c, :],
                                         start=(c == 0), stop=(c == CHUNKS - 1))
                    last.then_inc(s_proj, 1)
                seen = set()
                for kind, which in ring_tiles(b):
                    if kind != "probsT" and kind not in seen:
                        seen.add(kind)
                        lag = which - b // PER
                        piece(kind, s, lambda b, lag=lag: b // PER + lag, which % 2)

            run_steps(pe, step)

            pe.wait_ge(s_rowtop, 1)
            pe.transpose(B7[0:1, 0:P], row_top, ident[:, :]).then_inc(s_pe, 1)
            pe.wait_ge(s_consts2, 1)
            pe.wait_ge(s_dve, 1)
            pe.matmul(B7[:, DIM:DIM + EXPERTS], all_ones[0:1, :], top_row[0:1, :], start=True, stop=True
                      ).then_inc(s_pe, 1)
            with pe.Fori(0, BISECTIONS) as turn:
                pe.wait_ge(s_count, turn + 1)
                pe.matmul(B6[:, 0:1], same_block, count, start=True, stop=True).then_inc(s_total, 1)
            for i, (block_of, col) in enumerate(((same_block, sure_n), (before_block, limit), (before_block, limit2))):
                pe.wait_ge(s_count, BISECTIONS + i + 1)
                pe.matmul(B6[:, i:i + 1], block_of, col, start=True, stop=True).then_inc(s_total, 1)
            pe.wait_ge(s_count, BISECTIONS + 4)
            pe.matmul(B7[:, DIM:DIM + EXPERTS], all_ones, own_sums, start=True, stop=True).then_inc(s_total, 1)
            pe.wait_ge(s_slots, 1)
            for i in range(2):
                for c, (t0, n) in enumerate(CUTS):
                    pe.transpose(S[0:n, i, c * P:(c + 1) * P], work[1 + i][:, t0:t0 + n], ident[:, :]
                                 ).then_inc(s_slotT, 1)

            def list_tokens(s, ahead):
                pe.wait_ge(s_onehot, s.n(lambda e: e + ahead + 1))
                if s.b + ahead > 0:
                    pe.wait_ge(s_number, s.n(lambda e: e + ahead))
                for c in range(len(CUTS)):
                    for g in range(SEGS):
                        last = pe.matmul(B7[:, DIM:DIM + 2 * TILES], onehot[:, c, g, :],
                                         tagged[:, c, g].rearrange("p a t -> p (a t)"),
                                         start=(c == 0 and g == 0), stop=(c == len(CUTS) - 1 and g == SEGS - 1))
                last.then_inc(s_list, 1)

            def ering_tile(s, i):
                if s.b >= 0 or i - XG_TILES >= 2:
                    pe.wait_ge(s_emoved, s.n(lambda e: ering(e, i - 1)))
                return R[ering(s.b, i) % 2]

            def weights(s):
                par = (s.b + 1) % 2
                pe.wait_ge(s_raw[par], s.n(lambda e: 48 * ((e + 1) // 2 + 1)))
                for i in range(W_TILES):
                    dst = ering_tile(s, XG_TILES + i)
                    for m in range(4):
                        if i < 4:
                            src = (w1_raw if i < 2 else w3_raw)[par][:, m, P * (i % 2):P * (i % 2 + 1)]
                        else:
                            hm = 2 * (i - 4) + m // 2
                            src = w2_raw[par][:, m % 2, P * hm:P * (hm + 1)]
                        last = pe.transpose(dst[:, P * m:P * (m + 1)], src, ident[:, :])
                    last.then_inc(s_ering, 1)

            pe.wait_ge(s_dve, ROUTED)
            list_tokens(Step(0), 0)
            weights(Step(-1))

            def expert(s):
                par = s.b % 2
                pe.wait_ge(s_xg[par], s.n(lambda e: 16 * TILES * (e // 2 + 1)))
                for i in range(XG_TILES):
                    dst = ering_tile(s, i)
                    for c in range(CHUNKS):
                        for t in (2 * i, 2 * i + 1):
                            n = tile_rows(t)
                            at0 = 2 * P * c + P * (t % 2)
                            last = pe.transpose(dst[:, at0:at0 + n], xg[par][0:n, t, P * c:P * (c + 1)],
                                                ident[0:n, 0:n])
                    last.then_inc(s_ering, 1)
                if s.b + 1 < EXPERTS:
                    list_tokens(s, 1)
                for i in range(2 * HM):
                    half, m = divmod(i, HM)
                    t0, t1 = HALVES[half]
                    n = sum(tile_rows(t) for t in range(t0, t1))
                    if m == 0:
                        pe.wait_ge(s_emoved, s.n(lambda e: ering(e, min(XG_TILES, (t1 + 1) // 2))))
                    if i >= 2:
                        pe.wait_ge(s_hT, s.n(lambda e: 2 * HM * e + i - 1))
                    for w, bank in ((w1T, 0), (w3T, 1)):
                        for k in range(CHUNKS):
                            last = pe.matmul(S[:, 2 * (i % 2) + bank, 0:n], w[par][:, k, P * m:P * (m + 1)],
                                             xgT[:, k, P * t0:P * t0 + n], start=(k == 0), stop=(k == CHUNKS - 1))
                    last.then_inc(s_hidden, 1)
                if s.b + 1 < EXPERTS:
                    weights(s)
                for t in range(TILES):
                    n = tile_rows(t)
                    if t in (HALVES[0][0], HALVES[1][0]):
                        pe.wait_ge(s_hT, s.n(lambda e: 2 * HM * e + HM * (1 if t == 0 else 2)))
                    if t >= 2:
                        pe.wait_ge(s_y_sb, s.n(lambda e: TILES * e + t - 1))
                    for m in range(HM):
                        last = pe.matmul((B6, B7)[t % 2][0:n, 0:DIM], hT[:, m, P * t:P * t + n], w2T[par][:, m, :],
                                         start=(m == 0), stop=(m == HM - 1))
                    last.then_inc(s_y, 1)

            run_experts(pe, expert)


_INS = ['x', 'txt', 'L0_tok_W', 'L0_tok_b', 'L0_tok_cls_token', 'L0_attn_Wq', 'L0_attn_Wk', 'L0_attn_Wv',
        'L0_attn_Wo', 'L0_attn_bo', 'L0_ffn_Wg', 'L0_ffn_W1', 'L0_ffn_W2', 'L0_ffn_W3']
_OUTS = [((ITEMS, ROWS, DIM), 'float32')]


def kernel(**inputs):
    import numpy as _np
    import concourse.bacc as _bacc
    from concourse import mybir as _mybir
    from concourse.bass_utils import run_bass_kernel_spmd as _run

    nc = _bacc.Bacc("TRN2", target_bir_lowering=False, num_devices=1)
    arrays, args = {}, []
    for name in _INS:
        a = _np.ascontiguousarray(inputs[name])
        arrays[f"in_{name}_dram"] = a
        args.append(nc.dram_tensor(f"in_{name}_dram", a.shape, _mybir.dt.from_np(a.dtype), kind="ExternalInput").ap())
    for i, (shape, dtype) in enumerate(_OUTS):
        dt = _mybir.dt.from_np(_np.dtype(dtype))
        args.append(nc.dram_tensor(f"out_{i}_dram", shape, dt, kind="ExternalOutput").ap())
    build(nc, *args)
    r = _run(nc, [arrays], core_ids=[0])
    return r.results[0]["out_0_dram"]
```

```python
import concourse.bass as bass
from concourse import mybir
from contextlib import ExitStack

F32 = mybir.dt.float32
BF16 = mybir.dt.bfloat16
F16 = mybir.dt.float16
I32 = mybir.dt.int32
U32 = mybir.dt.uint32
ALU = mybir.AluOpType
ACT = mybir.ActivationFunctionType
AX = mybir.AxisListType

ITEMS, CHANNELS, IMAGE = 64, 3, 64
PATCH = 16
GRID = IMAGE // PATCH
PATCHES = GRID * GRID
PATCH_DIM = CHANNELS * PATCH * PATCH
TEXT = 77
DIM = 256
ROWS = 1 + PATCHES + TEXT
HEADS, HEAD = 16, 16
EXPERTS, HIDDEN = 8, 512
TOKENS = ITEMS * ROWS
CAPACITY = TOKENS // EXPERTS
EPS = 1e-5
P = 128
CHUNKS = DIM // P
PER = 4
GROUPS = ITEMS // PER
SPAN = PER * ROWS
LOOP = 8
MASKED = -1e30
ROW = DIM + EXPERTS
CUTS_IN = 4
ROUNDS, UNROLLED = 16, 4
TILES = -(-CAPACITY // P)
LAST = CAPACITY - (TILES - 1) * P
HALVES = ((0, 3), (3, TILES))
HM = HIDDEN // P
SEGS = P // EXPERTS
CUTS = [(c * P, min(P, SPAN - c * P)) for c in range(-(-SPAN // P))]
OWN_TOP, ROUTED = 3, 3 + 2 + 3 * ROUNDS + 3 + 16
QK_SCALE, V_SCALE, P_SCALE = 32.0, 64.0, 4096.0
PAIRS = HEADS // 2
VCOLS = 2 * HEAD + 1
SIDE = HEADS - 1
TAG = 64


class Step:

    def __init__(self, b, turn=None, stride=LOOP):
        self.b, self.turn, self.stride = b, turn, stride

    def n(self, f):
        v = f(self.b)
        return v if self.turn is None else v + (f(self.b + self.stride) - v) * self.turn


FIRST_STEPS, LAST_STEP = 2 * LOOP, 4 * (GROUPS - 1) + 13
LOOP_TURNS = GROUPS // 2 - 3


def run_steps(eng, step):
    for b in range(FIRST_STEPS):
        step(Step(b))
    with eng.Fori(0, LOOP_TURNS) as turn:
        for b in range(FIRST_STEPS, FIRST_STEPS + LOOP):
            step(Step(b, turn))
    for b in range(FIRST_STEPS + LOOP * LOOP_TURNS, LAST_STEP):
        step(Step(b))


def run_experts(eng, step):
    for e in range(2):
        step(Step(e))
    with eng.Fori(0, EXPERTS // 2 - 2) as turn:
        for e in range(2, 4):
            step(Step(e, turn, stride=2))
    for e in range(EXPERTS - 2, EXPERTS):
        step(Step(e))


SPLIT = ("q", "k", "v")


def pieces(b):
    g, k = divmod(b, PER)
    kinds = ([("gateT", g - 3, 0), ("q", g + 1, 0), ("q", g + 1, 1)],
             [("k", g + 1, 0), ("k", g + 1, 1)],
             [("x2T", g - 2, 0), ("x2T", g - 2, 1), ("v", g + 1, 0)],
             [("v", g + 1, 1), ("gate", g - 2, 0), ("xT", g + 2, 0), ("xT", g + 2, 1)])[k]
    return [t for t in kinds if 0 <= t[1] < GROUPS]


def ring_tiles(b):
    probs = [("probsT", b - 2, r) for r in range(4)] if 0 <= b - 2 < ITEMS else []
    attn = [("attnT", b - 4, 0)] if 0 <= b - 4 < ITEMS else []
    return probs[0:2] + pieces(b) + attn + probs[2:4]


UNITS = 2 * GRID
FIRST_PIECES = [(_kind, _g, _i) for _kind, _g in (("xT", 0), ("q", 0), ("k", 0), ("v", 0), ("xT", 1))
                for _i in range(2)]
RING_AT = {}
SPLIT_AT = {}

EARLY_UNITS = 6


def unit_tile(u, i):
    return 2 * u + i + (len(FIRST_PIECES) if u >= EARLY_UNITS else 0)


_n, _m = 2 * EARLY_UNITS, 0
for _t in FIRST_PIECES + [_t for _b in range(LAST_STEP) for _t in ring_tiles(_b)]:
    RING_AT[_t] = _n
    _n += 1
    if _t == FIRST_PIECES[-1]:
        _n += 2 * (UNITS - EARLY_UNITS)
    if _t[0] in SPLIT:
        SPLIT_AT[_t] = _m
        _m += 1


def build(nc, x, txt, tok_W, tok_b, cls_token, Wq, Wk, Wv, Wo, bo, Wg, W1, W2, W3, out):
    out_rows = out.rearrange("b s c -> (b s) c")
    patch_rows = nc.dram_tensor("patch_rows", [ITEMS, PATCHES, DIM], F32).ap()
    stored = nc.dram_tensor("stored", [TOKENS, ROW], F32).ap()
    gate_rows = nc.dram_tensor("gate_rows", [EXPERTS, TOKENS], F32).ap()
    q_rows = nc.dram_tensor("q_rows", [2, DIM, SPAN], F16).ap()
    k_rows = nc.dram_tensor("k_rows", [2, DIM, SPAN], F16).ap()

    ctx = ExitStack()
    with ctx:
        def sb(name, shape, dt=F32):
            return ctx.enter_context(nc.sbuf_tensor(name, shape, dt))

        def sem(name):
            return ctx.enter_context(nc.semaphore(name))

        ident = sb("ident", [P, P])
        ident_b = sb("ident_b", [P, P], BF16)
        iota_f = sb("iota_f", [P, P])

        ARENA = 48000
        arena = sb("arena", [P, ARENA])

        class Carve:
            def __init__(self):
                self.at = 0

            def __call__(self, *shape, dt=F32, parts=P):
                n = 1
                for s in shape:
                    n *= s
                words = n if dt in (F32, I32, U32) else (n + 1) // 2
                ap = arena[0:parts, self.at:self.at + words]
                self.at += (words + 7) // 8 * 8
                assert self.at <= ARENA, self.at
                if dt != F32:
                    ap = ap.bitcast(dt)[:, 0:n]
                if len(shape) > 1:
                    names = "abcde"[:len(shape)]
                    ap = ap.rearrange(f"p ({' '.join(names)}) -> p {' '.join(names)}",
                                      **dict(zip(names[1:], shape[1:])))
                return ap

        at = Carve()
        h = at(ITEMS, DIM, parts=ROWS)
        wq, wk, wv, wo = (at(CHUNKS, DIM) for _ in range(4))
        wgT = at(CHUNKS, EXPERTS)
        wg_rows = at(DIM, parts=EXPERTS)
        bo_rep = at(DIM, parts=ROWS)
        mask = at(4, ROWS, dt=BF16, parts=ROWS)
        minus_half = at(PER, parts=ROWS)
        v = [at(PER, HEADS, VCOLS, dt=F16, parts=ROWS) for _ in range(2)]
        K2_WORDS = PAIRS * 2 * SPAN // 2
        k2_words = [at(K2_WORDS) for _ in range(2)]
        K2 = [w.bitcast(F16).rearrange("p (a o t) -> p a o t", o=2, t=SPAN) for w in k2_words]
        working = at.at
        Q2 = [at(PAIRS, SPAN, dt=F16) for _ in range(2)]
        q_parts, k_parts = ([at(CHUNKS, SPAN, dt=F16) for _ in range(2)] for _ in range(2))
        staged = [at(512) for _ in range(2)]
        xn = at(PER, DIM, parts=ROWS)
        xT = at(CHUNKS, SPAN)
        prob = [at(4, 4, ROWS, parts=ROWS) for _ in range(4)]
        probT = [at(4, 4, ROWS, dt=F16, parts=ROWS) for _ in range(2)]
        unnormed = at(HEADS, VCOLS, parts=ROWS)
        summed = at(HEADS, HEAD, parts=ROWS)
        attn = at(DIM, parts=ROWS)
        attn_nT = at(CHUNKS, ROWS)
        xn2 = [at(PER, ROW, parts=ROWS) for _ in range(2)]
        x2T = at(CHUNKS, SPAN)
        gate_sb = [at(SPAN, parts=EXPERTS) for _ in range(2)]
        top = at(4, 4, parts=ROWS)
        recip = at(HEADS, parts=ROWS)
        stats = [at(PER, 6, parts=ROWS) for _ in range(2)]
        mean_var = [at(PER, 2, parts=ROWS) for _ in range(2)]
        spread = [at(PER, parts=ROWS) for _ in range(2)]
        rstd = [at(PER, parts=ROWS) for _ in range(2)]
        minus_mean = [at(PER, parts=ROWS) for _ in range(2)]
        shift = [at(PER, parts=ROWS) for _ in range(2)]
        pt = Carve()
        pt.at = working
        images = [pt(CHANNELS, PATCH * IMAGE) for _ in range(2)]
        columns = [pt(CHANNELS, GRID, PATCH * PATCH) for _ in range(2)]
        tokw = pt(PATCH_DIM // P, DIM)
        tokb = pt(DIM)
        patchT = [pt(PATCH_DIM // P, P) for _ in range(2)]
        patch_sb = [pt(DIM) for _ in range(2)]

        rt = Carve()
        sc = rt(SPAN)
        work = [rt(SPAN) for _ in range(5)]
        ints = [rt(SPAN, dt=I32) for _ in range(3)]
        low, high, highest, count, passed = (rt(1) for _ in range(5))
        quarters, step_of, multiples = rt(ROUNDS), rt(ROUNDS), rt(CUTS_IN - 1)
        tried, reached, offered = (rt(ROUNDS, CUTS_IN - 1) for _ in range(3))
        counts = rt(CUTS_IN - 1)
        row_top, abs_top, bound, own_top, row_sum, need, limit, sure_n, limit2 = (rt(1) for _ in range(9))
        top_row = rt(EXPERTS)
        own_sums = rt(EXPERTS)
        same_block = rt(P)
        before_block = rt(P)
        all_ones = rt(P)
        own = rt(EXPERTS)
        top_all = rt(EXPERTS)
        recip_all = rt(EXPERTS)
        slotT = [rt(len(CUTS), EXPERTS, SEGS) for _ in range(2)]
        tag = [rt(len(CUTS), SEGS) for _ in range(2)]
        tag_i = rt(3, len(CUTS), SEGS, dt=I32)
        onehot = rt(len(CUTS), SEGS, P, dt=BF16)
        match = rt(len(CUTS), SEGS, TILES)
        tagged = rt(len(CUTS), SEGS, 2, TILES, dt=BF16)
        number = rt(2, TILES)
        index = [rt(TILES, dt=U32) for _ in range(2)]
        xg = [rt(TILES, ROW) for _ in range(2)]
        xgT = rt(CHUNKS, CAPACITY)
        w1_raw, w3_raw = ([rt(HM, DIM) for _ in range(2)] for _ in range(2))
        w2_raw = [rt(CHUNKS, HIDDEN) for _ in range(2)]
        w1T, w3T = ([rt(CHUNKS, HIDDEN) for _ in range(2)] for _ in range(2))
        w2T = [rt(HM, DIM) for _ in range(2)]
        gated = [rt(3 * P) for _ in range(2)]
        hT = rt(HM, CAPACITY)
        token_w = [rt(TILES) for _ in range(2)]
        y = [rt(TILES, DIM) for _ in range(2)]

        S = ctx.enter_context(nc.psum_tensor("S", [P, 4, 512], F32))
        R = [ctx.enter_context(nc.psum_tensor(f"R{i}", [P, 512], F32)) for i in range(2)]
        B6 = ctx.enter_context(nc.psum_tensor("B6", [P, 512], F32))
        B7 = ctx.enter_context(nc.psum_tensor("B7", [P, 512], F32))

        s_weights, s_patchw = sem("s_weights"), sem("s_patchw")
        s_text = [sem(f"s_text{i}") for i in range(2)]
        s_rows_in = [sem(f"s_rows_in{i}") for i in range(2)]
        s_images = [sem(f"s_images{i}") for i in range(2)]
        s_columns = sem("s_columns")
        s_build, s_const = sem("s_build"), sem("s_const")
        s_patch, s_patch_sb = sem("s_patch"), sem("s_patch_sb")
        s_patch_out = [sem(f"s_patch_out{i}") for i in range(2)]
        s_wgT, s_wgT_sb = sem("s_wgT"), sem("s_wgT_sb")
        s_ring = sem("s_ring")
        s_free = [sem(f"s_free{i}") for i in range(2)]
        s_high = sem("s_high")
        s_parted = sem("s_parted")
        s_split = sem("s_split")
        s_q_out, s_q_in, s_k_out, s_k_in = map(sem, ("s_q_out", "s_q_in", "s_k_out", "s_k_in"))
        s_scores, s_max, s_sub, s_exp = map(sem, ("s_scores", "s_max", "s_sub", "s_exp"))
        s_pv, s_unnormed, s_recip, s_summed, s_norm, s_proj, s_res = map(
            sem, ("s_pv", "s_unnormed", "s_recip", "s_summed", "s_norm", "s_proj", "s_res"))
        s_stats = [sem(f"s_stats{i}") for i in range(2)]
        s_aggr = [sem(f"s_aggr{i}") for i in range(2)]
        s_var = [sem(f"s_var{i}") for i in range(2)]
        s_pow = [sem(f"s_pow{i}") for i in range(2)]
        s_rstd = [sem(f"s_rstd{i}") for i in range(2)]
        s_normed = [sem(f"s_normed{i}") for i in range(2)]
        s_bias, s_h_out = sem("s_bias"), sem("s_h_out")
        s_stored = [sem(f"s_stored{i}") for i in range(2)]
        s_gate_out = [sem(f"s_gate_out{i}") for i in range(2)]
        s_sc, s_consts2, s_build2 = map(sem, ("s_sc", "s_consts2", "s_build2"))
        s_dve, s_rowtop, s_abs, s_pe, s_count, s_total, s_expd = map(
            sem, ("s_dve", "s_rowtop", "s_abs", "s_pe", "s_count", "s_total", "s_expd"))
        s_slots, s_slotT, s_slotT_sb = map(sem, ("s_slots", "s_slotT", "s_slotT_sb"))
        s_match, s_onehot, s_list, s_number, s_index = map(
            sem, ("s_match", "s_onehot", "s_list", "s_number", "s_index"))
        s_raw = [sem(f"s_raw{i}") for i in range(2)]
        s_xg = [sem(f"s_xg{i}") for i in range(2)]
        s_ering, s_emoved = sem("s_ering"), sem("s_emoved")
        s_hidden, s_silu, s_hT = map(sem, ("s_hidden", "s_silu", "s_hT"))
        s_wexp, s_tokw, s_y, s_y_sb = map(sem, ("s_wexp", "s_tokw", "s_y", "s_y_sb"))
        s_added = [sem(f"s_added{i}") for i in range(2)]

        block = ctx.enter_context(nc.Block())

        XG_TILES, W_TILES = TILES // 2, 6
        EXPERT_TILES = XG_TILES + W_TILES

        def ring_tile(kind, which, i=0):
            n = RING_AT[(kind, which, i)]
            return n % 2, n // 2 + 1

        def wait_moved(eng, kind, s, which, i=0):
            eng.wait_ge(s_free[ring_tile(kind, which(s.b), i)[0]],
                        s.n(lambda b: ring_tile(kind, which(b), i)[1]))

        def filled(kind, which, i=0):
            return RING_AT[(kind, which, i)] + 1

        def ering(e, i):
            return W_TILES + e * EXPERT_TILES + i

        def in_register(eng, n):
            counts = [k if isinstance(k, int) else eng.to_reg(k) for k in n]
            eng.wait_ge(s_const, 1)
            return counts

        def tile_rows(t):
            return P if t < TILES - 1 else LAST

        @block.sync
        def _(sp):
            xv = x.rearrange("b c (g i) w -> b g c (i w)", g=GRID)
            n = ITEMS // 8

            def load_images(t):
                for c in range(CHANNELS):
                    sp.dma_start(images[t][:, c, :], xv[32 * t:32 * (t + 1), :, c, :]).then_inc(s_images[t], 16)

            def load_text(q):
                sp.dma_start(h[1 + PATCHES:ROWS, n * q:n * (q + 1), :],
                             txt[n * q:n * (q + 1)].rearrange("b s c -> s b c")).then_inc(s_text[q // 4], 16)

            load_images(0)
            sp.dma_start(tokw, tok_W.rearrange("(k p) e -> p k e", p=P)).then_inc(s_patchw, 16)
            sp.dma_start(tokb, tok_b.rearrange("(a e) -> a e", a=1).to_broadcast([P, DIM])).then_inc(s_patchw, 16)
            sp.dma_start(h[0:1, :, :], cls_token.to_broadcast([1, ITEMS, DIM])).then_inc(s_text[0], 16)
            load_images(1)
            load_text(0)
            for w, dram in ((wq, Wq), (wk, Wk), (wv, Wv), (wo, Wo)):
                sp.dma_start(w, dram.rearrange("(k p) e -> p k e", p=P)).then_inc(s_weights, 16)
            sp.dma_start(wg_rows, Wg).then_inc(s_weights, 16)
            sp.dma_start(bo_rep, bo.rearrange("(a e) -> a e", a=1).to_broadcast([ROWS, DIM])
                         ).then_inc(s_weights, 16)
            by_row = patch_rows.rearrange("b (i j) e -> (b i) j e", i=GRID)

            def store_patches(u):
                t, j = divmod(u, GRID)
                sp.wait_ge(s_patch_sb, u + 1)
                sp.dma_start(by_row[P * t:P * (t + 1), j, :], patch_sb[u % 2]).then_inc(s_patch_out[u % 2], 16)

            def reload_patches(t):
                for i in range(2):
                    sp.wait_ge(s_patch_out[i], 16 * (t + 1) * GRID // 2)
                half = slice(ITEMS // 2 * t, ITEMS // 2 * (t + 1))
                sp.dma_start(h[1:1 + PATCHES, half, :], patch_rows[half].rearrange("b n e -> n b e")
                             ).then_inc(s_rows_in[t], 16)

            for u in range(UNITS // 2):
                store_patches(u)
                if 1 + u < 4:
                    load_text(1 + u)
            reload_patches(0)
            for u in range(UNITS // 2, EARLY_UNITS):
                store_patches(u)
            for q in range(4, 8):
                load_text(q)

            def restack(kind, s, which, gpar, first=False):
                parts, rows = (q_parts, q_rows) if kind == "q" else (k_parts, k_rows)
                s_out, s_in, reads = (s_q_out, s_q_in, 4) if kind == "q" else (s_k_out, s_k_in, 8)
                split, read, written, scored = in_register(sp, [
                    s.n(lambda b: SPLIT_AT[(kind, which(b), 1)] + 1), s.n(lambda b: 16 * reads * which(b)),
                    s.n(lambda b: 32 * (which(b) + 1)), s.n(lambda b: 4 * PER * (which(b) - 1))])
                sp.wait_ge(s_split, split)
                if which(s.b) > 0:
                    sp.wait_ge(s_in, read)
                for i in range(2):
                    sp.dma_start(rows[i].rearrange("(c p) t -> p c t", p=P), parts[i]).then_inc(s_out, 16)
                sp.wait_ge(s_const, 1)
                sp.wait_ge(s_out, written)
                if which(s.b) >= 2:
                    sp.wait_ge(s_scores, scored)
                for mine in range(2):
                    for other in range(2):
                        if kind == "q":
                            p0 = 64 * other + 32 * mine
                            sp.dma_start(Q2[gpar][p0:p0 + 32],
                                         rows[mine].rearrange("(a p) t -> p a t", p=32)).then_inc(s_in, 16)
                        else:
                            for o in range(2):
                                p0 = 64 * mine + 32 * other + 16 * o
                                sp.dma_start(K2[gpar][p0:p0 + 16, :, o, :],
                                             rows[mine].rearrange("(a o p) t -> o p a t", o=2, p=16)[o]
                                             ).then_inc(s_in, 16)

            sp.wait_ge(s_const, 1)
            for kind, which, i in FIRST_PIECES:
                if kind in ("q", "k") and i == 1:
                    restack(kind, Step(0), lambda b: which, which % 2)
            for u in range(EARLY_UNITS, UNITS):
                store_patches(u)
            reload_patches(1)

            def step(s):
                b = s.b
                g, k = divmod(b, PER)
                if k == 0 and g + 1 < GROUPS:
                    restack("q", s, lambda b: b // PER + 1, (g + 1) % 2)
                if k == 0 and 0 <= g - 2 < GROUPS:
                    rows = bass.ds(s.n(lambda b: b - 2 * PER), PER)
                    sp.wait_ge(s_res, s.n(lambda b: b - 4))
                    sp.dma_start(out.rearrange("b s c -> s b c")[:, rows, :], h[:, rows, :]).then_inc(s_h_out, 16)
                if k == 0 and 0 <= g - 3 < GROUPS:
                    par = (g - 3) % 2
                    wait_moved(sp, "gateT", s, lambda b: b // PER - 3)
                    sp.dma_start(stored.rearrange("(b s) c -> s b c", s=ROWS)[
                        :, bass.ds(s.n(lambda b: b - 3 * PER), PER), :], xn2[par]).then_inc(s_stored[par], 16)
                if k == 1 and g + 1 < GROUPS:
                    restack("k", s, lambda b: b // PER + 1, (g + 1) % 2)
                if k == 3 and 0 <= g - 2 < GROUPS:
                    par = g % 2
                    wait_moved(sp, "gate", s, lambda b: b // PER - 2)
                    sp.dma_start(gate_rows[:, bass.ds(s.n(lambda b: (b // PER - 2) * SPAN), SPAN)], gate_sb[par]
                                 ).then_inc(s_gate_out[par], 16)

            run_steps(sp, step)

            for i in range(2):
                sp.wait_ge(s_gate_out[i], 16 * GROUPS // 2)
                sp.wait_ge(s_stored[i], 16 * GROUPS // 2)
            sp.wait_ge(s_h_out, 16 * GROUPS)
            sp.dma_start(sc, gate_rows.rearrange("e (g t) -> (e g) t", g=SEGS)).then_inc(s_sc, 16)

            def load_expert(s):
                par = s.b % 2
                if s.b >= 0:
                    sp.wait_ge(s_ering, s.n(lambda e: ering(e - 1, XG_TILES + W_TILES)))
                e = s.n(lambda e: e + 2)
                sp.dma_start(w1_raw[par], W1.rearrange("e (m p) c -> p e m c", p=P)[:, e]).then_inc(s_raw[par], 16)
                sp.dma_start(w3_raw[par], W3.rearrange("e (m p) c -> p e m c", p=P)[:, e]).then_inc(s_raw[par], 16)
                sp.dma_start(w2_raw[par], W2.rearrange("e (m p) c -> p e m c", p=P)[:, e]).then_inc(s_raw[par], 16)

            load_expert(Step(-2))
            load_expert(Step(-1))
            with sp.Fori(0, EXPERTS // 2 - 1) as turn:
                for e in range(2):
                    load_expert(Step(e, turn, stride=2))
            for i in range(2):
                sp.wait_ge(s_added[i], 16 * TILES * EXPERTS // 2)

        @block.gpsimd
        def _(pool):
            pool.memset(ident[:, :], 0.0)
            pool.memset(mask, 0.0)
            pool.memset(minus_half, -0.5)
            for i in range(2):
                pool.memset(k2_words[i], 0.0)
            pool.iota(iota_f[:, :], pattern=[[1, P]], base=0, channel_multiplier=0,
                      allow_small_or_imprecise_dtypes=True).then_inc(s_build, 1)
            pool.wait_ge(s_build, 1)
            pool.affine_select(out=ident[:, :], in_=ident[:, :], compare_op=ALU.not_equal, fill=1.0, base=0,
                               pattern=[[-1, P]], channel_multiplier=1)
            pool.affine_select(out=mask, in_=mask, compare_op=ALU.is_ge, fill=MASKED, base=0,
                               pattern=[[0, 4], [-1, ROWS]], channel_multiplier=1)
            for i in range(2):
                last = pool.memset(v[i].rearrange("p a b c -> p (a b) c")[:, :, VCOLS - 1:VCOLS], V_SCALE)
            last.then_inc(s_build, 1)
            pool.wait_ge(s_build, 2)
            pool.tensor_copy(ident_b[:, :], ident[:, :]).then_inc(s_const, 1)

            def power(norm, count):
                pool.wait_ge(s_var[norm], count)
                pool.tensor_tensor(rstd[norm], spread[norm], minus_half, ALU.pow).then_inc(s_pow[norm], 1)
                pool.wait_ge(s_pow[norm], count)
                pool.tensor_tensor(shift[norm], minus_mean[norm], rstd[norm], ALU.mult).then_inc(s_rstd[norm], 1)

            def add_bias(g, count):
                pool.wait_ge(s_normed[0], count)
                rows = h[:, bass.ds(g * PER, PER), :]
                pool.tensor_tensor(rows, rows, bo_rep.unsqueeze(1).to_broadcast([ROWS, PER, DIM]), ALU.add
                                   ).then_inc(s_bias, 1)

            def piece(kind, s, which, gpar, i):
                if kind not in SPLIT:
                    return
                n = SPLIT_AT[(kind, which(s.b), i)]
                pool.wait_ge(s_parted, s.n(lambda b: SPLIT_AT[(kind, which(b), i)] + 1))
                if kind == "v":
                    items = v[gpar][:, 2 * i:2 * i + 2]
                    high, low = items[:, :, :, 0:HEAD], items[:, :, :, HEAD:2 * HEAD]
                    whole = staged[n % 2][0:ROWS].rearrange("p (i h d) -> p i h d", i=2, d=HEAD)
                else:
                    high, low = ((q_parts if kind == "q" else k_parts)[j][:, i, :] for j in range(2))
                    whole = staged[n % 2][:, 0:SPAN]
                pool.tensor_tensor(low, whole, high, ALU.subtract).then_inc(s_split, 1)

            def group_pieces(s):
                for kind, which, i in pieces(s.b):
                    piece(kind, s, lambda b, lag=which - s.b // PER: b // PER + lag, which % 2, i)

            pool.wait_ge(s_weights, 16 * 6)
            for g in range(2):
                power(0, g + 1)
            for g in range(2):
                for kind, which, i in FIRST_PIECES:
                    if which == g:
                        piece(kind, Step(0), lambda b: which, which % 2, i)
                add_bias(g, g + 1)

            def step(s):
                b = s.b
                g, k = divmod(b, PER)
                if k == 1 and 0 <= g - 2 < GROUPS:
                    power(1, s.n(lambda b: b // PER - 1))
                if k == 2 and g + 2 < GROUPS:
                    power(0, s.n(lambda b: b // PER + 3))
                group_pieces(s)
                if 0 <= b - 3 < ITEMS:
                    pool.wait_ge(s_unnormed, s.n(lambda b: b - 2))
                    pool.tensor_tensor(summed, unnormed[:, :, 0:HEAD], unnormed[:, :, HEAD:2 * HEAD], ALU.add
                                       ).then_inc(s_summed, 1)
                    pool.wait_ge(s_summed, s.n(lambda b: b - 2))
                    pool.wait_ge(s_recip, s.n(lambda b: b - 2))
                    if b - 3 > 0:
                        pool.wait_ge(s_ring, s.n(lambda b: filled("attnT", b - 4)))
                    pool.tensor_tensor(attn.rearrange("p (h d) -> p h d", d=HEAD), summed,
                                       recip.unsqueeze(2).to_broadcast([ROWS, HEADS, HEAD]), ALU.mult
                                       ).then_inc(s_norm, 1)
                if k == 3 and g + 2 < GROUPS:
                    add_bias(s.n(lambda b: b // PER + 2), s.n(lambda b: b // PER + 3))

            run_steps(pool, step)

            pool.wait_ge(s_sc, 16)
            pool.memset(all_ones, 1.0)
            for n in range(ROUNDS):
                pool.memset(quarters[:, n:n + 1], 2.0 * CUTS_IN ** -(n + 1))
            for i in range(1, CUTS_IN):
                pool.memset(multiples[:, i - 1:i], float(i))
            pool.memset(own, 1.0)
            pool.memset(work[3], 0.0)
            for i in range(2):
                pool.memset(slotT[i], -1.0)
                pool.memset(xg[i][:, TILES - 1, :], 0.0)
            pool.iota(tag_i[:, 0], pattern=[[P, len(CUTS)], [SPAN, SEGS]], base=0, channel_multiplier=1
                      ).then_inc(s_build2, 1)
            pool.wait_ge(s_build2, 1)
            pool.affine_select(out=own, in_=own, compare_op=ALU.is_ge, fill=0.0, base=0,
                               pattern=[[-SEGS, EXPERTS]], channel_multiplier=1).then_inc(s_build2, 1)
            pool.wait_ge(s_build2, 2)
            pool.affine_select(out=own, in_=own, compare_op=ALU.is_ge, fill=0.0, base=SEGS - 1,
                               pattern=[[SEGS, EXPERTS]], channel_multiplier=-1).then_inc(s_build2, 1)
            pool.wait_ge(s_build2, 3)
            pool.tensor_copy(same_block.rearrange("p (e s) -> p e s", s=SEGS),
                             own.unsqueeze(2).to_broadcast([P, EXPERTS, SEGS])).then_inc(s_build2, 1)
            pool.wait_ge(s_build2, 4)
            pool.affine_select(out=before_block, in_=same_block, compare_op=ALU.is_gt, fill=0.0, base=0,
                               pattern=[[1, P]], channel_multiplier=-1).then_inc(s_consts2, 1)
            pool.wait_ge(s_rowtop, 2)
            pool.partition_all_reduce(bound, abs_top, P, bass.bass_isa.ReduceOp.max).then_inc(s_abs, 1)

            def gather(s, ahead):
                par = (s.b + ahead) % 2
                chosen, used = in_register(pool, [s.n(lambda e: e + ahead + 1),
                                                  s.n(lambda e: TILES * max(e + ahead - 1, 0))])
                pool.wait_ge(s_index, chosen)
                pool.wait_ge(s_y_sb, used)
                for t in range(TILES):
                    n = tile_rows(t)
                    pool.indirect_dma_start(
                        out=xg[par][0:n, t, :], out_offset=None, in_=stored,
                        in_offset=bass.IndirectOffsetOnAxis(ap=index[par][0:n, t:t + 1], axis=0),
                    ).then_inc(s_xg[par], 16)

            def scatter(s):
                par = s.b % 2
                weighted, landed = in_register(pool, [s.n(lambda e: TILES * (e + 1)),
                                                      s.n(lambda e: 16 * TILES * ((e + 1) // 2))])
                pool.wait_ge(s_y_sb, weighted)
                pool.wait_ge(s_added[1 - par], landed)
                for t in range(TILES):
                    n = tile_rows(t)
                    pool.indirect_dma_start(
                        out=out_rows, out_offset=bass.IndirectOffsetOnAxis(ap=index[par][0:n, t:t + 1], axis=0),
                        in_=y[par][0:n, t, :], in_offset=None, compute_op=ALU.add,
                    ).then_inc(s_added[par], 16)

            def expert(s):
                if s.b + 1 < EXPERTS:
                    gather(s, 1)
                scatter(s)

            gather(Step(0), 0)
            gather(Step(0), 1)
            scatter(Step(0))
            with pool.Fori(0, EXPERTS // 2 - 1) as turn:
                for e in range(1, 3):
                    expert(Step(e, turn, stride=2))
            expert(Step(EXPERTS - 1))

        @block.scalar
        def _(act):
            def move(dst, src, bank):
                act.activation(dst, src, ACT.Copy).then_inc(s_free[bank], 1)

            def split(kind, s, which, i, high, whole, src, scale):
                act.activation(whole, src, ACT.Copy, scale=scale).then_inc(s_free[ring_tile(kind, which(s.b), i)[0]], 1)
                wait_moved(act, kind, s, which, i)
                act.activation(high, whole, ACT.Copy).then_inc(s_parted, 1)

            def move_patches(u):
                if u >= 2:
                    act.wait_ge(s_patch, u - 1)
                act.wait_ge(s_ring, unit_tile(u, 0) + 1)
                move(patchT[u % 2][:, 0:4, :], R[0][:, :].rearrange("p (k n) -> p k n", k=4), 0)
                act.wait_ge(s_ring, unit_tile(u, 1) + 1)
                move(patchT[u % 2][:, 4:6, :], R[1][:, 0:2 * P].rearrange("p (k n) -> p k n", k=2), 1)

            for u in range(EARLY_UNITS):
                move_patches(u)
            act.wait_ge(s_const, 1)

            def piece(kind, s, which, gpar, i):
                bank = ring_tile(kind, which(s.b), i)[0]
                if kind in ("q", "k") and i == 0 and which(s.b) > 0:
                    act.wait_ge(s_q_out if kind == "q" else s_k_out, s.n(lambda b: 32 * which(b)))
                if kind == "v" and i == 0 and which(s.b) >= 2:
                    act.wait_ge(s_pv, s.n(lambda b: 4 * PER * (which(b) - 1)))
                if kind == "gate" and which(s.b) >= 2:
                    act.wait_ge(s_gate_out[gpar], s.n(lambda b: 16 * (which(b) // 2)))
                act.wait_ge(s_ring, s.n(lambda b: filled(kind, which(b), i)))
                if kind == "xT":
                    move(xT[:, i, :], R[bank][:, 0:SPAN], bank)
                if kind in SPLIT:
                    n = SPLIT_AT[(kind, which(s.b), i)]
                    if n >= 2:
                        act.wait_ge(s_split, s.n(lambda b: SPLIT_AT[(kind, which(b), i)] - 1))
                if kind in ("q", "k"):
                    split(kind, s, which, i, (q_parts if kind == "q" else k_parts)[0][:, i, :],
                          staged[n % 2][:, 0:SPAN], R[bank][:, 0:SPAN], QK_SCALE)
                if kind == "v":
                    split(kind, s, which, i, v[gpar][:, 2 * i:2 * i + 2, :, 0:HEAD],
                          staged[n % 2][0:ROWS].rearrange("p (i h d) -> p i h d", i=2, d=HEAD),
                          R[bank][0:ROWS, :].rearrange("p (i h d) -> p i h d", i=2, d=HEAD), V_SCALE)
                if kind == "x2T":
                    move(x2T[:, i, :], R[bank][:, 0:SPAN], bank)
                if kind == "gate":
                    move(gate_sb[gpar], R[bank][0:EXPERTS, 0:SPAN], bank)
                if kind == "gateT":
                    move(xn2[gpar][:, :, DIM:ROW],
                         R[bank][0:ROWS, 0:PER * EXPERTS].rearrange("p (i e) -> p i e", i=PER), bank)

            def norm_row(norm, g, dst, count, i):
                if i == 0:
                    act.wait_ge(s_rstd[norm], count)
                ins = act.activation(dst[:, i, 0:DIM], h[:, g * PER + i, :], ACT.Identity,
                                     bias=shift[norm][:, i:i + 1], scale=rstd[norm][:, i:i + 1])
                if i == PER - 1:
                    ins.then_inc(s_normed[norm], 1)

            act.wait_ge(s_text[0], 16 * 5)
            act.wait_ge(s_rows_in[0], 16)
            for kind, which, i in FIRST_PIECES:
                if kind == "xT" and i == 0:
                    if which > 0:
                        act.wait_ge(s_ring, filled("xT", 0, 1))
                    for j in range(PER):
                        norm_row(0, which, xn, which + 1, j)
                piece(kind, Step(0), lambda b: which, which % 2, i)
            for u in range(EARLY_UNITS, UNITS):
                move_patches(u)

            def group_pieces(s):
                for kind, which, i in pieces(s.b):
                    piece(kind, s, lambda b, lag=which - s.b // PER: b // PER + lag, which % 2, i)

            def step(s):
                b = s.b

                def turned(r):
                    if 0 <= b - 2 < ITEMS:
                        if b - 2 > 0:
                            act.wait_ge(s_pv, s.n(lambda b: 4 * (b - 3) + r + 1))
                        act.wait_ge(s_ring, s.n(lambda b: filled("probsT", b - 2, r)))
                        act.activation(probT[0][:, r], R[ring_tile("probsT", b - 2, r)[0]][0:ROWS, 0:SPAN]
                                       .rearrange("p (j t) -> p j t", j=4), ACT.Copy, scale=P_SCALE
                                       ).then_inc(s_high, 1)

                def row(i):
                    g, k = divmod(b, PER)
                    if k == 1 and 0 <= g - 2 < GROUPS:
                        if i == 0 and g - 2 >= 2:
                            act.wait_ge(s_stored[g % 2], s.n(lambda b: 16 * ((b // PER - 2) // 2)))
                        norm_row(1, s.n(lambda b: b // PER - 2), xn2[g % 2], s.n(lambda b: b // PER - 1), i)
                    if k == 2 and g + 2 < GROUPS:
                        if i == 0:
                            act.wait_ge(s_ring, s.n(lambda b: filled("xT", b // PER + 1, 1)))
                        norm_row(0, s.n(lambda b: b // PER + 2), xn, s.n(lambda b: b // PER + 3), i)

                turned(0)
                turned(1)
                if 0 <= b - 1 < ITEMS:
                    act.wait_ge(s_sub, s.n(lambda b: 4 * b))
                    act.activation(prob[(b - 1) % 4], prob[(b - 1) % 4], ACT.Exp,
                                   scale=HEAD ** -0.5 / QK_SCALE ** 2).then_inc(s_exp, 1)
                if 0 <= b - 3 < ITEMS:
                    act.wait_ge(s_pv, s.n(lambda b: 4 * (b - 2)))
                    if b - 3 > 0:
                        act.wait_ge(s_norm, s.n(lambda b: b - 3))
                    act.activation(unnormed[:, 0:SIDE, :], B6[0:ROWS, 0:SIDE * VCOLS]
                                   .rearrange("p (h d) -> p h d", d=VCOLS), ACT.Copy)
                    act.activation(unnormed[:, SIDE, :], B7[0:ROWS, 0:VCOLS], ACT.Copy).then_inc(s_unnormed, 1)
                group_pieces(s)
                if 0 <= b - 4 < ITEMS:
                    if b - 4 > 0:
                        act.wait_ge(s_proj, s.n(lambda b: b - 4))
                    act.wait_ge(s_ring, s.n(lambda b: filled("attnT", b - 4)))
                    bank = ring_tile("attnT", b - 4)[0]
                    move(attn_nT, R[bank][:, 0:2 * ROWS].rearrange("p (c t) -> p c t", c=2), bank)
                turned(2)
                turned(3)
                for i in range(PER):
                    row(i)

            run_steps(act, step)

            act.wait_ge(s_dve, OWN_TOP)
            act.activation(work[0], sc, ACT.Exp, bias=own_top).then_inc(s_expd, 1)

            def emove(i, dst, src):
                act.activation(dst, src, ACT.Copy).then_inc(s_emoved, 1)

            def weights(s, first):
                par = (s.b + 1) % 2
                for i in range(W_TILES):
                    act.wait_ge(s_ering, s.n(lambda e: ering(e, XG_TILES + i + 1)))
                    src = R[ering(s.b, XG_TILES + i) % 2]
                    if i < 4:
                        dst = (w1T if i < 2 else w3T)[par][:, i % 2, :]
                        emove(i, dst, src[:, :])
                    else:
                        emove(i, w2T[par][:, 2 * (i - 4):2 * (i - 4) + 2, :],
                              src[:, :].rearrange("p (m c) -> p m c", m=2))

            weights(Step(-1), None)

            def expert(s):
                par = s.b % 2
                e = s.n(lambda e: e)
                for i in range(XG_TILES):
                    act.wait_ge(s_ering, s.n(lambda e: ering(e, i + 1)))
                    w = tile_rows(2 * i + 1) + P
                    emove(i, xgT[:, :, 2 * P * i:2 * P * i + w],
                          R[ering(s.b, i) % 2][:, :].rearrange("p (c t) -> p c t", c=2)[:, :, 0:w])
                act.wait_ge(s_xg[par], s.n(lambda e: 16 * TILES * (e // 2 + 1)))
                act.activation(token_w[par], xg[par][:, :, bass.ds(e + DIM, 1)].rearrange("p t a -> p (t a)"),
                               ACT.Exp, bias=top_all[:, bass.ds(e, 1)]).then_inc(s_wexp, 1)
                for i in range(2 * HM):
                    t0, t1 = HALVES[i // HM]
                    n = sum(tile_rows(t) for t in range(t0, t1))
                    act.wait_ge(s_hidden, s.n(lambda e: 2 * HM * e + i + 1))
                    if i >= 2:
                        act.wait_ge(s_hT, s.n(lambda e: 2 * HM * e + i - 1))
                    act.activation(gated[i % 2][:, 0:n], S[:, 2 * (i % 2), 0:n], ACT.Silu).then_inc(s_silu, 1)
                if s.b + 1 < EXPERTS:
                    weights(s, None)
                act.wait_ge(s_tokw, s.n(lambda e: e + 1))
                if s.b >= 2:
                    act.wait_ge(s_added[par], s.n(lambda e: 16 * TILES * (e // 2)))
                for t in range(TILES):
                    n = tile_rows(t)
                    act.wait_ge(s_y, s.n(lambda e: TILES * e + t + 1))
                    act.activation(y[par][0:n, t, :], (B6, B7)[t % 2][0:n, 0:DIM], ACT.Identity,
                                   scale=token_w[par][0:n, t:t + 1]).then_inc(s_y_sb, 1)

            run_experts(act, expert)

        @block.vector
        def _(dve):
            def gather_columns(t):
                dve.wait_ge(s_images[t], 16 * CHANNELS)
                for c in range(CHANNELS):
                    last = dve.tensor_copy(
                        columns[t][:, c].rearrange("p j (i w) -> p j i w", i=PATCH),
                        images[t][:, c, :].rearrange("p (i j w) -> p j i w", i=PATCH, j=GRID))
                last.then_inc(s_columns, 1)

            def add_patch_bias(u):
                dve.wait_ge(s_patch, u + 1)
                if u >= 2:
                    dve.wait_ge(s_patch_out[u % 2], 16 * (u // 2))
                dve.tensor_tensor(patch_sb[u % 2], (B6, B7)[u % 2][:, 0:DIM], tokb, ALU.add
                                  ).then_inc(s_patch_sb, 1)

            gather_columns(0)
            dve.wait_ge(s_patchw, 32)
            for u in range(UNITS // 2 + 1):
                if u == 2:
                    gather_columns(1)
                add_patch_bias(u)

            def norm_stats(norm, g, count, later=True):
                for i in range(PER):
                    last = dve.bn_stats(stats[norm][:, i, :], h[:, g * PER + i, :])
                last.then_inc(s_stats[norm], 1)
                before, count = in_register(dve, [count - 1, count])
                dve.wait_ge(s_stats[norm], count)
                if later:
                    dve.wait_ge(s_normed[norm], before)
                for i in range(PER):
                    last = dve.bn_aggr(mean_var[norm][:, i, :], stats[norm][:, i, :])
                last.then_inc(s_aggr[norm], 1)
                dve.wait_ge(s_aggr[norm], count)
                dve.tensor_scalar(minus_mean[norm], mean_var[norm][:, :, 0], -1.0, None, ALU.mult)
                dve.tensor_scalar(spread[norm], mean_var[norm][:, :, 1], EPS, None, ALU.add
                                  ).then_inc(s_var[norm], 1)

            dve.wait_ge(s_text[0], 16 * 5)
            dve.wait_ge(s_rows_in[0], 16)
            dve.wait_ge(s_const, 1)
            for g in range(2):
                norm_stats(0, g, g + 1, later=g > 0)
                if g == 0:
                    for u in range(UNITS // 2 + 1, EARLY_UNITS):
                        add_patch_bias(u)
            for u in range(EARLY_UNITS, UNITS):
                add_patch_bias(u)
            dve.wait_ge(s_wgT, 1)
            dve.tensor_copy(wgT, B6[:, 0:CHUNKS * EXPERTS].rearrange("p (c e) -> p c e", c=CHUNKS)
                            ).then_inc(s_wgT_sb, 1)
            def step(s):
                b = s.b

                def scores(r):
                    return S[0:ROWS, r, 0:SPAN].rearrange("p (j t) -> p j t", j=4)

                def largest(r):
                    if b < ITEMS:
                        dve.wait_ge(s_scores, s.n(lambda b: 4 * b + r + 1))
                        dve.tensor_reduce(top[:, r, :], scores(r), AX.X, ALU.max).then_inc(s_max, 1)

                def turned(r):
                    if 0 <= b - 2 < ITEMS:
                        bank = ring_tile("probsT", b - 2, r)[0]
                        dve.wait_ge(s_high, s.n(lambda b: 4 * (b - 2) + r + 1))
                        dve.scalar_tensor_tensor(probT[1][:, r], R[bank][0:ROWS, 0:SPAN]
                                                 .rearrange("p (j t) -> p j t", j=4), P_SCALE, probT[0][:, r],
                                                 ALU.mult, ALU.subtract).then_inc(s_free[bank], 1)

                def less_largest(r):
                    if b < ITEMS:
                        dve.wait_ge(s_max, s.n(lambda b: 4 * b + r + 1))
                        if b >= 4:
                            dve.wait_ge(s_ring, s.n(lambda b: filled("probsT", b - 4, r)))
                        dve.tensor_tensor(prob[b % 4][:, r], scores(r),
                                          top[:, r, :].unsqueeze(2).to_broadcast([ROWS, 4, ROWS]),
                                          ALU.subtract).then_inc(s_sub, 1)

                if b == 2:
                    for i in range(2):
                        dve.wait_ge(s_patch_out[i], 16 * UNITS // 2)
                if b == 8:
                    dve.wait_ge(s_text[1], 16 * 4)
                    dve.wait_ge(s_rows_in[1], 16)
                turned(0)
                turned(1)
                largest(0)
                largest(1)
                largest(2)
                largest(3)
                less_largest(0)
                less_largest(1)
                less_largest(2)
                if 0 <= b - 3 < ITEMS:
                    dve.wait_ge(s_unnormed, s.n(lambda b: b - 2))
                    dve.reciprocal(recip, unnormed[:, :, VCOLS - 1]).then_inc(s_recip, 1)
                if b % PER == 0 and 0 <= b // PER - 2 < GROUPS:
                    dve.wait_ge(s_res, s.n(lambda b: b - 4))
                    norm_stats(1, s.n(lambda b: b // PER - 2), s.n(lambda b: b // PER - 1), later=b // PER > 2)
                if b % PER == 1 and b // PER + 2 < GROUPS:
                    norm_stats(0, s.n(lambda b: b // PER + 2), s.n(lambda b: b // PER + 3))
                turned(2)
                turned(3)
                less_largest(3)
                if 0 <= b - 4 < ITEMS:
                    if b % PER == 0:
                        dve.wait_ge(s_bias, s.n(lambda b: b // PER))
                    dve.wait_ge(s_proj, s.n(lambda b: b - 3))
                    row = h[:, s.n(lambda b: b - 4), :]
                    dve.tensor_tensor(row, row, B7[0:ROWS, DIM:2 * DIM], ALU.add).then_inc(s_res, 1)

            run_steps(dve, step)

            chain = [0]

            def then(ins):
                chain[0] += 1
                ins.then_inc(s_dve, 1)
                dve.wait_ge(s_dve, chain[0])

            dve.wait_ge(s_sc, 16)
            dve.wait_ge(s_consts2, 1)
            dve.tensor_reduce(row_top, sc, AX.X, ALU.max).then_inc(s_rowtop, 1)
            dve.tensor_reduce(abs_top, sc, AX.X, ALU.max, apply_absolute_value=True).then_inc(s_rowtop, 1)
            dve.wait_ge(s_pe, 1)
            then(dve.tensor_reduce(top_row[0:1, :], B7[0:1, 0:P].rearrange("p (e s) -> p e s", s=SEGS),
                                   AX.X, ALU.max, negate=True))
            dve.wait_ge(s_pe, 2)
            then(dve.tensor_copy(top_all, B7[:, DIM:DIM + EXPERTS]))
            then(dve.tensor_tensor_reduce(own_sums, top_all, own, 1.0, 0.0, ALU.mult, ALU.add, own_top))
            assert chain[0] == OWN_TOP
            dve.wait_ge(s_abs, 1)
            then(dve.tensor_scalar(highest, bound, 1.001, 1e-30, ALU.mult, ALU.add))
            dve.tensor_scalar(step_of, quarters, highest, None, ALU.mult)
            then(dve.tensor_scalar(low, highest, -1.0, None, ALU.mult))
            start, links = chain[0], 3
            with dve.Fori(0, ROUNDS // UNROLLED) as turn:
                for i in range(UNROLLED):
                    n = turn * UNROLLED + i
                    at_n = bass.ds(n, 1)
                    first, second, third, total = [dve.to_reg(v) for v in (
                        n * links + (start + 1), n * links + (start + 2), n * links + (start + 3), n + 1)]
                    here = tried[:, at_n, :].rearrange("p a c -> p (a c)")
                    dve.scalar_tensor_tensor(here, multiples, step_of[:, at_n],
                                             low.to_broadcast([P, CUTS_IN - 1]), ALU.mult, ALU.add).then_inc(s_dve, 1)
                    dve.wait_ge(s_const, 1)
                    dve.wait_ge(s_dve, first)
                    for j in range(CUTS_IN - 1):
                        last = dve.tensor_scalar(work[(1, 2, 4)[j]], sc,
                                                 tried[:, at_n, j:j + 1].rearrange("p a c -> p (a c)"), None,
                                                 ALU.is_ge, ALU.add, accum_out=counts[:, j:j + 1])
                    last.then_inc(s_count, 1)
                    dve.wait_ge(s_const, 1)
                    dve.wait_ge(s_total, total)
                    dve.tensor_scalar(reached[:, at_n, :].rearrange("p a c -> p (a c)"), B6[:, 0:CUTS_IN - 1],
                                      float(CAPACITY), None, ALU.is_ge, ALU.add, accum_out=passed
                                      ).then_inc(s_dve, 1)
                    dve.wait_ge(s_const, 1)
                    dve.wait_ge(s_dve, second)
                    dve.scalar_tensor_tensor(low, passed, step_of[:, at_n], low, ALU.mult, ALU.add).then_inc(s_dve, 1)
                    dve.wait_ge(s_const, 1)
                    dve.wait_ge(s_dve, third)
            chain[0] += links * ROUNDS
            then(dve.scalar_tensor_tensor(offered, reached, -MASKED, tried, ALU.mult, ALU.add))
            then(dve.tensor_reduce(high, offered.rearrange("p n c -> p (n c)"), AX.X, ALU.min))
            then(dve.tensor_tensor(high, high, highest, ALU.min))
            sure, maybe, order, zero = work[1], work[2], work[4], work[3]
            then(dve.tensor_scalar(sure, sc, high, None, ALU.is_ge, ALU.add, accum_out=count))
            dve.tensor_copy(sure_n, count).then_inc(s_count, 1)
            then(dve.scalar_tensor_tensor(maybe, sc, low, sure, ALU.is_ge, ALU.subtract))
            then(dve.tensor_tensor_scan(order, maybe, zero, 0.0, ALU.add, ALU.add))
            dve.tensor_copy(limit, order[:, SPAN - 1:SPAN]).then_inc(s_count, 1)
            dve.wait_ge(s_total, ROUNDS + 2)
            then(dve.tensor_scalar(need, B6[:, 0:1], -1.0, float(CAPACITY), ALU.mult, ALU.add))
            then(dve.tensor_tensor(need, need, B6[:, 1:2], ALU.subtract))
            then(dve.scalar_tensor_tensor(maybe, order, need, maybe, ALU.is_le, ALU.mult))
            then(dve.tensor_tensor(sure, sure, maybe, ALU.add))
            then(dve.tensor_tensor_scan(order, sure, zero, 0.0, ALU.add, ALU.add))
            dve.tensor_copy(limit2, order[:, SPAN - 1:SPAN]).then_inc(s_count, 1)
            dve.wait_ge(s_expd, 1)
            then(dve.tensor_tensor_reduce(maybe, work[0], sure, 1.0, 0.0, ALU.mult, ALU.add, row_sum))
            dve.tensor_scalar(own_sums, own, row_sum, None, ALU.mult).then_inc(s_count, 1)
            dve.wait_ge(s_total, ROUNDS + 3)
            then(dve.scalar_tensor_tensor(order, order, B6[:, 2:3], sure, ALU.add, ALU.mult))
            then(dve.tensor_scalar(ints[0], order, -1.0, None, ALU.add))
            dve.tensor_scalar(ints[1], ints[0], 7, None, ALU.arith_shift_right)
            then(dve.tensor_scalar(ints[2], ints[0], P - 1, None, ALU.bitwise_and))
            dve.tensor_copy(work[1], ints[1])
            dve.tensor_copy(work[2], ints[2]).then_inc(s_slots, 1)
            dve.tensor_scalar(tag_i[:, 1], tag_i[:, 0], 6, None, ALU.arith_shift_right)
            then(dve.tensor_scalar(tag_i[:, 2], tag_i[:, 0], TAG - 1, None, ALU.bitwise_and))
            dve.tensor_copy(tag[0], tag_i[:, 1])
            then(dve.tensor_copy(tag[1], tag_i[:, 2]))
            dve.wait_ge(s_total, ROUNDS + 4)
            then(dve.reciprocal(recip_all, B7[:, DIM:DIM + EXPERTS]))
            for i in range(2):
                dve.wait_ge(s_slotT, len(CUTS) * (i + 1))
                for c, (t0, n) in enumerate(CUTS):
                    last = dve.tensor_copy(slotT[i][0:n, c].rearrange("p e s -> p (e s)"),
                                           S[0:n, i, c * P:(c + 1) * P])
            then(last)

            def one_hots(s, ahead):
                if s.b + ahead > 0:
                    dve.wait_ge(s_list, s.n(lambda e: e + ahead))
                at_e = s.n(lambda e: e + ahead)
                tile_of = slotT[0][:, :, bass.ds(at_e, 1), :].rearrange("p c a s -> p c (a s)")
                row_of = slotT[1][:, :, bass.ds(at_e, 1), :].rearrange("p c a s -> p c (a s)")
                shape = [P, len(CUTS), SEGS]
                dve.tensor_tensor(match, tile_of.unsqueeze(3).to_broadcast(shape + [TILES]),
                                  iota_f[:, 0:TILES].unsqueeze(1).unsqueeze(1).to_broadcast(shape + [TILES]),
                                  ALU.is_equal).then_inc(s_match, 1)
                dve.tensor_tensor(onehot, row_of.unsqueeze(3).to_broadcast(shape + [P]),
                                  iota_f[:, :].unsqueeze(1).unsqueeze(1).to_broadcast(shape + [P]), ALU.is_equal)
                dve.wait_ge(s_match, s.n(lambda e: e + ahead + 1))
                for i in range(2):
                    last = dve.tensor_tensor(tagged[:, :, :, i, :], match,
                                             tag[i].unsqueeze(3).to_broadcast(shape + [TILES]), ALU.mult)
                last.then_inc(s_onehot, 1)

            def list_tokens(s, ahead):
                par = (s.b + ahead) % 2
                dve.wait_ge(s_list, s.n(lambda e: e + ahead + 1))
                dve.tensor_copy(number, B7[:, DIM:DIM + 2 * TILES].rearrange("p (a t) -> p a t", a=2)
                                ).then_inc(s_number, 1)
                dve.wait_ge(s_number, s.n(lambda e: e + ahead + 1))
                if s.b + ahead >= 2:
                    dve.wait_ge(s_added[par], s.n(lambda e: 16 * TILES * ((e + ahead) // 2)))
                dve.scalar_tensor_tensor(index[par], number[:, 0], float(TAG), number[:, 1], ALU.mult, ALU.add
                                         ).then_inc(s_index, 1)

            one_hots(Step(0), 0)
            list_tokens(Step(0), 0)
            one_hots(Step(0), 1)

            def expert(s):
                par = s.b % 2
                if s.b + 1 < EXPERTS:
                    list_tokens(s, 1)
                dve.wait_ge(s_wexp, s.n(lambda e: e + 1))
                dve.tensor_scalar(token_w[par], token_w[par], recip_all[:, bass.ds(s.n(lambda e: e), 1)], None,
                                  ALU.mult).then_inc(s_tokw, 1)
                for i in range(2 * HM):
                    t0, t1 = HALVES[i // HM]
                    n = sum(tile_rows(t) for t in range(t0, t1))
                    dve.wait_ge(s_silu, s.n(lambda e: 2 * HM * e + i + 1))
                    dve.tensor_tensor(hT[:, i % HM, t0 * P:t0 * P + n], gated[i % 2][:, 0:n],
                                      S[:, 2 * (i % 2) + 1, 0:n], ALU.mult).then_inc(s_hT, 1)
                if s.b + 2 < EXPERTS:
                    one_hots(s, 2)

            run_experts(dve, expert)

        @block.tensor
        def _(pe):
            def ring_free(kind, s, which, i):
                pe.wait_ge(s_free[ring_tile(kind, which(s.b), i)[0]],
                           s.n(lambda b: ring_tile(kind, which(b), i)[1] - 1))

            def turn_patches(u):
                t, j = divmod(u, GRID)
                if u % GRID == 0:
                    pe.wait_ge(s_columns, t + 1)
                for i in range(2):
                    if u > 0:
                        pe.wait_ge(s_free[i], unit_tile(u, i) // 2)
                    for k in range(4 * i, min(4 * i + 4, PATCH_DIM // P)):
                        c, half = divmod(k, 2)
                        last = pe.transpose(R[i][:, P * (k % 4):P * (k % 4 + 1)],
                                            columns[t][:, c, j, P * half:P * (half + 1)], ident[:, :])
                    last.then_inc(s_ring, 1)

            def project_patches(u):
                for i in range(2):
                    pe.wait_ge(s_free[i], unit_tile(u, i) // 2 + 1)
                if u >= 2:
                    pe.wait_ge(s_patch_sb, u - 1)
                for k in range(PATCH_DIM // P):
                    last = pe.matmul((B6, B7)[u % 2][:, 0:DIM], patchT[u % 2][:, k, :], tokw[:, k, :],
                                     start=(k == 0), stop=(k == PATCH_DIM // P - 1))
                last.then_inc(s_patch, 1)

            pe.wait_ge(s_const, 1)
            turn_patches(0)
            pe.wait_ge(s_patchw, 32)

            def patches(units):
                for u in units:
                    if u + 1 in units:
                        turn_patches(u + 1)
                    project_patches(u)

            patches(range(EARLY_UNITS))
            pe.wait_ge(s_weights, 16 * 6)

            def also_moved(kind, s, which, next_bank):
                for i in range(2 if kind != "gate" else 1):
                    if ring_tile(kind, which(s.b), i)[0] != next_bank:
                        wait_moved(pe, kind, s, which, i)

            def piece(kind, s, which, gpar, i):
                bank = ring_tile(kind, which(s.b), i)[0]
                dst = R[bank]
                if kind in ("xT", "x2T"):
                    norm, rows = (0, xn) if kind == "xT" else (1, xn2[gpar])
                    pe.wait_ge(s_normed[norm], s.n(lambda b: which(b) + 1))
                    ring_free(kind, s, which, i)
                    for j in range(PER):
                        last = pe.transpose(dst[:, ROWS * j:ROWS * (j + 1)], rows[:, j, P * i:P * (i + 1)],
                                            ident[0:ROWS, 0:ROWS])
                if kind in ("q", "k"):
                    w = wq if kind == "q" else wk
                    also_moved("xT", s, which, bank)
                    ring_free(kind, s, which, i)
                    for k in range(CHUNKS):
                        last = pe.matmul(dst[:, 0:SPAN], w[:, k, P * i:P * (i + 1)], xT[:, k, :],
                                         start=(k == 0), stop=(k == CHUNKS - 1))
                if kind == "v":
                    ring_free(kind, s, which, i)
                    for j in range(2):
                        for k in range(CHUNKS):
                            last = pe.matmul(dst[0:ROWS, DIM * j:DIM * (j + 1)],
                                             xT[:, k, ROWS * (2 * i + j):ROWS * (2 * i + j + 1)], wv[:, k, :],
                                             start=(k == 0), stop=(k == CHUNKS - 1))
                if kind == "gate":
                    also_moved("x2T", s, which, bank)
                    ring_free(kind, s, which, i)
                    for k in range(CHUNKS):
                        last = pe.matmul(dst[0:EXPERTS, 0:SPAN], wgT[:, k, :], x2T[:, k, :],
                                         start=(k == 0), stop=(k == CHUNKS - 1))
                if kind == "gateT":
                    router, free = in_register(pe, [s.n(lambda b: ring_tile("gate", which(b))[1]),
                                                    s.n(lambda b: ring_tile("gateT", which(b))[1] - 1)])
                    if ring_tile("gate", which(s.b))[0] != bank:
                        pe.wait_ge(s_free[1 - bank], router)
                    pe.wait_ge(s_free[bank], free)
                    for j in range(PER):
                        last = pe.transpose(dst[0:ROWS, EXPERTS * j:EXPERTS * (j + 1)],
                                            gate_sb[gpar][:, ROWS * j:ROWS * (j + 1)],
                                            ident[0:EXPERTS, 0:EXPERTS])
                last.then_inc(s_ring, 1)

            for kind, which, i in FIRST_PIECES:
                piece(kind, Step(0), lambda b: which, which % 2, i)
            turn_patches(EARLY_UNITS)
            patches(range(EARLY_UNITS, UNITS))
            pe.wait_ge(s_patch_sb, UNITS)
            for c in range(CHUNKS):
                last = pe.transpose(B6[:, c * EXPERTS:(c + 1) * EXPERTS], wg_rows[:, c * P:(c + 1) * P],
                                    ident[0:EXPERTS, 0:EXPERTS])
            last.then_inc(s_wgT, 1)
            pe.wait_ge(s_wgT_sb, 1)

            def group_pieces(s):
                for kind, which, i in pieces(s.b):
                    piece(kind, s, lambda b, lag=which - s.b // PER: b // PER + lag, which % 2, i)

            def step(s):
                b = s.b

                def scores(ahead, r):
                    b = s.b + ahead
                    if b >= ITEMS:
                        return
                    gpar, item = b // PER % 2, b % PER
                    if item == 0 and r == 0:
                        pe.wait_ge(s_q_in, s.n(lambda b: 16 * 4 * ((b + ahead) // PER + 1)))
                        pe.wait_ge(s_k_in, s.n(lambda b: 16 * 8 * ((b + ahead) // PER + 1)))
                    if b > 0:
                        pe.wait_ge(s_sub, s.n(lambda b: 4 * (b + ahead) - 3 + r))
                    pe.matmul(S[0:ROWS, r, 0:SPAN], ident_b[0:ROWS, 0:ROWS],
                              mask.rearrange("p j t -> p (j t)"), start=True, stop=False, skip_group_check=True)
                    for a in (2 * r, 2 * r + 1):
                        last = pe.matmul(S[0:ROWS, r, 2 * ROWS * (a % 2):2 * ROWS * (a % 2 + 1)],
                                         Q2[gpar][:, a, ROWS * item:ROWS * (item + 1)],
                                         K2[gpar][:, a, :, ROWS * item:ROWS * (item + 1)],
                                         start=False, stop=(a % 2 == 1), skip_group_check=True)
                    last.then_inc(s_scores, 1)

                def turn(r):
                    if not 0 <= b - 2 < ITEMS:
                        return
                    if r == 0:
                        pe.wait_ge(s_exp, s.n(lambda b: b - 1))
                    ring_free("probsT", s, lambda b: b - 2, r)
                    dst = R[ring_tile("probsT", b - 2, r)[0]]
                    for j in range(4):
                        last = pe.transpose(dst[0:ROWS, ROWS * j:ROWS * (j + 1)],
                                            prob[(b - 2) % 4][:, r, j, :], ident[0:ROWS, 0:ROWS])
                    last.then_inc(s_ring, 1)

                def outputs(behind, r):
                    b = s.b - behind
                    if not 0 <= b < ITEMS:
                        return
                    wait_moved(pe, "probsT", s, lambda b: b - behind, r)
                    gpar, item = b // PER % 2, b % PER
                    if item == 0 and r == 0:
                        pe.wait_ge(s_split, s.n(lambda b: SPLIT_AT[("v", (b - behind) // PER, 1)] + 1))
                    if r == 0 and b > 0:
                        pe.wait_ge(s_unnormed, s.n(lambda b: b - behind))
                    if r == 3 and b > 1:
                        pe.wait_ge(s_res, s.n(lambda b: b - behind - 1))
                    for j in range(4):
                        head = 4 * r + j
                        dst = B7[0:ROWS, 0:VCOLS] if head == SIDE else \
                            B6[0:ROWS, VCOLS * head:VCOLS * (head + 1)]
                        for part in range(2):
                            last = pe.matmul(dst, probT[part][:, r, j, :], v[gpar][:, item, head, :],
                                             start=(part == 0), stop=(part == 1), skip_group_check=True)
                    last.then_inc(s_pv, 1)

                turn(0)
                turn(1)
                if b == 0:
                    scores(0, 0)
                    scores(0, 1)
                scores(0, 2)
                scores(0, 3)
                outputs(3, 3)
                group_pieces(s)
                outputs(2, 0)
                if 0 <= b - 4 < ITEMS:
                    pe.wait_ge(s_norm, s.n(lambda b: b - 3))
                    ring_free("attnT", s, lambda b: b - 4, 0)
                    dst = R[ring_tile("attnT", b - 4)[0]]
                    for c in range(CHUNKS):
                        last = pe.transpose(dst[:, ROWS * c:ROWS * (c + 1)], attn[:, P * c:P * (c + 1)],
                                            ident[0:ROWS, 0:ROWS])
                    last.then_inc(s_ring, 1)
                outputs(2, 1)
                turn(2)
                turn(3)
                scores(1, 0)
                if 0 <= b - 4 < ITEMS:
                    wait_moved(pe, "attnT", s, lambda b: b - 4)
                    if b - 4 < ITEMS - 1:
                        pe.wait_ge(s_unnormed, s.n(lambda b: b - 2))
                    if b - 4 > 0:
                        pe.wait_ge(s_res, s.n(lambda b: b - 4))
                    for c in range(CHUNKS):
                        last = pe.matmul(B7[0:ROWS, DIM:2 * DIM], attn_nT[:, c, :], wo[:, c, :],
                                         start=(c == 0), stop=(c == CHUNKS - 1))
                    last.then_inc(s_proj, 1)
                scores(1, 1)
                outputs(2, 2)

            run_steps(pe, step)

            def ering_tile(s, i):
                if s.b >= 0 or i - XG_TILES >= 2:
                    pe.wait_ge(s_emoved, s.n(lambda e: ering(e, i - 1)))
                return R[ering(s.b, i) % 2]

            def weights(s, tiles=range(W_TILES)):
                par = (s.b + 1) % 2
                if tiles[0] == 0:
                    pe.wait_ge(s_raw[par], s.n(lambda e: 48 * ((e + 1) // 2 + 1)))
                for i in tiles:
                    dst = ering_tile(s, XG_TILES + i)
                    for m in range(4):
                        if i < 4:
                            src = (w1_raw if i < 2 else w3_raw)[par][:, m, P * (i % 2):P * (i % 2 + 1)]
                        else:
                            hm = 2 * (i - 4) + m // 2
                            src = w2_raw[par][:, m % 2, P * hm:P * (hm + 1)]
                        last = pe.transpose(dst[:, P * m:P * (m + 1)], src, ident[:, :])
                    last.then_inc(s_ering, 1)

            pe.wait_ge(s_rowtop, 1)
            pe.transpose(B7[0:1, 0:P], row_top, ident[:, :]).then_inc(s_pe, 1)
            pe.wait_ge(s_consts2, 1)
            pe.wait_ge(s_dve, 1)
            pe.matmul(B7[:, DIM:DIM + EXPERTS], all_ones[0:1, :], top_row[0:1, :], start=True, stop=True
                      ).then_inc(s_pe, 1)

            def total(turn):
                pe.wait_ge(s_count, turn + 1)
                pe.matmul(B6[:, 0:CUTS_IN - 1], same_block, counts, start=True, stop=True).then_inc(s_total, 1)

            for n in range(W_TILES):
                total(n)
                weights(Step(-1), (n,))
            with pe.Fori(W_TILES, ROUNDS) as turn:
                total(turn)
            for i, (block_of, col) in enumerate(((same_block, sure_n), (before_block, limit), (before_block, limit2))):
                pe.wait_ge(s_count, ROUNDS + i + 1)
                pe.matmul(B6[:, i:i + 1], block_of, col, start=True, stop=True).then_inc(s_total, 1)
            pe.wait_ge(s_count, ROUNDS + 4)
            pe.matmul(B7[:, DIM:DIM + EXPERTS], all_ones, own_sums, start=True, stop=True).then_inc(s_total, 1)
            pe.wait_ge(s_slots, 1)
            for i in range(2):
                for c, (t0, n) in enumerate(CUTS):
                    pe.transpose(S[0:n, i, c * P:(c + 1) * P], work[1 + i][:, t0:t0 + n], ident[:, :]
                                 ).then_inc(s_slotT, 1)

            def list_tokens(s, ahead):
                pe.wait_ge(s_onehot, s.n(lambda e: e + ahead + 1))
                if s.b + ahead > 0:
                    pe.wait_ge(s_number, s.n(lambda e: e + ahead))
                for c in range(len(CUTS)):
                    for g in range(SEGS):
                        last = pe.matmul(B7[:, DIM:DIM + 2 * TILES], onehot[:, c, g, :],
                                         tagged[:, c, g].rearrange("p a t -> p (a t)"),
                                         start=(c == 0 and g == 0), stop=(c == len(CUTS) - 1 and g == SEGS - 1))
                last.then_inc(s_list, 1)

            pe.wait_ge(s_dve, ROUTED)
            list_tokens(Step(0), 0)

            def expert(s):
                par = s.b % 2
                pe.wait_ge(s_xg[par], s.n(lambda e: 16 * TILES * (e // 2 + 1)))
                for i in range(XG_TILES):
                    dst = ering_tile(s, i)
                    for c in range(CHUNKS):
                        for t in (2 * i, 2 * i + 1):
                            n = tile_rows(t)
                            at0 = 2 * P * c + P * (t % 2)
                            last = pe.transpose(dst[:, at0:at0 + n], xg[par][0:n, t, P * c:P * (c + 1)],
                                                ident[0:n, 0:n])
                    last.then_inc(s_ering, 1)
                if s.b + 1 < EXPERTS:
                    list_tokens(s, 1)
                for i in range(2 * HM):
                    half, m = divmod(i, HM)
                    t0, t1 = HALVES[half]
                    n = sum(tile_rows(t) for t in range(t0, t1))
                    if m == 0:
                        pe.wait_ge(s_emoved, s.n(lambda e: ering(e, min(XG_TILES, (t1 + 1) // 2))))
                    if i >= 2:
                        pe.wait_ge(s_hT, s.n(lambda e: 2 * HM * e + i - 1))
                    for w, bank in ((w1T, 0), (w3T, 1)):
                        for k in range(CHUNKS):
                            last = pe.matmul(S[:, 2 * (i % 2) + bank, 0:n], w[par][:, k, P * m:P * (m + 1)],
                                             xgT[:, k, P * t0:P * t0 + n], start=(k == 0), stop=(k == CHUNKS - 1))
                    last.then_inc(s_hidden, 1)
                if s.b + 1 < EXPERTS:
                    weights(s)
                for t in range(TILES):
                    n = tile_rows(t)
                    if t in (HALVES[0][0], HALVES[1][0]):
                        pe.wait_ge(s_hT, s.n(lambda e: 2 * HM * e + HM * (1 if t == 0 else 2)))
                    if t >= 2:
                        pe.wait_ge(s_y_sb, s.n(lambda e: TILES * e + t - 1))
                    for m in range(HM):
                        last = pe.matmul((B6, B7)[t % 2][0:n, 0:DIM], hT[:, m, P * t:P * t + n], w2T[par][:, m, :],
                                         start=(m == 0), stop=(m == HM - 1))
                    last.then_inc(s_y, 1)

            run_experts(pe, expert)


_INS = ['x', 'txt', 'L0_tok_W', 'L0_tok_b', 'L0_tok_cls_token', 'L0_attn_Wq', 'L0_attn_Wk', 'L0_attn_Wv',
        'L0_attn_Wo', 'L0_attn_bo', 'L0_ffn_Wg', 'L0_ffn_W1', 'L0_ffn_W2', 'L0_ffn_W3']
_OUTS = [((ITEMS, ROWS, DIM), 'float32')]


def kernel(**inputs):
    import numpy as _np
    import concourse.bacc as _bacc
    from concourse import mybir as _mybir
    from concourse.bass_utils import run_bass_kernel_spmd as _run

    nc = _bacc.Bacc("TRN2", target_bir_lowering=False, num_devices=1)
    arrays, args = {}, []
    for name in _INS:
        a = _np.ascontiguousarray(inputs[name])
        arrays[f"in_{name}_dram"] = a
        args.append(nc.dram_tensor(f"in_{name}_dram", a.shape, _mybir.dt.from_np(a.dtype), kind="ExternalInput").ap())
    for i, (shape, dtype) in enumerate(_OUTS):
        dt = _mybir.dt.from_np(_np.dtype(dtype))
        args.append(nc.dram_tensor(f"out_{i}_dram", shape, dt, kind="ExternalOutput").ap())
    build(nc, *args)
    r = _run(nc, [arrays], core_ids=[0])
    return r.results[0]["out_0_dram"]
```

```python
import concourse.bass as bass
from concourse import mybir
from contextlib import ExitStack

F32 = mybir.dt.float32
BF16 = mybir.dt.bfloat16
F16 = mybir.dt.float16
I32 = mybir.dt.int32
U32 = mybir.dt.uint32
ALU = mybir.AluOpType
ACT = mybir.ActivationFunctionType
AX = mybir.AxisListType

ITEMS, CHANNELS, IMAGE = 64, 3, 64
PATCH = 16
GRID = IMAGE // PATCH
PATCHES = GRID * GRID
PATCH_DIM = CHANNELS * PATCH * PATCH
TEXT = 77
DIM = 256
ROWS = 1 + PATCHES + TEXT
HEADS, HEAD = 16, 16
EXPERTS, HIDDEN = 8, 512
TOKENS = ITEMS * ROWS
CAPACITY = TOKENS // EXPERTS
EPS = 1e-5
P = 128
CHUNKS = DIM // P
PER = 4
GROUPS = ITEMS // PER
SPAN = PER * ROWS
LOOP = 8
MASKED = -1e30
EXPONENT = 0x7F800000
ROW = DIM + EXPERTS
CUTS_IN = 4
ROUNDS, UNROLLED = 16, 4
TILES = -(-CAPACITY // P)
LAST = CAPACITY - (TILES - 1) * P
HALVES = ((0, 3), (3, TILES))
HM = HIDDEN // P
SEGS = P // EXPERTS
CUTS = [(c * P, min(P, SPAN - c * P)) for c in range(-(-SPAN // P))]
OWN_TOP, ROUTED = 3, 3 + 3 + 5 + 16
QK_SCALE, V_SCALE, P_SCALE = 32.0, 64.0, 4096.0
X_SCALE, HID_SCALE, W_SCALE = 32.0, 8.0, 256.0
SPLIT_PAIRS = ((0, 0), (0, 1), (1, 0))
PAIRS = HEADS // 2
VCOLS = 2 * HEAD + 1
SIDE = HEADS - 1
TAG = 64


class Step:

    def __init__(self, b, turn=None, stride=LOOP):
        self.b, self.turn, self.stride = b, turn, stride

    def n(self, f):
        v = f(self.b)
        return v if self.turn is None else v + (f(self.b + self.stride) - v) * self.turn


FIRST_STEPS, LAST_STEP = 2 * LOOP, 4 * (GROUPS - 1) + 13
LOOP_TURNS = GROUPS // 2 - 3


def run_steps(eng, step):
    for b in range(FIRST_STEPS):
        step(Step(b))
    with eng.Fori(0, LOOP_TURNS) as turn:
        for b in range(FIRST_STEPS, FIRST_STEPS + LOOP):
            step(Step(b, turn))
    for b in range(FIRST_STEPS + LOOP * LOOP_TURNS, LAST_STEP):
        step(Step(b))


def run_experts(eng, step):
    for e in range(2):
        step(Step(e))
    with eng.Fori(0, EXPERTS // 2 - 2) as turn:
        for e in range(2, 4):
            step(Step(e, turn, stride=2))
    for e in range(EXPERTS - 2, EXPERTS):
        step(Step(e))


SPLIT = ("q", "k", "v")


def pieces(b):
    g, k = divmod(b, PER)
    kinds = ([("gateT", g - 3, 0), ("q", g + 1, 0), ("q", g + 1, 1)],
             [("k", g + 1, 0), ("k", g + 1, 1)],
             [("x2T", g - 2, 0), ("x2T", g - 2, 1), ("v", g + 1, 0)],
             [("v", g + 1, 1), ("gate", g - 2, 0), ("xT", g + 2, 0), ("xT", g + 2, 1)])[k]
    return [t for t in kinds if 0 <= t[1] < GROUPS]


def ring_tiles(b):
    probs = [("probsT", b - 2, r) for r in range(4)] if 0 <= b - 2 < ITEMS else []
    attn = [("attnT", b - 4, 0)] if 0 <= b - 4 < ITEMS else []
    return probs[0:2] + pieces(b) + attn + probs[2:4]


UNITS = 2 * GRID
FIRST_PIECES = [(_kind, _g, _i) for _kind, _g in (("xT", 0), ("q", 0), ("k", 0), ("v", 0), ("xT", 1))
                for _i in range(2)]
RING_AT = {}
SPLIT_AT = {}

EARLY_UNITS = 6


def unit_tile(u, i):
    return 2 * u + i + (len(FIRST_PIECES) if u >= EARLY_UNITS else 0)


_n, _m = 2 * EARLY_UNITS, 0
for _t in FIRST_PIECES + [_t for _b in range(LAST_STEP) for _t in ring_tiles(_b)]:
    RING_AT[_t] = _n
    _n += 1
    if _t == FIRST_PIECES[-1]:
        _n += 2 * (UNITS - EARLY_UNITS)
    if _t[0] in SPLIT:
        SPLIT_AT[_t] = _m
        _m += 1


def build(nc, x, txt, tok_W, tok_b, cls_token, Wq, Wk, Wv, Wo, bo, Wg, W1, W2, W3, out):
    out_rows = out.rearrange("b s c -> (b s) c")
    patch_rows = nc.dram_tensor("patch_rows", [ITEMS, PATCHES, DIM], F32).ap()
    stored = nc.dram_tensor("stored", [TOKENS, ROW], F32).ap()
    gate_rows = nc.dram_tensor("gate_rows", [EXPERTS, TOKENS], F32).ap()
    q_rows = nc.dram_tensor("q_rows", [2, DIM, SPAN], F16).ap()
    k_rows = nc.dram_tensor("k_rows", [2, DIM, SPAN], F16).ap()

    ctx = ExitStack()
    with ctx:
        def sb(name, shape, dt=F32):
            return ctx.enter_context(nc.sbuf_tensor(name, shape, dt))

        def sem(name):
            return ctx.enter_context(nc.semaphore(name))

        ident = sb("ident", [P, P])
        ident_b = sb("ident_b", [P, P], BF16)
        iota_f = sb("iota_f", [P, P])

        ARENA = 48000
        arena = sb("arena", [P, ARENA])

        class Carve:
            def __init__(self):
                self.at = 0

            def __call__(self, *shape, dt=F32, parts=P):
                n = 1
                for s in shape:
                    n *= s
                words = n if dt in (F32, I32, U32) else (n + 1) // 2
                ap = arena[0:parts, self.at:self.at + words]
                self.at += (words + 7) // 8 * 8
                assert self.at <= ARENA, self.at
                if dt != F32:
                    ap = ap.bitcast(dt)[:, 0:n]
                if len(shape) > 1:
                    names = "abcde"[:len(shape)]
                    ap = ap.rearrange(f"p ({' '.join(names)}) -> p {' '.join(names)}",
                                      **dict(zip(names[1:], shape[1:])))
                return ap

        at = Carve()
        h = at(ITEMS, DIM, parts=ROWS)
        wq, wk, wv, wo = (at(CHUNKS, DIM) for _ in range(4))
        wgT = at(CHUNKS, EXPERTS)
        wg_rows = at(DIM, parts=EXPERTS)
        bo_rep = at(DIM, parts=ROWS)
        mask = at(4, ROWS, dt=BF16, parts=ROWS)
        minus_half = at(PER, parts=ROWS)
        v = [at(PER, HEADS, VCOLS, dt=F16, parts=ROWS) for _ in range(2)]
        K2_WORDS = PAIRS * 2 * SPAN // 2
        k2_words = [at(K2_WORDS) for _ in range(2)]
        K2 = [w.bitcast(F16).rearrange("p (a o t) -> p a o t", o=2, t=SPAN) for w in k2_words]
        working = at.at
        Q2 = [at(PAIRS, SPAN, dt=F16) for _ in range(2)]
        q_parts, k_parts = ([at(CHUNKS, SPAN, dt=F16) for _ in range(2)] for _ in range(2))
        staged = [at(512) for _ in range(2)]
        xn = at(PER, DIM, parts=ROWS)
        xT = at(CHUNKS, SPAN)
        prob = [at(4, 4, ROWS, parts=ROWS) for _ in range(4)]
        probT = [at(4, 4, ROWS, dt=F16, parts=ROWS) for _ in range(2)]
        unnormed = at(HEADS, VCOLS, parts=ROWS)
        summed = at(HEADS, HEAD, parts=ROWS)
        attn = at(DIM, parts=ROWS)
        attn_nT = at(CHUNKS, ROWS)
        xn2 = [at(PER, ROW, parts=ROWS) for _ in range(2)]
        x2T = at(CHUNKS, SPAN)
        gate_sb = [at(SPAN, parts=EXPERTS) for _ in range(2)]
        top = at(4, 4, parts=ROWS)
        recip = at(HEADS, parts=ROWS)
        stats = [at(PER, 6, parts=ROWS) for _ in range(2)]
        mean_var = [at(PER, 2, parts=ROWS) for _ in range(2)]
        spread = [at(PER, parts=ROWS) for _ in range(2)]
        rstd = [at(PER, parts=ROWS) for _ in range(2)]
        minus_mean = [at(PER, parts=ROWS) for _ in range(2)]
        shift = [at(PER, parts=ROWS) for _ in range(2)]
        pt = Carve()
        pt.at = working
        images = [pt(CHANNELS, PATCH * IMAGE) for _ in range(2)]
        columns = [pt(CHANNELS, GRID, PATCH * PATCH) for _ in range(2)]
        tokw = pt(PATCH_DIM // P, DIM)
        tokb = pt(DIM)
        patchT = [pt(PATCH_DIM // P, P) for _ in range(2)]
        patch_sb = [pt(DIM) for _ in range(2)]

        early = Carve()
        early.at = at.at
        sc = early(SPAN)
        same_block = early(P)
        before_block = early(P)
        own = early(EXPERTS)
        quarters, multiples = early(ROUNDS + 1), early(CUTS_IN - 1)
        rt = Carve()
        work = [rt(SPAN) for _ in range(5)]
        ints = [rt(SPAN, dt=I32) for _ in range(3)]
        low, high, highest, count, passed, base = (rt(1) for _ in range(6))
        step_of = rt(ROUNDS + 1)
        tried = rt(ROUNDS + 1, CUTS_IN - 1)
        reached, missed, offered, offered_low = (rt(ROUNDS, CUTS_IN - 1) for _ in range(4))
        ahead = rt(CUTS_IN - 1)
        counts = rt(CUTS_IN - 1)
        row_top, abs_top, bound, own_top, row_sum, need, limit, sure_n, limit2 = (rt(1) for _ in range(9))
        top_row = rt(EXPERTS)
        own_sums = rt(EXPERTS)
        all_ones = rt(P)
        top_all = rt(EXPERTS)
        recip_all = rt(EXPERTS)
        slotT = [rt(len(CUTS), EXPERTS, SEGS) for _ in range(2)]
        tag = [rt(len(CUTS), SEGS) for _ in range(2)]
        tag_i = rt(3, len(CUTS), SEGS, dt=I32)
        onehot = rt(len(CUTS), SEGS, P, dt=BF16)
        match = rt(len(CUTS), SEGS, TILES)
        tagged = rt(len(CUTS), SEGS, 2, TILES, dt=BF16)
        number = rt(2, TILES)
        index = [rt(TILES, dt=U32) for _ in range(2)]
        xg = [rt(TILES, ROW) for _ in range(2)]
        xgT = [rt(CHUNKS, CAPACITY, dt=F16) for _ in range(2)]
        w1_raw, w3_raw = ([rt(HM, DIM) for _ in range(2)] for _ in range(2))
        w2_raw = [rt(CHUNKS, HIDDEN) for _ in range(2)]
        w1T, w3T = ([[rt(CHUNKS, HIDDEN, dt=F16) for _ in range(2)] for _ in range(2)] for _ in range(2))
        w2T = [[rt(HM, DIM, dt=F16) for _ in range(2)] for _ in range(2)]
        first_weights = rt(6, HIDDEN)
        gated = [rt(3 * P) for _ in range(2)]
        hidden = [rt(3 * P) for _ in range(2)]
        hT = [rt(HM, CAPACITY, dt=F16) for _ in range(2)]
        token_w = [rt(TILES) for _ in range(2)]
        y = [rt(TILES, DIM) for _ in range(2)]

        S = ctx.enter_context(nc.psum_tensor("S", [P, 4, 512], F32))
        R = [ctx.enter_context(nc.psum_tensor(f"R{i}", [P, 512], F32)) for i in range(2)]
        B6 = ctx.enter_context(nc.psum_tensor("B6", [P, 512], F32))
        B7 = ctx.enter_context(nc.psum_tensor("B7", [P, 512], F32))

        s_weights, s_patchw = sem("s_weights"), sem("s_patchw")
        s_text = [sem(f"s_text{i}") for i in range(2)]
        s_rows_in = [sem(f"s_rows_in{i}") for i in range(2)]
        s_images = [sem(f"s_images{i}") for i in range(2)]
        s_columns = sem("s_columns")
        s_build, s_const = sem("s_build"), sem("s_const")
        s_patch, s_patch_sb = sem("s_patch"), sem("s_patch_sb")
        s_patch_out = [sem(f"s_patch_out{i}") for i in range(2)]
        s_wgT, s_wgT_sb = sem("s_wgT"), sem("s_wgT_sb")
        s_ring = sem("s_ring")
        s_free = [sem(f"s_free{i}") for i in range(2)]
        s_high = sem("s_high")
        s_parted = sem("s_parted")
        s_split = sem("s_split")
        s_q_out, s_q_in, s_k_out, s_k_in = map(sem, ("s_q_out", "s_q_in", "s_k_out", "s_k_in"))
        s_scores, s_max, s_sub, s_exp = map(sem, ("s_scores", "s_max", "s_sub", "s_exp"))
        s_pv, s_unnormed, s_recip, s_summed, s_norm, s_proj, s_res = map(
            sem, ("s_pv", "s_unnormed", "s_recip", "s_summed", "s_norm", "s_proj", "s_res"))
        s_stats = [sem(f"s_stats{i}") for i in range(2)]
        s_aggr = [sem(f"s_aggr{i}") for i in range(2)]
        s_var = [sem(f"s_var{i}") for i in range(2)]
        s_pow = [sem(f"s_pow{i}") for i in range(2)]
        s_rstd = [sem(f"s_rstd{i}") for i in range(2)]
        s_normed = [sem(f"s_normed{i}") for i in range(2)]
        s_bias, s_h_out = sem("s_bias"), sem("s_h_out")
        s_stored = [sem(f"s_stored{i}") for i in range(2)]
        s_gate_out = [sem(f"s_gate_out{i}") for i in range(2)]
        s_sc, s_consts2, s_build2, s_ones, s_tags = map(sem, ("s_sc", "s_consts2", "s_build2", "s_ones", "s_tags"))
        s_tried, s_ahead, s_passed, s_base = map(sem, ("s_tried", "s_ahead", "s_passed", "s_base"))
        s_dve, s_rowtop, s_abs, s_pe, s_count, s_total, s_expd = map(
            sem, ("s_dve", "s_rowtop", "s_abs", "s_pe", "s_count", "s_total", "s_expd"))
        s_slots, s_slotT, s_slotT_sb = map(sem, ("s_slots", "s_slotT", "s_slotT_sb"))
        s_match, s_onehot, s_list, s_number, s_index = map(
            sem, ("s_match", "s_onehot", "s_list", "s_number", "s_index"))
        s_raw = [sem(f"s_raw{i}") for i in range(2)]
        s_xg = [sem(f"s_xg{i}") for i in range(2)]
        s_ering, s_emoved = sem("s_ering"), sem("s_emoved")
        s_ehigh, s_first_low = sem("s_ehigh"), sem("s_first_low")
        s_hidden, s_silu, s_product, s_hidden_high, s_hT = map(
            sem, ("s_hidden", "s_silu", "s_product", "s_hidden_high", "s_hT"))
        s_wexp, s_tokw, s_y, s_y_sb = map(sem, ("s_wexp", "s_tokw", "s_y", "s_y_sb"))
        s_added = [sem(f"s_added{i}") for i in range(2)]

        block = ctx.enter_context(nc.Block())

        XG_TILES, W_TILES = TILES // 2, 6
        EXPERT_TILES = XG_TILES + W_TILES

        def ring_tile(kind, which, i=0):
            n = RING_AT[(kind, which, i)]
            return n % 2, n // 2 + 1

        def wait_moved(eng, kind, s, which, i=0):
            eng.wait_ge(s_free[ring_tile(kind, which(s.b), i)[0]],
                        s.n(lambda b: ring_tile(kind, which(b), i)[1]))

        def filled(kind, which, i=0):
            return RING_AT[(kind, which, i)] + 1

        def ering(e, i):
            return W_TILES + e * EXPERT_TILES + i

        def weight_parts(e, i):
            if i < 4:
                return [part[:, i % 2, :] for part in (w1T if i < 2 else w3T)[e % 2]]
            return [part[:, 2 * (i - 4):2 * (i - 4) + 2, :].rearrange("p m c -> p (m c)") for part in w2T[e % 2]]

        def in_register(eng, n):
            counts = [k if isinstance(k, int) else eng.to_reg(k) for k in n]
            eng.wait_ge(s_const, 1)
            return counts

        def half_of(i):
            t0, t1 = HALVES[i // HM]
            return t0, sum(tile_rows(t) for t in range(t0, t1))

        def tile_rows(t):
            return P if t < TILES - 1 else LAST

        @block.sync
        def _(sp):
            xv = x.rearrange("b c (g i) w -> b g c (i w)", g=GRID)
            n = ITEMS // 8

            def load_images(t):
                for c in range(CHANNELS):
                    sp.dma_start(images[t][:, c, :], xv[32 * t:32 * (t + 1), :, c, :]).then_inc(s_images[t], 16)

            def load_text(q):
                sp.dma_start(h[1 + PATCHES:ROWS, n * q:n * (q + 1), :],
                             txt[n * q:n * (q + 1)].rearrange("b s c -> s b c")).then_inc(s_text[q // 4], 16)

            load_images(0)
            sp.dma_start(tokw, tok_W.rearrange("(k p) e -> p k e", p=P)).then_inc(s_patchw, 16)
            sp.dma_start(tokb, tok_b.rearrange("(a e) -> a e", a=1).to_broadcast([P, DIM])).then_inc(s_patchw, 16)
            sp.dma_start(h[0:1, :, :], cls_token.to_broadcast([1, ITEMS, DIM])).then_inc(s_text[0], 16)
            load_images(1)
            load_text(0)
            for w, dram in ((wq, Wq), (wk, Wk), (wv, Wv), (wo, Wo)):
                sp.dma_start(w, dram.rearrange("(k p) e -> p k e", p=P)).then_inc(s_weights, 16)
            sp.dma_start(wg_rows, Wg).then_inc(s_weights, 16)
            sp.dma_start(bo_rep, bo.rearrange("(a e) -> a e", a=1).to_broadcast([ROWS, DIM])
                         ).then_inc(s_weights, 16)
            by_row = patch_rows.rearrange("b (i j) e -> (b i) j e", i=GRID)

            def store_patches(u):
                t, j = divmod(u, GRID)
                sp.wait_ge(s_patch_sb, u + 1)
                sp.dma_start(by_row[P * t:P * (t + 1), j, :], patch_sb[u % 2]).then_inc(s_patch_out[u % 2], 16)

            def reload_patches(t):
                for i in range(2):
                    sp.wait_ge(s_patch_out[i], 16 * (t + 1) * GRID // 2)
                half = slice(ITEMS // 2 * t, ITEMS // 2 * (t + 1))
                sp.dma_start(h[1:1 + PATCHES, half, :], patch_rows[half].rearrange("b n e -> n b e")
                             ).then_inc(s_rows_in[t], 16)

            for u in range(UNITS // 2):
                store_patches(u)
                if 1 + u < 4:
                    load_text(1 + u)
            reload_patches(0)
            for u in range(UNITS // 2, EARLY_UNITS):
                store_patches(u)
            for q in range(4, 8):
                load_text(q)

            def restack(kind, s, which, gpar, first=False):
                parts, rows = (q_parts, q_rows) if kind == "q" else (k_parts, k_rows)
                s_out, s_in, reads = (s_q_out, s_q_in, 4) if kind == "q" else (s_k_out, s_k_in, 8)
                split, read, written, scored = in_register(sp, [
                    s.n(lambda b: SPLIT_AT[(kind, which(b), 1)] + 1), s.n(lambda b: 16 * reads * which(b)),
                    s.n(lambda b: 32 * (which(b) + 1)), s.n(lambda b: 4 * PER * (which(b) - 1))])
                sp.wait_ge(s_split, split)
                if which(s.b) > 0:
                    sp.wait_ge(s_in, read)
                for i in range(2):
                    sp.dma_start(rows[i].rearrange("(c p) t -> p c t", p=P), parts[i]).then_inc(s_out, 16)
                sp.wait_ge(s_const, 1)
                sp.wait_ge(s_out, written)
                if which(s.b) >= 2:
                    sp.wait_ge(s_scores, scored)
                for mine in range(2):
                    for other in range(2):
                        if kind == "q":
                            p0 = 64 * other + 32 * mine
                            sp.dma_start(Q2[gpar][p0:p0 + 32],
                                         rows[mine].rearrange("(a p) t -> p a t", p=32)).then_inc(s_in, 16)
                        else:
                            for o in range(2):
                                p0 = 64 * mine + 32 * other + 16 * o
                                sp.dma_start(K2[gpar][p0:p0 + 16, :, o, :],
                                             rows[mine].rearrange("(a o p) t -> o p a t", o=2, p=16)[o]
                                             ).then_inc(s_in, 16)

            sp.wait_ge(s_const, 1)
            for kind, which, i in FIRST_PIECES:
                if kind in ("q", "k") and i == 1:
                    restack(kind, Step(0), lambda b: which, which % 2)
            for u in range(EARLY_UNITS, UNITS):
                store_patches(u)
            reload_patches(1)

            def step(s):
                b = s.b
                g, k = divmod(b, PER)
                if k == 0 and g + 1 < GROUPS:
                    restack("q", s, lambda b: b // PER + 1, (g + 1) % 2)
                if k == 0 and 0 <= g - 2 < GROUPS:
                    rows = bass.ds(s.n(lambda b: b - 2 * PER), PER)
                    sp.wait_ge(s_res, s.n(lambda b: b - 4))
                    sp.dma_start(out.rearrange("b s c -> s b c")[:, rows, :], h[:, rows, :]).then_inc(s_h_out, 16)
                if b == LAST_STEP - 1:
                    for i in range(2):
                        sp.wait_ge(s_gate_out[i], 16 * GROUPS // 2)
                    sp.dma_start(sc, gate_rows.rearrange("e (g t) -> (e g) t", g=SEGS)).then_inc(s_sc, 16)
                if k == 0 and 0 <= g - 3 < GROUPS:
                    par = (g - 3) % 2
                    wait_moved(sp, "gateT", s, lambda b: b // PER - 3)
                    sp.dma_start(stored.rearrange("(b s) c -> s b c", s=ROWS)[
                        :, bass.ds(s.n(lambda b: b - 3 * PER), PER), :], xn2[par]).then_inc(s_stored[par], 16)
                if k == 1 and g + 1 < GROUPS:
                    restack("k", s, lambda b: b // PER + 1, (g + 1) % 2)
                if k == 3 and 0 <= g - 2 < GROUPS:
                    par = g % 2
                    wait_moved(sp, "gate", s, lambda b: b // PER - 2)
                    sp.dma_start(gate_rows[:, bass.ds(s.n(lambda b: (b // PER - 2) * SPAN), SPAN)], gate_sb[par]
                                 ).then_inc(s_gate_out[par], 16)

            run_steps(sp, step)

            sp.wait_ge(s_h_out, 16 * GROUPS)

            def load_expert(s):
                par = s.b % 2
                if s.b >= 0:
                    sp.wait_ge(s_ering, s.n(lambda e: ering(e - 1, XG_TILES + W_TILES)))
                e = s.n(lambda e: e + 2)
                sp.dma_start(w1_raw[par], W1.rearrange("e (m p) c -> p e m c", p=P)[:, e]).then_inc(s_raw[par], 16)
                sp.dma_start(w3_raw[par], W3.rearrange("e (m p) c -> p e m c", p=P)[:, e]).then_inc(s_raw[par], 16)
                sp.dma_start(w2_raw[par], W2.rearrange("e (m p) c -> p e m c", p=P)[:, e]).then_inc(s_raw[par], 16)

            load_expert(Step(-2))
            load_expert(Step(-1))
            with sp.Fori(0, EXPERTS // 2 - 1) as turn:
                for e in range(2):
                    load_expert(Step(e, turn, stride=2))
            for i in range(2):
                sp.wait_ge(s_added[i], 16 * TILES * EXPERTS // 2)

        @block.gpsimd
        def _(pool):
            pool.memset(ident[:, :], 0.0)
            pool.memset(mask, 0.0)
            pool.memset(minus_half, -0.5)
            for i in range(2):
                pool.memset(k2_words[i], 0.0)
            pool.iota(iota_f[:, :], pattern=[[1, P]], base=0, channel_multiplier=0,
                      allow_small_or_imprecise_dtypes=True).then_inc(s_build, 1)
            pool.wait_ge(s_build, 1)
            pool.affine_select(out=ident[:, :], in_=ident[:, :], compare_op=ALU.not_equal, fill=1.0, base=0,
                               pattern=[[-1, P]], channel_multiplier=1)
            pool.affine_select(out=mask, in_=mask, compare_op=ALU.is_ge, fill=MASKED, base=0,
                               pattern=[[0, 4], [-1, ROWS]], channel_multiplier=1)
            for i in range(2):
                last = pool.memset(v[i].rearrange("p a b c -> p (a b) c")[:, :, VCOLS - 1:VCOLS], V_SCALE)
            last.then_inc(s_build, 1)
            pool.wait_ge(s_build, 2)
            pool.tensor_copy(ident_b[:, :], ident[:, :]).then_inc(s_const, 1)

            for n in range(ROUNDS + 1):
                pool.memset(quarters[:, n:n + 1], 2.0 * CUTS_IN ** -(n + 1))
            for i in range(1, CUTS_IN):
                pool.memset(multiples[:, i - 1:i], float(i))
            pool.memset(own, 1.0).then_inc(s_build2, 1)
            pool.wait_ge(s_build2, 1)
            pool.affine_select(out=own, in_=own, compare_op=ALU.is_ge, fill=0.0, base=0,
                               pattern=[[-SEGS, EXPERTS]], channel_multiplier=1).then_inc(s_build2, 1)
            pool.wait_ge(s_build2, 2)
            pool.affine_select(out=own, in_=own, compare_op=ALU.is_ge, fill=0.0, base=SEGS - 1,
                               pattern=[[SEGS, EXPERTS]], channel_multiplier=-1).then_inc(s_build2, 1)
            pool.wait_ge(s_build2, 3)
            pool.tensor_copy(same_block.rearrange("p (e s) -> p e s", s=SEGS),
                             own.unsqueeze(2).to_broadcast([P, EXPERTS, SEGS])).then_inc(s_build2, 1)
            pool.wait_ge(s_build2, 4)
            pool.affine_select(out=before_block, in_=same_block, compare_op=ALU.is_gt, fill=0.0, base=0,
                               pattern=[[1, P]], channel_multiplier=-1).then_inc(s_consts2, 1)

            def power(norm, count):
                pool.wait_ge(s_var[norm], count)
                pool.tensor_tensor(rstd[norm], spread[norm], minus_half, ALU.pow).then_inc(s_pow[norm], 1)
                pool.wait_ge(s_pow[norm], count)
                pool.tensor_tensor(shift[norm], minus_mean[norm], rstd[norm], ALU.mult).then_inc(s_rstd[norm], 1)

            def add_bias(g, count):
                pool.wait_ge(s_normed[0], count)
                rows = h[:, bass.ds(g * PER, PER), :]
                pool.tensor_tensor(rows, rows, bo_rep.unsqueeze(1).to_broadcast([ROWS, PER, DIM]), ALU.add
                                   ).then_inc(s_bias, 1)

            def piece(kind, s, which, gpar, i):
                if kind not in SPLIT:
                    return
                n = SPLIT_AT[(kind, which(s.b), i)]
                pool.wait_ge(s_parted, s.n(lambda b: SPLIT_AT[(kind, which(b), i)] + 1))
                if kind == "v":
                    items = v[gpar][:, 2 * i:2 * i + 2]
                    high, low = items[:, :, :, 0:HEAD], items[:, :, :, HEAD:2 * HEAD]
                    whole = staged[n % 2][0:ROWS].rearrange("p (i h d) -> p i h d", i=2, d=HEAD)
                else:
                    high, low = ((q_parts if kind == "q" else k_parts)[j][:, i, :] for j in range(2))
                    whole = staged[n % 2][:, 0:SPAN]
                pool.tensor_tensor(low, whole, high, ALU.subtract).then_inc(s_split, 1)

            def group_pieces(s):
                for kind, which, i in pieces(s.b):
                    piece(kind, s, lambda b, lag=which - s.b // PER: b // PER + lag, which % 2, i)

            pool.wait_ge(s_weights, 16 * 6)
            for g in range(2):
                power(0, g + 1)
            for g in range(2):
                for kind, which, i in FIRST_PIECES:
                    if which == g:
                        piece(kind, Step(0), lambda b: which, which % 2, i)
                add_bias(g, g + 1)

            def step(s):
                b = s.b
                g, k = divmod(b, PER)
                if k == 1 and 0 <= g - 2 < GROUPS:
                    power(1, s.n(lambda b: b // PER - 1))
                if k == 2 and g + 2 < GROUPS:
                    power(0, s.n(lambda b: b // PER + 3))
                group_pieces(s)
                if 0 <= b - 3 < ITEMS:
                    pool.wait_ge(s_unnormed, s.n(lambda b: b - 2))
                    pool.tensor_tensor(summed, unnormed[:, :, 0:HEAD], unnormed[:, :, HEAD:2 * HEAD], ALU.add
                                       ).then_inc(s_summed, 1)
                    pool.wait_ge(s_summed, s.n(lambda b: b - 2))
                    pool.wait_ge(s_recip, s.n(lambda b: b - 2))
                    if b - 3 > 0:
                        pool.wait_ge(s_ring, s.n(lambda b: filled("attnT", b - 4)))
                    pool.tensor_tensor(attn.rearrange("p (h d) -> p h d", d=HEAD), summed,
                                       recip.unsqueeze(2).to_broadcast([ROWS, HEADS, HEAD]), ALU.mult
                                       ).then_inc(s_norm, 1)
                if k == 3 and g + 2 < GROUPS:
                    add_bias(s.n(lambda b: b // PER + 2), s.n(lambda b: b // PER + 3))

            run_steps(pool, step)

            pool.wait_ge(s_sc, 16)
            pool.wait_ge(s_h_out, 16 * GROUPS)
            pool.memset(all_ones, 1.0).then_inc(s_ones, 1)
            pool.wait_ge(s_rowtop, 2)
            pool.partition_all_reduce(bound, abs_top, P, bass.bass_isa.ReduceOp.max).then_inc(s_abs, 1)
            pool.memset(work[3], 0.0)
            for i in range(2):
                pool.memset(slotT[i], -1.0)
                pool.memset(xg[i][:, TILES - 1, :], 0.0)
            pool.iota(tag_i[:, 0], pattern=[[P, len(CUTS)], [SPAN, SEGS]], base=0, channel_multiplier=1
                      ).then_inc(s_tags, 1)

            for i in range(W_TILES):
                high, low = weight_parts(0, i)
                pool.wait_ge(s_ehigh, i + 1)
                pool.tensor_tensor(low, first_weights[:, i, :], high, ALU.subtract).then_inc(s_first_low, 1)

            def gather(s, ahead):
                par = (s.b + ahead) % 2
                chosen, used = in_register(pool, [s.n(lambda e: e + ahead + 1),
                                                  s.n(lambda e: TILES * max(e + ahead - 1, 0))])
                pool.wait_ge(s_index, chosen)
                pool.wait_ge(s_y_sb, used)
                for t in range(TILES):
                    n = tile_rows(t)
                    pool.indirect_dma_start(
                        out=xg[par][0:n, t, :], out_offset=None, in_=stored,
                        in_offset=bass.IndirectOffsetOnAxis(ap=index[par][0:n, t:t + 1], axis=0),
                    ).then_inc(s_xg[par], 16)

            def scatter(s):
                par = s.b % 2
                landed, *weighted = in_register(pool, [s.n(lambda e: 16 * TILES * ((e + 1) // 2))] +
                                                [s.n(lambda e: TILES * e + t + 1) for t in range(TILES)])
                pool.wait_ge(s_y_sb, weighted[0])
                pool.wait_ge(s_added[1 - par], landed)
                for t in range(TILES):
                    n = tile_rows(t)
                    if t > 0:
                        pool.wait_ge(s_const, 1)
                        pool.wait_ge(s_y_sb, weighted[t])
                    pool.indirect_dma_start(
                        out=out_rows, out_offset=bass.IndirectOffsetOnAxis(ap=index[par][0:n, t:t + 1], axis=0),
                        in_=y[par][0:n, t, :], in_offset=None, compute_op=ALU.add,
                    ).then_inc(s_added[par], 16)

            def expert(s):
                if s.b + 1 < EXPERTS:
                    gather(s, 1)
                scatter(s)

            for i in range(2):
                pool.wait_ge(s_stored[i], 16 * GROUPS // 2)
            gather(Step(0), 0)
            gather(Step(0), 1)
            scatter(Step(0))
            with pool.Fori(0, EXPERTS // 2 - 1) as turn:
                for e in range(1, 3):
                    expert(Step(e, turn, stride=2))
            expert(Step(EXPERTS - 1))

        @block.scalar
        def _(act):
            def move(dst, src, bank):
                act.activation(dst, src, ACT.Copy).then_inc(s_free[bank], 1)

            def split(kind, s, which, i, high, whole, src, scale):
                act.activation(whole, src, ACT.Copy, scale=scale).then_inc(s_free[ring_tile(kind, which(s.b), i)[0]], 1)
                wait_moved(act, kind, s, which, i)
                act.activation(high, whole, ACT.Copy).then_inc(s_parted, 1)

            def move_patches(u):
                if u >= 2:
                    act.wait_ge(s_patch, u - 1)
                act.wait_ge(s_ring, unit_tile(u, 0) + 1)
                move(patchT[u % 2][:, 0:4, :], R[0][:, :].rearrange("p (k n) -> p k n", k=4), 0)
                act.wait_ge(s_ring, unit_tile(u, 1) + 1)
                move(patchT[u % 2][:, 4:6, :], R[1][:, 0:2 * P].rearrange("p (k n) -> p k n", k=2), 1)

            for u in range(EARLY_UNITS):
                move_patches(u)
            act.wait_ge(s_const, 1)

            def piece(kind, s, which, gpar, i):
                bank = ring_tile(kind, which(s.b), i)[0]
                if kind in ("q", "k") and i == 0 and which(s.b) > 0:
                    act.wait_ge(s_q_out if kind == "q" else s_k_out, s.n(lambda b: 32 * which(b)))
                if kind == "v" and i == 0 and which(s.b) >= 2:
                    act.wait_ge(s_pv, s.n(lambda b: 4 * PER * (which(b) - 1)))
                if kind == "gate" and which(s.b) >= 2:
                    act.wait_ge(s_gate_out[gpar], s.n(lambda b: 16 * (which(b) // 2)))
                act.wait_ge(s_ring, s.n(lambda b: filled(kind, which(b), i)))
                if kind == "xT":
                    move(xT[:, i, :], R[bank][:, 0:SPAN], bank)
                if kind in SPLIT:
                    n = SPLIT_AT[(kind, which(s.b), i)]
                    if n >= 2:
                        act.wait_ge(s_split, s.n(lambda b: SPLIT_AT[(kind, which(b), i)] - 1))
                if kind in ("q", "k"):
                    split(kind, s, which, i, (q_parts if kind == "q" else k_parts)[0][:, i, :],
                          staged[n % 2][:, 0:SPAN], R[bank][:, 0:SPAN], QK_SCALE)
                if kind == "v":
                    split(kind, s, which, i, v[gpar][:, 2 * i:2 * i + 2, :, 0:HEAD],
                          staged[n % 2][0:ROWS].rearrange("p (i h d) -> p i h d", i=2, d=HEAD),
                          R[bank][0:ROWS, :].rearrange("p (i h d) -> p i h d", i=2, d=HEAD), V_SCALE)
                if kind == "x2T":
                    move(x2T[:, i, :], R[bank][:, 0:SPAN], bank)
                if kind == "gate":
                    move(gate_sb[gpar], R[bank][0:EXPERTS, 0:SPAN], bank)
                if kind == "gateT":
                    move(xn2[gpar][:, :, DIM:ROW],
                         R[bank][0:ROWS, 0:PER * EXPERTS].rearrange("p (i e) -> p i e", i=PER), bank)

            def norm_row(norm, g, dst, count, i):
                if i == 0:
                    act.wait_ge(s_rstd[norm], count)
                ins = act.activation(dst[:, i, 0:DIM], h[:, g * PER + i, :], ACT.Identity,
                                     bias=shift[norm][:, i:i + 1], scale=rstd[norm][:, i:i + 1])
                if i == PER - 1:
                    ins.then_inc(s_normed[norm], 1)

            act.wait_ge(s_text[0], 16 * 5)
            act.wait_ge(s_rows_in[0], 16)
            for kind, which, i in FIRST_PIECES:
                if kind == "xT" and i == 0:
                    if which > 0:
                        act.wait_ge(s_ring, filled("xT", 0, 1))
                    for j in range(PER):
                        norm_row(0, which, xn, which + 1, j)
                piece(kind, Step(0), lambda b: which, which % 2, i)
            for u in range(EARLY_UNITS, UNITS):
                move_patches(u)

            def group_pieces(s):
                for kind, which, i in pieces(s.b):
                    piece(kind, s, lambda b, lag=which - s.b // PER: b // PER + lag, which % 2, i)

            def step(s):
                b = s.b

                def turned(r):
                    if 0 <= b - 2 < ITEMS:
                        if b - 2 > 0:
                            act.wait_ge(s_pv, s.n(lambda b: 4 * (b - 3) + r + 1))
                        act.wait_ge(s_ring, s.n(lambda b: filled("probsT", b - 2, r)))
                        act.activation(probT[0][:, r], R[ring_tile("probsT", b - 2, r)[0]][0:ROWS, 0:SPAN]
                                       .rearrange("p (j t) -> p j t", j=4), ACT.Copy, scale=P_SCALE
                                       ).then_inc(s_high, 1)

                def row(i):
                    g, k = divmod(b, PER)
                    if k == 1 and 0 <= g - 2 < GROUPS:
                        if i == 0 and g - 2 >= 2:
                            act.wait_ge(s_stored[g % 2], s.n(lambda b: 16 * ((b // PER - 2) // 2)))
                        norm_row(1, s.n(lambda b: b // PER - 2), xn2[g % 2], s.n(lambda b: b // PER - 1), i)
                    if k == 2 and g + 2 < GROUPS:
                        if i == 0:
                            act.wait_ge(s_ring, s.n(lambda b: filled("xT", b // PER + 1, 1)))
                        norm_row(0, s.n(lambda b: b // PER + 2), xn, s.n(lambda b: b // PER + 3), i)

                turned(0)
                turned(1)
                if 0 <= b - 1 < ITEMS:
                    act.wait_ge(s_sub, s.n(lambda b: 4 * b - 2))
                    rows_of = prob[(b - 1) % 4][:, 0:2]
                    act.activation(rows_of, rows_of, ACT.Exp, scale=HEAD ** -0.5 / QK_SCALE ** 2
                                   ).then_inc(s_exp, 1)
                if 0 <= b - 3 < ITEMS:
                    act.wait_ge(s_pv, s.n(lambda b: 4 * (b - 2)))
                    if b - 3 > 0:
                        act.wait_ge(s_norm, s.n(lambda b: b - 3))
                    act.activation(unnormed[:, 0:SIDE, :], B6[0:ROWS, 0:SIDE * VCOLS]
                                   .rearrange("p (h d) -> p h d", d=VCOLS), ACT.Copy)
                    act.activation(unnormed[:, SIDE, :], B7[0:ROWS, 0:VCOLS], ACT.Copy).then_inc(s_unnormed, 1)
                group_pieces(s)
                if 0 <= b - 4 < ITEMS:
                    if b - 4 > 0:
                        act.wait_ge(s_proj, s.n(lambda b: b - 4))
                    act.wait_ge(s_ring, s.n(lambda b: filled("attnT", b - 4)))
                    bank = ring_tile("attnT", b - 4)[0]
                    move(attn_nT, R[bank][:, 0:2 * ROWS].rearrange("p (c t) -> p c t", c=2), bank)
                row(0)
                row(1)
                turned(2)
                turned(3)
                if 0 <= b - 1 < ITEMS:
                    act.wait_ge(s_sub, s.n(lambda b: 4 * b))
                    rows_of = prob[(b - 1) % 4][:, 2:4]
                    act.activation(rows_of, rows_of, ACT.Exp, scale=HEAD ** -0.5 / QK_SCALE ** 2
                                   ).then_inc(s_exp, 1)
                row(2)
                row(3)

            run_steps(act, step)

            act.wait_ge(s_dve, OWN_TOP)
            act.activation(work[0], sc, ACT.Exp, bias=own_top).then_inc(s_expd, 1)

            for i in range(W_TILES):
                act.wait_ge(s_ering, i + 1)
                act.activation(first_weights[:, i, :], R[i % 2][:, :], ACT.Copy, scale=W_SCALE).then_inc(s_emoved, 1)
                act.wait_ge(s_emoved, i + 1)
                act.activation(weight_parts(0, i)[0], first_weights[:, i, :], ACT.Copy).then_inc(s_ehigh, 1)

            def high(dst, src, scale):
                act.activation(dst, src, ACT.Copy, scale=scale).then_inc(s_ehigh, 1)

            def weight_tile(s, i):
                if s.b + 1 < EXPERTS and 0 <= i < W_TILES:
                    act.wait_ge(s_ering, s.n(lambda e: ering(e, XG_TILES + i + 1)))
                    high(weight_parts(s.b + 1, i)[0], R[ering(s.b, XG_TILES + i) % 2][:, :], W_SCALE)

            def gathered_tile(s, ahead, i):
                if s.b + ahead < EXPERTS:
                    act.wait_ge(s_ering, s.n(lambda e: ering(e + ahead, i + 1)))
                    w = tile_rows(2 * i + 1) + P
                    high(xgT[0][:, :, 2 * P * i:2 * P * i + w],
                         R[ering(s.b + ahead, i) % 2][:, :].rearrange("p (c t) -> p c t", c=2)[:, :, 0:w], X_SCALE)

            def expert(s):
                par = s.b % 2
                e = s.n(lambda e: e)
                act.wait_ge(s_xg[par], s.n(lambda e: 16 * TILES * (e // 2 + 1)))
                act.activation(token_w[par], xg[par][:, :, bass.ds(e + DIM, 1)].rearrange("p t a -> p (t a)"),
                               ACT.Exp, bias=top_all[:, bass.ds(e, 1)]).then_inc(s_wexp, 1)

                def hidden_high(i):
                    t0, n = half_of(i)
                    act.wait_ge(s_product, s.n(lambda e: 2 * HM * e + i + 1))
                    act.activation(hT[0][:, i % HM, t0 * P:t0 * P + n], hidden[i % 2][:, 0:n], ACT.Copy
                                   ).then_inc(s_hidden_high, 1)

                for i in range(2 * HM):
                    n = half_of(i)[1]
                    act.wait_ge(s_hidden, s.n(lambda e: 2 * HM * e + i + 1))
                    if i >= 2:
                        act.wait_ge(s_product, s.n(lambda e: 2 * HM * e + i - 1))
                    act.activation(gated[i % 2][:, 0:n], S[:, 2 * (i % 2), 0:n], ACT.Silu,
                                   scale=1.0 / (X_SCALE * W_SCALE)).then_inc(s_silu, 1)
                    if i > 0:
                        hidden_high(i - 1)
                    weight_tile(s, i - 1)
                hidden_high(2 * HM - 1)
                for i in range(2):
                    gathered_tile(s, 1, i)
                act.wait_ge(s_tokw, s.n(lambda e: e + 1))
                if s.b >= 2:
                    act.wait_ge(s_added[par], s.n(lambda e: 16 * TILES * (e // 2)))
                for t in range(TILES):
                    n = tile_rows(t)
                    act.wait_ge(s_y, s.n(lambda e: TILES * e + t + 1))
                    act.activation(y[par][0:n, t, :], (B6, B7)[t % 2][0:n, 0:DIM], ACT.Identity,
                                   scale=token_w[par][0:n, t:t + 1]).then_inc(s_y_sb, 1)
                    if t == 1:
                        gathered_tile(s, 1, 2)

            assert XG_TILES == 3
            for i in range(XG_TILES):
                gathered_tile(Step(0), 0, i)
            run_experts(act, expert)

        @block.vector
        def _(dve):
            def gather_columns(t):
                dve.wait_ge(s_images[t], 16 * CHANNELS)
                for c in range(CHANNELS):
                    last = dve.tensor_copy(
                        columns[t][:, c].rearrange("p j (i w) -> p j i w", i=PATCH),
                        images[t][:, c, :].rearrange("p (i j w) -> p j i w", i=PATCH, j=GRID))
                last.then_inc(s_columns, 1)

            def add_patch_bias(u):
                dve.wait_ge(s_patch, u + 1)
                if u >= 2:
                    dve.wait_ge(s_patch_out[u % 2], 16 * (u // 2))
                dve.tensor_tensor(patch_sb[u % 2], (B6, B7)[u % 2][:, 0:DIM], tokb, ALU.add
                                  ).then_inc(s_patch_sb, 1)

            gather_columns(0)
            dve.wait_ge(s_patchw, 32)
            for u in range(UNITS // 2 + 1):
                if u == 2:
                    gather_columns(1)
                add_patch_bias(u)

            def norm_stats(norm, g, count, later=True):
                for i in range(PER):
                    last = dve.bn_stats(stats[norm][:, i, :], h[:, g * PER + i, :])
                last.then_inc(s_stats[norm], 1)
                before, count = in_register(dve, [count - 1, count])
                dve.wait_ge(s_stats[norm], count)
                if later:
                    dve.wait_ge(s_normed[norm], before)
                for i in range(PER):
                    last = dve.bn_aggr(mean_var[norm][:, i, :], stats[norm][:, i, :])
                last.then_inc(s_aggr[norm], 1)
                dve.wait_ge(s_aggr[norm], count)
                dve.tensor_scalar(minus_mean[norm], mean_var[norm][:, :, 0], -1.0, None, ALU.mult)
                dve.tensor_scalar(spread[norm], mean_var[norm][:, :, 1], EPS, None, ALU.add
                                  ).then_inc(s_var[norm], 1)

            dve.wait_ge(s_text[0], 16 * 5)
            dve.wait_ge(s_rows_in[0], 16)
            dve.wait_ge(s_const, 1)
            for g in range(2):
                norm_stats(0, g, g + 1, later=g > 0)
                if g == 0:
                    for u in range(UNITS // 2 + 1, EARLY_UNITS):
                        add_patch_bias(u)
            for u in range(EARLY_UNITS, UNITS):
                add_patch_bias(u)
            dve.wait_ge(s_wgT, 1)
            dve.tensor_copy(wgT, B6[:, 0:CHUNKS * EXPERTS].rearrange("p (c e) -> p c e", c=CHUNKS)
                            ).then_inc(s_wgT_sb, 1)
            def step(s):
                b = s.b

                def scores(r):
                    return S[0:ROWS, r, 0:SPAN].rearrange("p (j t) -> p j t", j=4)

                def largest(r):
                    if b < ITEMS:
                        dve.wait_ge(s_scores, s.n(lambda b: 4 * b + r + 1))
                        dve.tensor_reduce(top[:, r, :], scores(r), AX.X, ALU.max).then_inc(s_max, 1)

                def turned(r):
                    if 0 <= b - 2 < ITEMS:
                        bank = ring_tile("probsT", b - 2, r)[0]
                        dve.wait_ge(s_high, s.n(lambda b: 4 * (b - 2) + r + 1))
                        dve.scalar_tensor_tensor(probT[1][:, r], R[bank][0:ROWS, 0:SPAN]
                                                 .rearrange("p (j t) -> p j t", j=4), P_SCALE, probT[0][:, r],
                                                 ALU.mult, ALU.subtract).then_inc(s_free[bank], 1)

                def less_largest(r):
                    if b < ITEMS:
                        dve.wait_ge(s_max, s.n(lambda b: 4 * b + r + 1))
                        if b >= 4:
                            dve.wait_ge(s_ring, s.n(lambda b: filled("probsT", b - 4, r)))
                        dve.tensor_tensor(prob[b % 4][:, r], scores(r),
                                          top[:, r, :].unsqueeze(2).to_broadcast([ROWS, 4, ROWS]),
                                          ALU.subtract).then_inc(s_sub, 1)

                if b == 2:
                    for i in range(2):
                        dve.wait_ge(s_patch_out[i], 16 * UNITS // 2)
                if b == 8:
                    dve.wait_ge(s_text[1], 16 * 4)
                    dve.wait_ge(s_rows_in[1], 16)
                turned(0)
                turned(1)
                largest(0)
                largest(1)
                largest(2)
                largest(3)
                less_largest(0)
                if b % PER == 0 and 0 <= b // PER - 2 < GROUPS:
                    dve.wait_ge(s_res, s.n(lambda b: b - 4))
                    norm_stats(1, s.n(lambda b: b // PER - 2), s.n(lambda b: b // PER - 1), later=b // PER > 2)
                if b % PER == 1 and b // PER + 2 < GROUPS:
                    norm_stats(0, s.n(lambda b: b // PER + 2), s.n(lambda b: b // PER + 3))
                less_largest(1)
                if 0 <= b - 3 < ITEMS:
                    dve.wait_ge(s_unnormed, s.n(lambda b: b - 2))
                    dve.reciprocal(recip, unnormed[:, :, VCOLS - 1]).then_inc(s_recip, 1)
                turned(2)
                turned(3)
                less_largest(2)
                if 0 <= b - 4 < ITEMS:
                    if b % PER == 0:
                        dve.wait_ge(s_bias, s.n(lambda b: b // PER))
                    dve.wait_ge(s_proj, s.n(lambda b: b - 3))
                    row = h[:, s.n(lambda b: b - 4), :]
                    dve.tensor_tensor(row, row, B7[0:ROWS, DIM:2 * DIM], ALU.add).then_inc(s_res, 1)
                less_largest(3)

            run_steps(dve, step)

            chain = [0]

            def then(ins):
                chain[0] += 1
                ins.then_inc(s_dve, 1)
                dve.wait_ge(s_dve, chain[0])

            dve.wait_ge(s_sc, 16)
            dve.wait_ge(s_consts2, 1)
            dve.wait_ge(s_h_out, 16 * GROUPS)
            dve.tensor_reduce(row_top, sc, AX.X, ALU.max).then_inc(s_rowtop, 1)
            dve.tensor_reduce(abs_top, sc, AX.X, ALU.max, apply_absolute_value=True).then_inc(s_rowtop, 1)
            dve.wait_ge(s_pe, 1)
            then(dve.tensor_reduce(top_row[0:1, :], B7[0:1, 0:P].rearrange("p (e s) -> p e s", s=SEGS),
                                   AX.X, ALU.max, negate=True))
            dve.wait_ge(s_pe, 2)
            then(dve.tensor_copy(top_all, B7[:, DIM:DIM + EXPERTS]))
            then(dve.tensor_tensor_reduce(own_sums, top_all, own, 1.0, 0.0, ALU.mult, ALU.add, own_top))
            assert chain[0] == OWN_TOP
            dve.wait_ge(s_abs, 1)
            then(dve.tensor_scalar(highest, bound, 2.0, 1e-30, ALU.mult, ALU.add))
            then(dve.tensor_scalar(highest.bitcast(I32), highest.bitcast(I32), EXPONENT, None, ALU.bitwise_and))
            dve.tensor_scalar(base, highest, -1.0, None, ALU.mult).then_inc(s_base, 1)
            then(dve.tensor_scalar(step_of, quarters, highest, None, ALU.mult))
            dve.wait_ge(s_base, 1)
            dve.scalar_tensor_tensor(tried[:, 0, :], multiples, step_of[:, 0:1], base.to_broadcast([P, CUTS_IN - 1]),
                                     ALU.mult, ALU.add).then_inc(s_tried, 1)
            with dve.Fori(0, ROUNDS // UNROLLED) as turn:
                for i in range(UNROLLED):
                    n = turn * UNROLLED + i
                    at_n, at_next = bass.ds(n, 1), bass.ds(n + 1, 1)
                    rounds = dve.to_reg(n + 1)
                    dve.wait_ge(s_tried, rounds)
                    for j in range(CUTS_IN - 1):
                        last = dve.tensor_scalar(work[(1, 2, 4)[j]], sc,
                                                 tried[:, at_n, j:j + 1].rearrange("p a c -> p (a c)"), None,
                                                 ALU.is_ge, ALU.add, accum_out=counts[:, j:j + 1])
                    last.then_inc(s_count, 1)
                    dve.wait_ge(s_const, 1)
                    dve.wait_ge(s_base, rounds)
                    dve.scalar_tensor_tensor(ahead, multiples, step_of[:, at_next],
                                             base.to_broadcast([P, CUTS_IN - 1]), ALU.mult, ALU.add
                                             ).then_inc(s_ahead, 1)
                    dve.wait_ge(s_const, 1)
                    dve.wait_ge(s_total, rounds)
                    dve.tensor_scalar(reached[:, at_n, :].rearrange("p a c -> p (a c)"), B6[:, 0:CUTS_IN - 1],
                                      float(CAPACITY), None, ALU.is_ge, ALU.add, accum_out=passed
                                      ).then_inc(s_passed, 1)
                    dve.wait_ge(s_ahead, rounds)
                    dve.wait_ge(s_passed, rounds)
                    dve.scalar_tensor_tensor(tried[:, at_next, :].rearrange("p a c -> p (a c)"),
                                             passed.to_broadcast([P, CUTS_IN - 1]), step_of[:, at_n], ahead,
                                             ALU.mult, ALU.add).then_inc(s_tried, 1)
                    dve.scalar_tensor_tensor(base, passed, step_of[:, at_n], base, ALU.mult, ALU.add
                                             ).then_inc(s_base, 1)
            dve.wait_ge(s_tried, ROUNDS + 1)
            searched = tried[:, 0:ROUNDS, :]
            dve.scalar_tensor_tensor(offered, reached, -MASKED, searched, ALU.mult, ALU.add)
            then(dve.tensor_scalar(missed, reached, -1.0, 1.0, ALU.mult, ALU.add))
            then(dve.scalar_tensor_tensor(offered_low, missed, MASKED, searched, ALU.mult, ALU.add))
            then(dve.tensor_reduce(high, offered.rearrange("p n c -> p (n c)"), AX.X, ALU.min))
            then(dve.tensor_tensor(high, high, highest, ALU.min))
            then(dve.tensor_reduce(low, offered_low.rearrange("p n c -> p (n c)"), AX.X, ALU.max))
            dve.wait_ge(s_tags, 1)
            sure, maybe, order, zero = work[1], work[2], work[4], work[3]
            then(dve.tensor_scalar(sure, sc, high, None, ALU.is_ge, ALU.add, accum_out=count))
            dve.tensor_copy(sure_n, count).then_inc(s_count, 1)
            then(dve.scalar_tensor_tensor(maybe, sc, low, sure, ALU.is_ge, ALU.subtract))
            then(dve.tensor_tensor_scan(order, maybe, zero, 0.0, ALU.add, ALU.add))
            dve.tensor_copy(limit, order[:, SPAN - 1:SPAN]).then_inc(s_count, 1)
            dve.wait_ge(s_total, ROUNDS + 2)
            then(dve.tensor_scalar(need, B6[:, 0:1], -1.0, float(CAPACITY), ALU.mult, ALU.add))
            then(dve.tensor_tensor(need, need, B6[:, 1:2], ALU.subtract))
            then(dve.scalar_tensor_tensor(maybe, order, need, maybe, ALU.is_le, ALU.mult))
            then(dve.tensor_tensor(sure, sure, maybe, ALU.add))
            then(dve.tensor_tensor_scan(order, sure, zero, 0.0, ALU.add, ALU.add))
            dve.tensor_copy(limit2, order[:, SPAN - 1:SPAN]).then_inc(s_count, 1)
            dve.wait_ge(s_expd, 1)
            then(dve.tensor_tensor_reduce(maybe, work[0], sure, 1.0, 0.0, ALU.mult, ALU.add, row_sum))
            dve.tensor_scalar(own_sums, own, row_sum, None, ALU.mult).then_inc(s_count, 1)
            dve.wait_ge(s_total, ROUNDS + 3)
            then(dve.scalar_tensor_tensor(order, order, B6[:, 2:3], sure, ALU.add, ALU.mult))
            then(dve.tensor_scalar(ints[0], order, -1.0, None, ALU.add))
            dve.tensor_scalar(ints[1], ints[0], 7, None, ALU.arith_shift_right)
            then(dve.tensor_scalar(ints[2], ints[0], P - 1, None, ALU.bitwise_and))
            dve.tensor_copy(work[1], ints[1])
            dve.tensor_copy(work[2], ints[2]).then_inc(s_slots, 1)
            dve.tensor_scalar(tag_i[:, 1], tag_i[:, 0], 6, None, ALU.arith_shift_right)
            then(dve.tensor_scalar(tag_i[:, 2], tag_i[:, 0], TAG - 1, None, ALU.bitwise_and))
            dve.tensor_copy(tag[0], tag_i[:, 1])
            then(dve.tensor_copy(tag[1], tag_i[:, 2]))
            dve.wait_ge(s_total, ROUNDS + 4)
            then(dve.reciprocal(recip_all, B7[:, DIM:DIM + EXPERTS]))
            for i in range(2):
                dve.wait_ge(s_slotT, len(CUTS) * (i + 1))
                for c, (t0, n) in enumerate(CUTS):
                    last = dve.tensor_copy(slotT[i][0:n, c].rearrange("p e s -> p (e s)"),
                                           S[0:n, i, c * P:(c + 1) * P])
            then(last)

            def one_hots(s, ahead):
                if s.b + ahead > 0:
                    dve.wait_ge(s_list, s.n(lambda e: e + ahead))
                at_e = s.n(lambda e: e + ahead)
                tile_of = slotT[0][:, :, bass.ds(at_e, 1), :].rearrange("p c a s -> p c (a s)")
                row_of = slotT[1][:, :, bass.ds(at_e, 1), :].rearrange("p c a s -> p c (a s)")
                shape = [P, len(CUTS), SEGS]
                dve.tensor_tensor(match, tile_of.unsqueeze(3).to_broadcast(shape + [TILES]),
                                  iota_f[:, 0:TILES].unsqueeze(1).unsqueeze(1).to_broadcast(shape + [TILES]),
                                  ALU.is_equal).then_inc(s_match, 1)
                dve.tensor_tensor(onehot, row_of.unsqueeze(3).to_broadcast(shape + [P]),
                                  iota_f[:, :].unsqueeze(1).unsqueeze(1).to_broadcast(shape + [P]), ALU.is_equal)
                dve.wait_ge(s_match, s.n(lambda e: e + ahead + 1))
                for i in range(2):
                    last = dve.tensor_tensor(tagged[:, :, :, i, :], match,
                                             tag[i].unsqueeze(3).to_broadcast(shape + [TILES]), ALU.mult)
                last.then_inc(s_onehot, 1)

            def list_tokens(s, ahead):
                dve.wait_ge(s_list, s.n(lambda e: e + ahead + 1))
                dve.tensor_copy(number, B7[:, DIM:DIM + 2 * TILES].rearrange("p (a t) -> p a t", a=2)
                                ).then_inc(s_number, 1)

            def token_index(s, ahead):
                par = (s.b + ahead) % 2
                dve.wait_ge(s_number, s.n(lambda e: e + ahead + 1))
                if s.b + ahead >= 2:
                    dve.wait_ge(s_added[par], s.n(lambda e: 16 * TILES * ((e + ahead) // 2)))
                dve.scalar_tensor_tensor(index[par], number[:, 0], float(TAG), number[:, 1], ALU.mult, ALU.add
                                         ).then_inc(s_index, 1)

            one_hots(Step(0), 0)
            list_tokens(Step(0), 0)
            token_index(Step(0), 0)
            one_hots(Step(0), 1)

            def take_low(s, i, low, tile, high, scale):
                dve.wait_ge(s_ehigh, s.n(lambda e: ering(e, i + 1)))
                dve.scalar_tensor_tensor(low, tile, scale, high, ALU.mult, ALU.subtract).then_inc(s_emoved, 1)

            def gathered_low(s, ahead, i):
                if s.b + ahead < EXPERTS:
                    w = tile_rows(2 * i + 1) + P
                    low, whole = xgT[1][:, :, 2 * P * i:2 * P * i + w], R[ering(s.b + ahead, i) % 2]
                    dve.wait_ge(s_ehigh, s.n(lambda e: ering(e + ahead, i + 1)))
                    dve.scalar_tensor_tensor(low, whole[:, :].rearrange("p (c t) -> p c t", c=2)[:, :, 0:w], X_SCALE,
                                             xgT[0][:, :, 2 * P * i:2 * P * i + w], ALU.mult, ALU.subtract
                                             ).then_inc(s_emoved, 1)

            def expert(s):
                par = s.b % 2
                dve.wait_ge(s_wexp, s.n(lambda e: e + 1))
                dve.tensor_scalar(token_w[par], token_w[par], recip_all[:, bass.ds(s.n(lambda e: e), 1)],
                                  1.0 / (HID_SCALE * W_SCALE), ALU.mult, ALU.mult).then_inc(s_tokw, 1)

                def hidden_low(i):
                    t0, n = half_of(i)
                    dve.wait_ge(s_hidden_high, s.n(lambda e: 2 * HM * e + i + 1))
                    dve.tensor_tensor(hT[1][:, i % HM, t0 * P:t0 * P + n], hidden[i % 2][:, 0:n],
                                      hT[0][:, i % HM, t0 * P:t0 * P + n], ALU.subtract).then_inc(s_hT, 1)

                for i in range(2 * HM):
                    n = half_of(i)[1]
                    dve.wait_ge(s_silu, s.n(lambda e: 2 * HM * e + i + 1))
                    if s.b > 0 or i >= 2:
                        dve.wait_ge(s_hT, s.n(lambda e: 2 * HM * e + i - 1))
                    dve.scalar_tensor_tensor(hidden[i % 2][:, 0:n], S[:, 2 * (i % 2) + 1, 0:n],
                                             HID_SCALE / (X_SCALE * W_SCALE), gated[i % 2][:, 0:n],
                                             ALU.mult, ALU.mult).then_inc(s_product, 1)
                    if i == 1 and s.b + 1 < EXPERTS:
                        list_tokens(s, 1)
                    if i > 0:
                        hidden_low(i - 1)
                    if i == 1 and s.b + 1 < EXPERTS:
                        token_index(s, 1)
                    if s.b + 1 < EXPERTS and 0 <= i - 1 < W_TILES:
                        high, low = weight_parts(s.b + 1, i - 1)
                        take_low(s, XG_TILES + i - 1, low, R[ering(s.b, XG_TILES + i - 1) % 2][:, :], high, W_SCALE)
                hidden_low(2 * HM - 1)
                for i in range(XG_TILES):
                    gathered_low(s, 1, i)
                if s.b + 2 < EXPERTS:
                    one_hots(s, 2)

            for i in range(XG_TILES):
                gathered_low(Step(0), 0, i)
            run_experts(dve, expert)

        @block.tensor
        def _(pe):
            def ring_free(kind, s, which, i):
                pe.wait_ge(s_free[ring_tile(kind, which(s.b), i)[0]],
                           s.n(lambda b: ring_tile(kind, which(b), i)[1] - 1))

            def turn_patches(u):
                t, j = divmod(u, GRID)
                if u % GRID == 0:
                    pe.wait_ge(s_columns, t + 1)
                for i in range(2):
                    if u > 0:
                        pe.wait_ge(s_free[i], unit_tile(u, i) // 2)
                    for k in range(4 * i, min(4 * i + 4, PATCH_DIM // P)):
                        c, half = divmod(k, 2)
                        last = pe.transpose(R[i][:, P * (k % 4):P * (k % 4 + 1)],
                                            columns[t][:, c, j, P * half:P * (half + 1)], ident[:, :])
                    last.then_inc(s_ring, 1)

            def project_patches(u):
                for i in range(2):
                    pe.wait_ge(s_free[i], unit_tile(u, i) // 2 + 1)
                if u >= 2:
                    pe.wait_ge(s_patch_sb, u - 1)
                for k in range(PATCH_DIM // P):
                    last = pe.matmul((B6, B7)[u % 2][:, 0:DIM], patchT[u % 2][:, k, :], tokw[:, k, :],
                                     start=(k == 0), stop=(k == PATCH_DIM // P - 1))
                last.then_inc(s_patch, 1)

            pe.wait_ge(s_const, 1)
            turn_patches(0)
            pe.wait_ge(s_patchw, 32)

            def patches(units):
                for u in units:
                    if u + 1 in units:
                        turn_patches(u + 1)
                    project_patches(u)

            patches(range(EARLY_UNITS))
            pe.wait_ge(s_weights, 16 * 6)

            def also_moved(kind, s, which, next_bank):
                for i in range(2 if kind != "gate" else 1):
                    if ring_tile(kind, which(s.b), i)[0] != next_bank:
                        wait_moved(pe, kind, s, which, i)

            def piece(kind, s, which, gpar, i):
                bank = ring_tile(kind, which(s.b), i)[0]
                dst = R[bank]
                if kind in ("xT", "x2T"):
                    norm, rows = (0, xn) if kind == "xT" else (1, xn2[gpar])
                    pe.wait_ge(s_normed[norm], s.n(lambda b: which(b) + 1))
                    ring_free(kind, s, which, i)
                    for j in range(PER):
                        last = pe.transpose(dst[:, ROWS * j:ROWS * (j + 1)], rows[:, j, P * i:P * (i + 1)],
                                            ident[0:ROWS, 0:ROWS])
                if kind in ("q", "k"):
                    w = wq if kind == "q" else wk
                    also_moved("xT", s, which, bank)
                    ring_free(kind, s, which, i)
                    for k in range(CHUNKS):
                        last = pe.matmul(dst[:, 0:SPAN], w[:, k, P * i:P * (i + 1)], xT[:, k, :],
                                         start=(k == 0), stop=(k == CHUNKS - 1))
                if kind == "v":
                    ring_free(kind, s, which, i)
                    for j in range(2):
                        for k in range(CHUNKS):
                            last = pe.matmul(dst[0:ROWS, DIM * j:DIM * (j + 1)],
                                             xT[:, k, ROWS * (2 * i + j):ROWS * (2 * i + j + 1)], wv[:, k, :],
                                             start=(k == 0), stop=(k == CHUNKS - 1))
                if kind == "gate":
                    also_moved("x2T", s, which, bank)
                    ring_free(kind, s, which, i)
                    for k in range(CHUNKS):
                        last = pe.matmul(dst[0:EXPERTS, 0:SPAN], wgT[:, k, :], x2T[:, k, :],
                                         start=(k == 0), stop=(k == CHUNKS - 1))
                if kind == "gateT":
                    router, free = in_register(pe, [s.n(lambda b: ring_tile("gate", which(b))[1]),
                                                    s.n(lambda b: ring_tile("gateT", which(b))[1] - 1)])
                    if ring_tile("gate", which(s.b))[0] != bank:
                        pe.wait_ge(s_free[1 - bank], router)
                    pe.wait_ge(s_free[bank], free)
                    for j in range(PER):
                        last = pe.transpose(dst[0:ROWS, EXPERTS * j:EXPERTS * (j + 1)],
                                            gate_sb[gpar][:, ROWS * j:ROWS * (j + 1)],
                                            ident[0:EXPERTS, 0:EXPERTS])
                last.then_inc(s_ring, 1)

            for kind, which, i in FIRST_PIECES:
                piece(kind, Step(0), lambda b: which, which % 2, i)
            turn_patches(EARLY_UNITS)
            patches(range(EARLY_UNITS, UNITS))
            pe.wait_ge(s_patch_sb, UNITS)
            for c in range(CHUNKS):
                last = pe.transpose(B6[:, c * EXPERTS:(c + 1) * EXPERTS], wg_rows[:, c * P:(c + 1) * P],
                                    ident[0:EXPERTS, 0:EXPERTS])
            last.then_inc(s_wgT, 1)
            pe.wait_ge(s_wgT_sb, 1)

            def group_pieces(s):
                for kind, which, i in pieces(s.b):
                    piece(kind, s, lambda b, lag=which - s.b // PER: b // PER + lag, which % 2, i)

            def step(s):
                b = s.b

                def scores(ahead, r):
                    b = s.b + ahead
                    if b >= ITEMS:
                        return
                    gpar, item = b // PER % 2, b % PER
                    if item == 0 and r == 0:
                        pe.wait_ge(s_q_in, s.n(lambda b: 16 * 4 * ((b + ahead) // PER + 1)))
                        pe.wait_ge(s_k_in, s.n(lambda b: 16 * 8 * ((b + ahead) // PER + 1)))
                    if b > 0:
                        pe.wait_ge(s_sub, s.n(lambda b: 4 * (b + ahead) - 3 + r))
                    pe.matmul(S[0:ROWS, r, 0:SPAN], ident_b[0:ROWS, 0:ROWS],
                              mask.rearrange("p j t -> p (j t)"), start=True, stop=False, skip_group_check=True)
                    for a in (2 * r, 2 * r + 1):
                        last = pe.matmul(S[0:ROWS, r, 2 * ROWS * (a % 2):2 * ROWS * (a % 2 + 1)],
                                         Q2[gpar][:, a, ROWS * item:ROWS * (item + 1)],
                                         K2[gpar][:, a, :, ROWS * item:ROWS * (item + 1)],
                                         start=False, stop=(a % 2 == 1), skip_group_check=True)
                    last.then_inc(s_scores, 1)

                def turn(r):
                    if not 0 <= b - 2 < ITEMS:
                        return
                    if r in (0, 2):
                        pe.wait_ge(s_exp, s.n(lambda b: 2 * (b - 2) + 1 + r // 2))
                    ring_free("probsT", s, lambda b: b - 2, r)
                    dst = R[ring_tile("probsT", b - 2, r)[0]]
                    for j in range(4):
                        last = pe.transpose(dst[0:ROWS, ROWS * j:ROWS * (j + 1)],
                                            prob[(b - 2) % 4][:, r, j, :], ident[0:ROWS, 0:ROWS])
                    last.then_inc(s_ring, 1)

                def outputs(behind, r):
                    b = s.b - behind
                    if not 0 <= b < ITEMS:
                        return
                    wait_moved(pe, "probsT", s, lambda b: b - behind, r)
                    gpar, item = b // PER % 2, b % PER
                    if item == 0 and r == 0:
                        pe.wait_ge(s_split, s.n(lambda b: SPLIT_AT[("v", (b - behind) // PER, 1)] + 1))
                    if r == 0 and b > 0:
                        pe.wait_ge(s_unnormed, s.n(lambda b: b - behind))
                    if r == 3 and b > 1:
                        pe.wait_ge(s_res, s.n(lambda b: b - behind - 1))
                    for j in range(4):
                        head = 4 * r + j
                        dst = B7[0:ROWS, 0:VCOLS] if head == SIDE else \
                            B6[0:ROWS, VCOLS * head:VCOLS * (head + 1)]
                        for part in range(2):
                            last = pe.matmul(dst, probT[part][:, r, j, :], v[gpar][:, item, head, :],
                                             start=(part == 0), stop=(part == 1), skip_group_check=True)
                    last.then_inc(s_pv, 1)

                if b == 0:
                    scores(0, 0)
                    scores(0, 1)
                turn(0)
                turn(1)
                scores(0, 2)
                scores(0, 3)
                outputs(3, 3)
                group_pieces(s)
                outputs(2, 0)
                if 0 <= b - 4 < ITEMS:
                    pe.wait_ge(s_norm, s.n(lambda b: b - 3))
                    ring_free("attnT", s, lambda b: b - 4, 0)
                    dst = R[ring_tile("attnT", b - 4)[0]]
                    for c in range(CHUNKS):
                        last = pe.transpose(dst[:, ROWS * c:ROWS * (c + 1)], attn[:, P * c:P * (c + 1)],
                                            ident[0:ROWS, 0:ROWS])
                    last.then_inc(s_ring, 1)
                outputs(2, 1)
                turn(2)
                turn(3)
                scores(1, 0)
                if 0 <= b - 4 < ITEMS:
                    wait_moved(pe, "attnT", s, lambda b: b - 4)
                    if b - 4 < ITEMS - 1:
                        pe.wait_ge(s_unnormed, s.n(lambda b: b - 2))
                    if b - 4 > 0:
                        pe.wait_ge(s_res, s.n(lambda b: b - 4))
                    for c in range(CHUNKS):
                        last = pe.matmul(B7[0:ROWS, DIM:2 * DIM], attn_nT[:, c, :], wo[:, c, :],
                                         start=(c == 0), stop=(c == CHUNKS - 1))
                    last.then_inc(s_proj, 1)
                scores(1, 1)
                outputs(2, 2)

            run_steps(pe, step)

            def ering_tile(s, i):
                if s.b >= 0 or i - XG_TILES >= 2:
                    pe.wait_ge(s_emoved, s.n(lambda e: ering(e, i - 1)))
                return R[ering(s.b, i) % 2]

            def weights(s, tiles=range(W_TILES)):
                par = (s.b + 1) % 2
                if tiles[0] == 0:
                    pe.wait_ge(s_raw[par], s.n(lambda e: 48 * ((e + 1) // 2 + 1)))
                for i in tiles:
                    dst = ering_tile(s, XG_TILES + i)
                    for m in range(4):
                        if i < 4:
                            src = (w1_raw if i < 2 else w3_raw)[par][:, m, P * (i % 2):P * (i % 2 + 1)]
                        else:
                            hm = 2 * (i - 4) + m // 2
                            src = w2_raw[par][:, m % 2, P * hm:P * (hm + 1)]
                        last = pe.transpose(dst[:, P * m:P * (m + 1)], src, ident[:, :])
                    last.then_inc(s_ering, 1)

            pe.wait_ge(s_rowtop, 1)
            pe.transpose(B7[0:1, 0:P], row_top, ident[:, :]).then_inc(s_pe, 1)
            pe.wait_ge(s_ones, 1)
            pe.wait_ge(s_dve, 1)
            pe.matmul(B7[:, DIM:DIM + EXPERTS], all_ones[0:1, :], top_row[0:1, :], start=True, stop=True
                      ).then_inc(s_pe, 1)

            def total(turn):
                pe.wait_ge(s_count, turn + 1)
                pe.matmul(B6[:, 0:CUTS_IN - 1], same_block, counts, start=True, stop=True).then_inc(s_total, 1)

            for n in range(W_TILES):
                total(n)
                weights(Step(-1), (n,))
            with pe.Fori(W_TILES, ROUNDS) as turn:
                total(turn)
            for i, (block_of, col) in enumerate(((same_block, sure_n), (before_block, limit), (before_block, limit2))):
                pe.wait_ge(s_count, ROUNDS + i + 1)
                pe.matmul(B6[:, i:i + 1], block_of, col, start=True, stop=True).then_inc(s_total, 1)
            pe.wait_ge(s_count, ROUNDS + 4)
            pe.matmul(B7[:, DIM:DIM + EXPERTS], all_ones, own_sums, start=True, stop=True).then_inc(s_total, 1)
            pe.wait_ge(s_slots, 1)
            for i in range(2):
                for c, (t0, n) in enumerate(CUTS):
                    pe.transpose(S[0:n, i, c * P:(c + 1) * P], work[1 + i][:, t0:t0 + n], ident[:, :]
                                 ).then_inc(s_slotT, 1)

            def list_tokens(s, ahead):
                pe.wait_ge(s_onehot, s.n(lambda e: e + ahead + 1))
                if s.b + ahead > 0:
                    pe.wait_ge(s_number, s.n(lambda e: e + ahead))
                if s.b > 0:
                    pe.wait_ge(s_y_sb, s.n(lambda e: TILES * e))
                for c in range(len(CUTS)):
                    for g in range(SEGS):
                        last = pe.matmul(B7[:, DIM:DIM + 2 * TILES], onehot[:, c, g, :],
                                         tagged[:, c, g].rearrange("p a t -> p (a t)"),
                                         start=(c == 0 and g == 0), stop=(c == len(CUTS) - 1 and g == SEGS - 1))
                last.then_inc(s_list, 1)

            pe.wait_ge(s_dve, ROUTED)
            list_tokens(Step(0), 0)

            def gathered(s, ahead, i):
                par = (s.b + ahead) % 2
                if s.b + ahead >= EXPERTS:
                    return
                if i == 0:
                    pe.wait_ge(s_xg[par], s.n(lambda e: 16 * TILES * ((e + ahead) // 2 + 1)))
                pe.wait_ge(s_emoved, s.n(lambda e: ering(e + ahead, i - 1)))
                dst = R[ering(s.b + ahead, i) % 2]
                for c in range(CHUNKS):
                    for t in (2 * i, 2 * i + 1):
                        n = tile_rows(t)
                        at0 = 2 * P * c + P * (t % 2)
                        last = pe.transpose(dst[:, at0:at0 + n], xg[par][0:n, t, P * c:P * (c + 1)],
                                            ident[0:n, 0:n])
                last.then_inc(s_ering, 1)

            for i in range(XG_TILES):
                gathered(Step(0), 0, i)

            def expert(s):
                par = s.b % 2
                for i in range(2 * HM):
                    half, m = divmod(i, HM)
                    t0, t1 = HALVES[half]
                    n = sum(tile_rows(t) for t in range(t0, t1))
                    if m == 0:
                        if s.b == 0:
                            pe.wait_ge(s_first_low, W_TILES)
                        pe.wait_ge(s_emoved, s.n(lambda e: ering(e, min(XG_TILES, (t1 + 1) // 2))))
                    if i >= 2:
                        pe.wait_ge(s_product, s.n(lambda e: 2 * HM * e + i - 1))
                    for w, bank in ((w1T, 0), (w3T, 1)):
                        terms = [(k, a, b) for k in range(CHUNKS) for a, b in SPLIT_PAIRS]
                        for k, a, b in terms:
                            last = pe.matmul(S[:, 2 * (i % 2) + bank, 0:n], w[par][a][:, k, P * m:P * (m + 1)],
                                             xgT[b][:, k, P * t0:P * t0 + n],
                                             start=((k, a, b) == terms[0]), stop=((k, a, b) == terms[-1]))
                    last.then_inc(s_hidden, 1)
                    if i == 1 and s.b + 1 < EXPERTS:
                        list_tokens(s, 1)
                    if s.b + 1 < EXPERTS and 0 <= i - 1 < W_TILES:
                        weights(s, (i - 1,))
                for i in range(2):
                    gathered(s, 1, i)
                for t in range(TILES):
                    n = tile_rows(t)
                    if t == 2:
                        gathered(s, 1, 2)
                    if t in (HALVES[0][0], HALVES[1][0]):
                        pe.wait_ge(s_hT, s.n(lambda e: 2 * HM * e + HM * (1 if t == 0 else 2)))
                    if t >= 2:
                        pe.wait_ge(s_y_sb, s.n(lambda e: TILES * e + t - 1))
                    terms = [(m, a, b) for m in range(HM) for a, b in SPLIT_PAIRS]
                    for m, a, b in terms:
                        last = pe.matmul((B6, B7)[t % 2][0:n, 0:DIM], hT[a][:, m, P * t:P * t + n],
                                         w2T[par][b][:, m, :],
                                         start=((m, a, b) == terms[0]), stop=((m, a, b) == terms[-1]))
                    last.then_inc(s_y, 1)

            run_experts(pe, expert)


_INS = ['x', 'txt', 'L0_tok_W', 'L0_tok_b', 'L0_tok_cls_token', 'L0_attn_Wq', 'L0_attn_Wk', 'L0_attn_Wv',
        'L0_attn_Wo', 'L0_attn_bo', 'L0_ffn_Wg', 'L0_ffn_W1', 'L0_ffn_W2', 'L0_ffn_W3']
_OUTS = [((ITEMS, ROWS, DIM), 'float32')]


def kernel(**inputs):
    import numpy as _np
    import concourse.bacc as _bacc
    from concourse import mybir as _mybir
    from concourse.bass_utils import run_bass_kernel_spmd as _run

    nc = _bacc.Bacc("TRN2", target_bir_lowering=False, num_devices=1)
    arrays, args = {}, []
    for name in _INS:
        a = _np.ascontiguousarray(inputs[name])
        arrays[f"in_{name}_dram"] = a
        args.append(nc.dram_tensor(f"in_{name}_dram", a.shape, _mybir.dt.from_np(a.dtype), kind="ExternalInput").ap())
    for i, (shape, dtype) in enumerate(_OUTS):
        dt = _mybir.dt.from_np(_np.dtype(dtype))
        args.append(nc.dram_tensor(f"out_{i}_dram", shape, dt, kind="ExternalOutput").ap())
    build(nc, *args)
    r = _run(nc, [arrays], core_ids=[0])
    return r.results[0]["out_0_dram"]
```
